# Optimizing a Trainium2 kernel written in Bass

```python
import numpy as np
import jax
import jax.numpy as jnp

def _softmax(x, axis=-1):
    return jax.nn.softmax(x, axis=axis)

def _gelu(x):
    return jax.nn.gelu(x, approximate=True)

def _silu(x):
    return jax.nn.silu(x)

def _sigmoid(x):
    return jax.nn.sigmoid(x)

def _layernorm(x, axis=-1, eps=1e-05):
    m = jnp.mean(x, axis=axis, keepdims=True)
    v = jnp.var(x, axis=axis, keepdims=True)
    return (x - m) / jnp.sqrt(v + eps)

def _scatter_add(tgt, idx, src, axis=0):
    return tgt.at[idx].add(src)

def _segment_sum(src, seg, n):
    return jax.ops.segment_sum(src, seg, n)
kernel_name = 'mk_prb_d1_jaxref_r4_2e7e13'

def setup_inputs(seed: int=0):
    np.random.seed(seed)
    _w = jnp.asarray

    def _L0_attn_setup():
        import math
        import jax, jax.numpy as jnp
        import numpy as np
        N_HEADS = 32
        N_KV_HEADS = 8
        ROPE_THETA = 10000.0
        LAYER_IDX = 12
        LAMBDA_INIT = 0.8 - 0.6 * math.exp(-0.3 * LAYER_IDX)

        def _rotate_half(x):
            x1, x2 = jnp.split(x, 2, axis=-1)
            return jnp.concatenate([-x2, x1], axis=-1)

        def _rope_tables(seq_len, head_dim, dtype):
            inv_freq = 1.0 / ROPE_THETA ** (jnp.arange(0, head_dim, 2, dtype=jnp.float32) / head_dim)
            freqs = jnp.arange(seq_len, dtype=jnp.float32)[:, None] * inv_freq[None, :]
            emb = jnp.concatenate([freqs, freqs], axis=-1)
            return (jnp.cos(emb).astype(dtype), jnp.sin(emb).astype(dtype))

        def _apply_rope(x, cos, sin):
            return x * cos[None, None] + _rotate_half(x) * sin[None, None]
        key = jax.random.key(seed)
        ks = jax.random.split(key, 9)
        B, S, H = (2, 256, 512)
        hd = H // N_HEADS
        return {'hidden_states': jax.random.normal(ks[0], (B, S, H), jnp.float32), 'wq': jax.random.normal(ks[1], (2 * H, H), jnp.float32) * 0.02, 'wk': jax.random.normal(ks[2], (2 * N_KV_HEADS * hd, H), jnp.float32) * 0.02, 'wv': jax.random.normal(ks[3], (N_KV_HEADS * hd, H), jnp.float32) * 0.02, 'wo': jax.random.normal(ks[4], (H, H), jnp.float32) * 0.02, 'lambda_q1': jax.random.normal(ks[5], (hd,), jnp.float32) * 0.1, 'lambda_k1': jax.random.normal(ks[6], (hd,), jnp.float32) * 0.1, 'lambda_q2': jax.random.normal(ks[7], (hd,), jnp.float32) * 0.1, 'lambda_k2': jax.random.normal(ks[8], (hd,), jnp.float32) * 0.1}
    _L0_attn_in = _L0_attn_setup()

    def _L0_ffn_setup():
        import jax, jax.numpy as jnp
        import numpy as np
        B_, S, D = (2, 512, 512)
        F_ = 2048
        R = 16
        H = 16
        HD = D // H
        MOD_SCALE = 0.1
        EPS = 1e-06

        def _rmsnorm(x, w):
            v = jnp.mean(x * x, axis=-1, keepdims=True)
            return x * jax.lax.rsqrt(v + EPS) * w

        def _attention(x, Wq, Wk, Wv, Wo):
            b, s, d = x.shape
            q = (x @ Wq.T).reshape(b, s, H, HD)
            k = (x @ Wk.T).reshape(b, s, H, HD)
            v = (x @ Wv.T).reshape(b, s, H, HD)
            scores = jnp.einsum('bqhd,bkhd->bhqk', q, k) / np.sqrt(HD).astype(np.float32)
            causal = jnp.tril(jnp.ones((s, s), bool))
            scores = jnp.where(causal, scores, jnp.finfo(scores.dtype).min)
            probs = jax.nn.softmax(scores, axis=-1)
            out = jnp.einsum('bhqk,bkhd->bqhd', probs, v).reshape(b, s, d)
            return out @ Wo.T
        key = jax.random.key(seed)
        ks = jax.random.split(key, 12)
        sd = 0.02
        return {'hidden_states': jax.random.normal(ks[0], (B_, S, D), jnp.float32), 'ln1_w': jnp.ones((D,), jnp.float32), 'ln2_w': jnp.ones((D,), jnp.float32), 'Wq': jax.random.normal(ks[1], (D, D), jnp.float32) * sd, 'Wk': jax.random.normal(ks[2], (D, D), jnp.float32) * sd, 'Wv': jax.random.normal(ks[3], (D, D), jnp.float32) * sd, 'Wo': jax.random.normal(ks[4], (D, D), jnp.float32) * sd, 'A': jax.random.normal(ks[5], (D, R), jnp.float32) * (0.01 / np.sqrt(D)), 'B': jax.random.normal(ks[6], (R, F_), jnp.float32) * (0.01 / np.sqrt(R)), 'W_in_base': jax.random.normal(ks[7], (F_, D), jnp.float32) * sd, 'W_up_base': jax.random.normal(ks[8], (F_, D), jnp.float32) * sd, 'W_down': jax.random.normal(ks[9], (D, F_), jnp.float32) * sd}
    _L0_ffn_in = _L0_ffn_setup()
    _d = {'L0_attn_hidden_states': _L0_attn_in['hidden_states'], 'L0_attn_wq': _L0_attn_in['wq'], 'L0_attn_wk': _L0_attn_in['wk'], 'L0_attn_wv': _L0_attn_in['wv'], 'L0_attn_wo': _L0_attn_in['wo'], 'L0_attn_lambda_q1': _L0_attn_in['lambda_q1'], 'L0_attn_lambda_k1': _L0_attn_in['lambda_k1'], 'L0_attn_lambda_q2': _L0_attn_in['lambda_q2'], 'L0_attn_lambda_k2': _L0_attn_in['lambda_k2'], 'L0_ffn_ln1_w': _L0_ffn_in['ln1_w'], 'L0_ffn_ln2_w': _L0_ffn_in['ln2_w'], 'L0_ffn_Wq': _L0_ffn_in['Wq'], 'L0_ffn_Wk': _L0_ffn_in['Wk'], 'L0_ffn_Wv': _L0_ffn_in['Wv'], 'L0_ffn_Wo': _L0_ffn_in['Wo'], 'L0_ffn_A': _L0_ffn_in['A'], 'L0_ffn_B': _L0_ffn_in['B'], 'L0_ffn_W_in_base': _L0_ffn_in['W_in_base'], 'L0_ffn_W_up_base': _L0_ffn_in['W_up_base'], 'L0_ffn_W_down': _L0_ffn_in['W_down']}
    _x0 = _d['L0_attn_hidden_states']
    _d['L0_attn_hidden_states'] = jax.random.normal(jax.random.fold_in(jax.random.key(seed), 1), (2, 1024, 512), dtype=_x0.dtype)
    del _x0
    return _d

def reference(L0_attn_hidden_states, L0_attn_wq, L0_attn_wk, L0_attn_wv, L0_attn_wo, L0_attn_lambda_q1, L0_attn_lambda_k1, L0_attn_lambda_q2, L0_attn_lambda_k2, L0_ffn_ln1_w, L0_ffn_ln2_w, L0_ffn_Wq, L0_ffn_Wk, L0_ffn_Wv, L0_ffn_Wo, L0_ffn_A, L0_ffn_B, L0_ffn_W_in_base, L0_ffn_W_up_base, L0_ffn_W_down):

    def _L0_attn_ref(hidden_states, wq, wk, wv, wo, lambda_q1, lambda_k1, lambda_q2, lambda_k2):
        import math
        import jax, jax.numpy as jnp
        import numpy as np
        N_HEADS = 32
        N_KV_HEADS = 8
        ROPE_THETA = 10000.0
        LAYER_IDX = 12
        LAMBDA_INIT = 0.8 - 0.6 * math.exp(-0.3 * LAYER_IDX)

        def _rotate_half(x):
            x1, x2 = jnp.split(x, 2, axis=-1)
            return jnp.concatenate([-x2, x1], axis=-1)

        def _rope_tables(seq_len, head_dim, dtype):
            inv_freq = 1.0 / ROPE_THETA ** (jnp.arange(0, head_dim, 2, dtype=jnp.float32) / head_dim)
            freqs = jnp.arange(seq_len, dtype=jnp.float32)[:, None] * inv_freq[None, :]
            emb = jnp.concatenate([freqs, freqs], axis=-1)
            return (jnp.cos(emb).astype(dtype), jnp.sin(emb).astype(dtype))

        def _apply_rope(x, cos, sin):
            return x * cos[None, None] + _rotate_half(x) * sin[None, None]
        B, S, H = hidden_states.shape
        hd = H // N_HEADS
        n_rep = N_HEADS // N_KV_HEADS
        qp = hidden_states @ wq.T
        kp = hidden_states @ wk.T
        v = hidden_states @ wv.T
        q1, q2 = jnp.split(qp, 2, axis=-1)
        k1, k2 = jnp.split(kp, 2, axis=-1)

        def to_heads(x):
            return x.reshape(B, S, -1, hd).transpose(0, 2, 1, 3)
        q1, q2 = (to_heads(q1), to_heads(q2))
        k1, k2 = (to_heads(k1), to_heads(k2))
        v = to_heads(v)
        cos, sin = _rope_tables(S, hd, hidden_states.dtype)
        q1, k1 = (_apply_rope(q1, cos, sin), _apply_rope(k1, cos, sin))
        q2, k2 = (_apply_rope(q2, cos, sin), _apply_rope(k2, cos, sin))
        k1 = jnp.repeat(k1, n_rep, axis=1)
        k2 = jnp.repeat(k2, n_rep, axis=1)
        v = jnp.repeat(v, n_rep, axis=1)
        scale = 1.0 / math.sqrt(hd)
        causal = jnp.where(jnp.tril(jnp.ones((S, S), dtype=bool)), 0.0, -1e+30).astype(jnp.float32)
        s1 = jnp.einsum('bhqd,bhkd->bhqk', q1, k1) * scale + causal
        s2 = jnp.einsum('bhqd,bhkd->bhqk', q2, k2) * scale + causal
        a1 = jax.nn.softmax(s1.astype(jnp.float32), axis=-1).astype(q1.dtype)
        a2 = jax.nn.softmax(s2.astype(jnp.float32), axis=-1).astype(q1.dtype)
        lam1 = jnp.exp(jnp.sum(lambda_q1 * lambda_k1))
        lam2 = jnp.exp(jnp.sum(lambda_q2 * lambda_k2))
        lam_full = lam1 - lam2 + LAMBDA_INIT
        aw = a1 - lam_full * a2
        attn = jnp.einsum('bhqk,bhkd->bhqd', aw, v) * (1.0 - LAMBDA_INIT)
        attn = attn.transpose(0, 2, 1, 3).reshape(B, S, H)
        return attn @ wo.T

    def _L0_ffn_ref(hidden_states, ln1_w, ln2_w, Wq, Wk, Wv, Wo, A, B, W_in_base, W_up_base, W_down):
        import jax, jax.numpy as jnp
        import numpy as np
        B_, S, D = (2, 512, 512)
        F_ = 2048
        R = 16
        H = 16
        HD = D // H
        MOD_SCALE = 0.1
        EPS = 1e-06

        def _rmsnorm(x, w):
            v = jnp.mean(x * x, axis=-1, keepdims=True)
            return x * jax.lax.rsqrt(v + EPS) * w

        def _attention(x, Wq, Wk, Wv, Wo):
            b, s, d = x.shape
            q = (x @ Wq.T).reshape(b, s, H, HD)
            k = (x @ Wk.T).reshape(b, s, H, HD)
            v = (x @ Wv.T).reshape(b, s, H, HD)
            scores = jnp.einsum('bqhd,bkhd->bhqk', q, k) / np.sqrt(HD).astype(np.float32)
            causal = jnp.tril(jnp.ones((s, s), bool))
            scores = jnp.where(causal, scores, jnp.finfo(scores.dtype).min)
            probs = jax.nn.softmax(scores, axis=-1)
            out = jnp.einsum('bhqk,bkhd->bqhd', probs, v).reshape(b, s, d)
            return out @ Wo.T
        residual = hidden_states
        x = _rmsnorm(hidden_states, ln1_w)
        attn = _attention(x, Wq, Wk, Wv, Wo)
        mod = MOD_SCALE * jnp.tanh(attn @ A)
        h = _rmsnorm(residual, ln2_w)
        gate_pre = h @ W_in_base.T + mod * (h @ A) @ B
        gate = jax.nn.silu(gate_pre)
        up = h @ W_up_base.T
        mlp_out = gate * up @ W_down.T
        return residual + mlp_out
    x = L0_attn_hidden_states
    xn = _layernorm(x, axis=-1)
    x = x + _L0_attn_ref(xn, L0_attn_wq, L0_attn_wk, L0_attn_wv, L0_attn_wo, L0_attn_lambda_q1, L0_attn_lambda_k1, L0_attn_lambda_q2, L0_attn_lambda_k2) + _L0_ffn_ref(xn, L0_ffn_ln1_w, L0_ffn_ln2_w, L0_ffn_Wq, L0_ffn_Wk, L0_ffn_Wv, L0_ffn_Wo, L0_ffn_A, L0_ffn_B, L0_ffn_W_in_base, L0_ffn_W_up_base, L0_ffn_W_down)
    return x

_drawn_inputs = setup_inputs


def setup_inputs(seed=0):
    import zlib

    import numpy as np

    out = dict(_drawn_inputs(seed))
    spreads = {'L0_ffn_ln1_w': (1.0, 0.6), 'L0_ffn_ln2_w': (1.0, 0.6)}
    factors = {'L0_attn_wq': 8.0,
     'L0_attn_wk': 8.0,
     'L0_attn_wv': 8.0,
     'L0_attn_wo': 8.0,
     'L0_attn_lambda_q1': 8.0,
     'L0_attn_lambda_k1': 8.0,
     'L0_attn_lambda_q2': 8.0,
     'L0_attn_lambda_k2': 8.0,
     'L0_ffn_Wq': 200.0,
     'L0_ffn_Wk': 200.0,
     'L0_ffn_Wv': 200.0,
     'L0_ffn_Wo': 200.0,
     'L0_ffn_A': 200.0,
     'L0_ffn_B': 200.0}
    for name, (base, spread) in spreads.items():
        noise = np.random.default_rng([zlib.crc32(name.encode()), seed]).standard_normal(out[name].shape)
        drawn = base * np.exp(spread * noise) if base else spread * noise
        out[name] = jnp.asarray(drawn.astype(out[name].dtype))
    for name, factor in factors.items():
        out[name] = (out[name] * factor).astype(out[name].dtype)
    return out
```

```python
from contextlib import ExitStack
import math

import numpy as np

import concourse.bass as bass
from concourse import mybir
from concourse.alu_op_type import AluOpType as ALU

F32 = mybir.dt.float32
BF16 = mybir.dt.bfloat16
F32R = mybir.dt.float32r
ACT = mybir.ActivationFunctionType
AX = mybir.AxisListType

P = 128
B, S, H = 2, 1024, 512
TOK = B * S
CH = 512
NCH = TOK // CH
KT = H // P
TT = CH // P
QB = S // P

NH0, NKV, D0 = 32, 8, 16
REP = NH0 // NKV
NQ0 = 2 * NH0 * D0 // P
NK0 = 2 * NKV * D0 // P
N0 = (2 * NH0 + 2 * NKV + NKV) * D0
NH1, D1, RK = 16, 32, 16
N1 = 2 * NH1 * D1
F = 2048
VW = D0 + 1
LAMBDA_INIT = 0.8 - 0.6 * math.exp(-0.3 * 12)
LN_EPS, RMS_EPS, MOD_SCALE = 1e-5, 1e-6, 0.1
NEG = -1e30

HI, LO = 0, 1
PASSES = ((HI, HI), (HI, LO), (LO, HI))


def f32(ap):
    return ap.bitcast(F32)


def weights_block(nc, ins, w0, w1, wp, ident):
    with ExitStack() as ctx:
        def sb(name, shape, dt=F32):
            return ctx.enter_context(nc.sbuf_tensor(name, shape, dt))

        def sem(name):
            return ctx.enter_context(nc.semaphore(name))

        raw0 = sb("raw0", [P, KT, N0])
        raw1 = sb("raw1", [P, KT, N1])
        wv = sb("wv_rows", [P, KT, H])
        wo = sb("wo_rows", [P, KT, H])
        a = sb("a_rows", [P, KT, RK])
        woa = sb("woa_heads", [P, KT, P // D1, RK])
        ps_woa = ctx.enter_context(nc.psum_tensor("ps_woa", [P, KT, RK], F32))
        ps_wp = ctx.enter_context(nc.psum_tensor("ps_wp", [P, KT, NH1 * RK], F32))

        small_loaded = sem("small_loaded")
        raw_loaded = [sem(f"raw_loaded{n}") for n in range(2)]
        woa_zeroed = sem("woa_zeroed")
        ident_zeroed = sem("ident_zeroed")
        ident_ready = sem("ident_ready")
        woa_summed = sem("woa_summed")
        woa_ready = sem("woa_ready")
        wp_summed = sem("wp_summed")
        hi_ready = sem("hi_ready")
        lo_ready = sem("lo_ready")
        block = ctx.enter_context(nc.Block())

        @block.sync
        def _(sp):
            sp.dma_start(wo[:], ins["wo1"].rearrange("(k p) n -> p k n", p=P)).then_inc(small_loaded, 16)
            sp.dma_start(a[:], ins["a"].rearrange("(k p) n -> p k n", p=P)).then_inc(small_loaded, 16)
            sp.dma_start(wv[:], ins["wv1"].rearrange("(k p) n -> p k n", p=P)).then_inc(small_loaded, 16)
            sp.dma_start(raw0[:], ins["w0t"].rearrange("(k p) n -> p k n", p=P)).then_inc(raw_loaded[0], 16)
            sp.dma_start(raw1[:], ins["w1t"].rearrange("(k p) n -> p k n", p=P)).then_inc(raw_loaded[1], 16)

        @block.gpsimd
        def _(pool):
            nc.gpsimd.memset(woa[:], 0.0).then_inc(woa_zeroed, 1)
            nc.gpsimd.memset(ident[:], 0.0).then_inc(ident_zeroed, 1)
            pool.wait_ge(ident_zeroed, 1)
            nc.gpsimd.affine_select(out=ident[:], in_=ident[:], compare_op=ALU.not_equal, fill=1.0,
                                    base=0, pattern=[[-1, P]], channel_multiplier=1).then_inc(ident_ready, 1)
            pool.wait_ge(ident_ready, 1)

        @block.tensor
        def _(pe):
            pe.wait_ge(small_loaded, 48)
            for m in range(KT):
                for k in range(KT):
                    mm = nc.tensor.matmul(ps_woa[:, m, :], wo[:, k, m * P:(m + 1) * P], a[:, k, :],
                                          start=(k == 0), stop=(k == KT - 1))
            mm.then_inc(woa_summed, 1)
            pe.wait_ge(woa_ready, P // D1)
            for n in range(KT):
                for m in range(KT):
                    mm = nc.tensor.matmul(ps_wp[:, n, m * 64:(m + 1) * 64], wv[:, m, n * P:(n + 1) * P],
                                          woa[:, m, :, :], start=True, stop=True)
            mm.then_inc(wp_summed, 1)

        @block.vector
        def _(dve):
            dve.wait_ge(woa_zeroed, 1)
            dve.wait_ge(woa_summed, 1)
            for j in range(P // D1):
                rows = slice(j * D1, (j + 1) * D1)
                nc.vector.tensor_copy(woa[rows, :, j, :], ps_woa[rows]).then_inc(woa_ready, 1)
            dve.wait_ge(hi_ready, 1)
            nc.vector.tensor_tensor(wp[:, LO], ps_wp[:], f32(wp[:, HI]), ALU.subtract).then_inc(lo_ready, 1)
            for n, (raw, w) in enumerate(((raw0, w0), (raw1, w1))):
                dve.wait_ge(hi_ready, n + 2)
                nc.vector.tensor_tensor(w[:, LO], raw[:], f32(w[:, HI]), ALU.subtract).then_inc(lo_ready, 1)
            dve.wait_ge(lo_ready, 3)

        @block.scalar
        def _(act):
            act.wait_ge(wp_summed, 1)
            nc.scalar.copy(wp[:, HI], ps_wp[:]).then_inc(hi_ready, 1)
            for n, (raw, w) in enumerate(((raw0, w0), (raw1, w1))):
                act.wait_ge(raw_loaded[n], 16)
                nc.scalar.copy(w[:, HI], raw[:]).then_inc(hi_ready, 1)
            act.wait_ge(hi_ready, 3)


L0_TILES = NQ0 + NK0
L1_TILES = N1 // P
TILES = L0_TILES + L1_TILES
V_UNITS = 2
UNITS = TILES + 2 * V_UNITS
L0_FIRST, L0_V, L1_FIRST, L1_V = 0, L0_TILES, L0_TILES + V_UNITS, L0_TILES + V_UNITS + L1_TILES
XN_JOBS, XS_JOBS = KT, 2 * KT
JOBS = XN_JOBS + XS_JOBS
NORM_STEPS = 12


def project_block(nc, ins, scr, w0, w1, wp, v0, v1, ident):
    with ExitStack() as ctx:
        def sb(name, shape, dt=F32):
            return ctx.enter_context(nc.sbuf_tensor(name, shape, dt))

        def sem(name):
            return ctx.enter_context(nc.semaphore(name))

        def psum(name, shape):
            return ctx.enter_context(nc.psum_tensor(name, shape, F32))

        cos = sb("cos", [P, S])
        sin = sb("sin", [P, S])
        ln1 = sb("ln1", [P, KT])
        ln2 = sb("ln2", [P, KT])
        xin = sb("xin", [P, TT, H])
        xn = sb("xn", [P, TT, H])
        stats = sb("stats", [P, TT, 6])
        mv = sb("mean_var", [P, TT, 2])
        var = sb("var", [P, 2, TT])
        inv = sb("inv", [P, 2, TT])
        root = sb("root", [P, 2, TT])
        newt = sb("newton", [P, 2, TT])
        sq = sb("square_sum", [P, TT])
        junk = sb("square", [P, H])
        y = sb("turned", [P, 4, CH])
        xnt = sb("xnt", [P, 2, KT, CH], F32R)
        x1t = sb("x1t", [P, 2, KT, CH], F32R)
        ht = sb("ht", [P, 2, 2, CH], F32R)
        qs = sb("q_raw", [P, 2, CH])
        qc = sb("q_cos", [P, 2, CH])
        qr = sb("q_rot", [P, 2, CH])
        parts = sb("q_parts", [P, 2, 2, CH], F32R)
        pj = psum("pj", [P, 2, CH])
        tp = psum("tp", [P, KT, CH])

        consts_loaded = sem("consts_loaded")
        ones_ready = sem("ones_ready")
        x_loaded = sem("x_loaded")
        norm_step = sem("norm_step")
        inv_ready = sem("inv_ready")
        root_ready = sem("root_ready")
        xn_ready = sem("xn_ready")
        squared = sem("squared")
        resid_ready = sem("resid_ready")
        resid_stored = sem("resid_stored")
        xs_ready = sem("xs_ready")
        turned = sem("turned")
        y_ready = sem("y_ready")
        split_hi = sem("split_hi")
        split_done = sem("split_done")
        h_stored = [sem(f"h_stored{n}") for n in range(2)]
        proj_done = sem("proj_done")
        proj_read = sem("proj_read")
        q_taken = sem("q_taken")
        cos_done = sem("cos_done")
        sin_done = sem("sin_done")
        rope_sum = sem("rope_sum")
        rope_hi = sem("rope_hi")
        rope_lo = sem("rope_lo")
        plain_hi = sem("plain_hi")
        plain_lo = sem("plain_lo")
        q_stored = [sem(f"q_stored{n}") for n in range(2)]
        block = ctx.enter_context(nc.Block())

        def first_job(ch, xs):
            return ch * JOBS + (XN_JOBS if xs else 0)

        @block.sync
        def _(sp):
            sp.dma_start(xin[:], ins["x"][0:CH].rearrange("(t p) n -> p t n", p=P)).then_inc(x_loaded, 16)
            sp.dma_start(cos[:], ins["cos"]).then_inc(consts_loaded, 16)
            sp.dma_start(sin[:], ins["sin"]).then_inc(consts_loaded, 16)
            sp.dma_start(ln1[:], ins["ln1"]).then_inc(consts_loaded, 16)
            sp.dma_start(ln2[:], ins["ln2"]).then_inc(consts_loaded, 16)

            def residual_store(ch):
                sp.wait_ge(resid_ready, TT * ch + TT)
                sp.dma_start(scr["resid"][bass.ds(ch * CH, CH)].rearrange("(t p) n -> p t n", p=P),
                             xin[:]).then_inc(resid_stored, 16)

            def parts_store(dst, ready, count, slot):
                sp.wait_ge(ready, count)
                sp.nop(nofuse=True)
                sp.dma_start(dst, f32(parts[:, slot])).then_inc(q_stored[slot], 16)

            def chunk(ch, last):
                b, col = ch // 2, (ch % 2) * CH
                for t in range(5):
                    rope_store(ch, t, b, col)
                h_store(ch)
                for t in range(5, L0_TILES):
                    rope_store(ch, t, b, col)
                for t in range(4):
                    plain_store(ch, t, b, col)
                if not last:
                    sp.wait_ge(resid_stored, 16 * ch + 16)
                    sp.nop(nofuse=True)
                    sp.dma_start(xin[:], ins["x"][bass.ds((ch + 1) * CH, CH)].rearrange(
                        "(t p) n -> p t n", p=P)).then_inc(x_loaded, 16)
                for t in range(4, L1_TILES):
                    plain_store(ch, t, b, col)
                if not last:
                    residual_store(ch + 1)

            def rope_store(ch, t, b, col):
                s, m = (t // (NQ0 // 2), t % (NQ0 // 2)) if t < NQ0 else (t - NQ0, 0)
                dst = scr["q0"] if t < NQ0 else scr["k0"]
                rows = (NH0 if t < NQ0 else NKV) * D0
                parts_store(dst[bass.ds(b * rows + m * P, P), s, :, bass.ds(col, CH)],
                            rope_lo, ch * L0_TILES + t + 3, t % 2)

            def plain_store(ch, t, b, col):
                dst = scr["q1"] if t < L1_TILES // 2 else scr["k1"]
                parts_store(dst[bass.ds(b * H + (t % (L1_TILES // 2)) * P, P), :, bass.ds(col, CH)],
                            plain_lo, ch * L1_TILES + t + 1, t % 2)

            def h_store(ch):
                for k in range(KT):
                    sp.wait_ge(split_done, first_job(ch, True) + 2 * k + 2 + 4)
                    sp.nop(nofuse=True)
                    sp.dma_start(scr["h"][:, :, k, bass.ds(ch * CH, CH)], f32(ht[:, k % 2])).then_inc(h_stored[k % 2], 16)

            residual_store(0)
            with sp.Fori(0, NCH - 1) as ch:
                chunk(ch, False)
            chunk(NCH - 1, True)
            sp.wait_ge(resid_stored, 16 * NCH)
            for n in range(2):
                sp.wait_ge(q_stored[n], 16 * NCH * TILES // 2 + 16)
                sp.wait_ge(h_stored[n], 16 * NCH * KT // 2 + 16)

        @block.tensor
        def _(pe):
            def turn(ch, xs):
                for k in range(KT):
                    if xs:
                        if k == 0:
                            pe.wait_ge(xs_ready, TT * ch + TT)
                        pe.wait_ge(y_ready, first_job(ch, False) + k + 1)
                    else:
                        if k == 0:
                            pe.wait_ge(xn_ready, TT * ch + TT)
                        if not (isinstance(ch, int) and ch == 0):
                            pe.wait_ge(y_ready, first_job(ch, False) - XS_JOBS + 2 * k + 2)
                    pe.nop(nofuse=True)
                    for t in range(TT):
                        mm = nc.tensor.transpose(tp[:, k, t * P:(t + 1) * P], xn[:, t, k * P:(k + 1) * P], ident[:])
                    mm.then_inc(turned, 1)

            def features(ch, u, w, col, xt):
                pe.wait_ge(proj_read, ch * UNITS + u + 1)
                pe.nop(nofuse=True)
                for k in range(KT):
                    for n, (a, c) in enumerate(PASSES):
                        mm = nc.tensor.matmul(pj[:, u % 2, :], w[:, a, k, col:col + P], xt[:, c, k, :],
                                              start=(k == 0 and n == 0), stop=(k == KT - 1 and n == 2))
                mm.then_inc(proj_done, 1)

            def values(ch, u, w, col, xt):
                pe.wait_ge(proj_read, ch * UNITS + u + 1)
                pe.nop(nofuse=True)
                for h in range(2):
                    t = 2 * (u % 2) + h
                    for k in range(KT):
                        for n, (a, c) in enumerate(PASSES):
                            mm = nc.tensor.matmul(pj[:, u % 2, h * 256:h * 256 + 256], xt[:, a, k, t * P:(t + 1) * P],
                                                  w[:, c, k, col:col + 256],
                                                  start=(k == 0 and n == 0), stop=(k == KT - 1 and n == 2))
                mm.then_inc(proj_done, 1)

            def chunk(ch, last):
                pe.wait_ge(split_done, first_job(ch, False) + XN_JOBS + 4)
                for t in range(5):
                    features(ch, L0_FIRST + t, w0, t * P, xnt)
                turn(ch, True)
                for t in range(5, L0_TILES):
                    features(ch, L0_FIRST + t, w0, t * P, xnt)
                for n in range(V_UNITS):
                    values(ch, L0_V + n, w0, N0 - 256, xnt)
                pe.wait_ge(split_done, first_job(ch, True) + XS_JOBS + 4)
                for t in range(4):
                    features(ch, L1_FIRST + t, w1, t * P, x1t)
                if not last:
                    turn(ch + 1, False)
                for t in range(4, L1_TILES):
                    features(ch, L1_FIRST + t, w1, t * P, x1t)
                for n in range(V_UNITS):
                    values(ch, L1_V + n, wp, 0, x1t)

            turn(0, False)
            with pe.Fori(0, NCH - 1) as ch:
                chunk(ch, False)
            chunk(NCH - 1, True)

        @block.scalar
        def _(act):
            act.sem_inc(proj_read, 2)
            act.wait_ge(consts_loaded, 64)

            def roots(ch):
                act.wait_ge(inv_ready, 2 * ch + 1)
                act.nop(nofuse=True)
                nc.scalar.activation(root[:, 0], inv[:, 0], ACT.Sqrt).then_inc(root_ready, 1)
                for t in range(TT):
                    act.wait_ge(xn_ready, TT * ch + t + 1)
                    act.nop(nofuse=True)
                    if t > 0:
                        act.wait_ge(squared, TT * ch + t)
                        act.nop(nofuse=True)
                    nc.scalar.activation(junk[:], xn[:, t], ACT.Square, accum_out=sq[:, t:t + 1]).then_inc(squared, 1)
                act.wait_ge(inv_ready, 2 * ch + 2)
                act.nop(nofuse=True)
                nc.scalar.activation(root[:, 1], inv[:, 1], ACT.Sqrt).then_inc(root_ready, 1)

            def read_turned(ch, xs):
                for k in range(KT):
                    act.wait_ge(turned, ch * 2 * KT + (KT if xs else 0) + k + 1)
                    act.nop(nofuse=True)
                    for n in range(2 if xs else 1):
                        job = first_job(ch, xs) + (2 * k + n if xs else k)
                        slot = (2 * k + n) % 4 if xs else k
                        act.wait_ge(split_done, job + 1)
                        act.nop(nofuse=True)
                        if xs:
                            nc.scalar.activation(y[:, slot], tp[:, k], ACT.Copy,
                                                 scale=(ln1, ln2)[n][:, k:k + 1]).then_inc(y_ready, 1)
                        else:
                            nc.scalar.copy(y[:, slot], tp[:, k]).then_inc(y_ready, 1)

            def read_tile(ch, u, q):
                act.wait_ge(proj_done, ch * UNITS + u + 1)
                act.nop(nofuse=True)
                act.wait_ge(q_taken, ch * TILES + q + 1)
                act.nop(nofuse=True)
                nc.scalar.copy(qs[:, q % 2], pj[:, u % 2]).then_inc(proj_read, 1)

            def read_values(ch, u, heads, off, dst):
                act.wait_ge(proj_done, ch * UNITS + u + 1)
                act.nop(nofuse=True)
                b, half = ch // 2, ch % 2
                for h in range(2):
                    tb = half * TT + 2 * (u % 2) + h
                    src = pj[:, u % 2, h * 256 + off:h * 256 + off + heads * D0].rearrange("p (h d) -> p h d", d=D0)
                    cp = nc.scalar.copy(dst(b, tb), src)
                cp.then_inc(proj_read, 1)

            def v0_at(b, tb):
                return v0[:, bass.ds(b * (NKV * QB) + tb, NKV, QB), 0:D0]

            def v1_at(b, tb):
                return v1[:, bass.ds(b * (NH1 * QB) + tb, NH1, QB), 0:D0]

            def chunk(ch, last):
                for t in range(5):
                    read_tile(ch, L0_FIRST + t, t)
                read_turned(ch, True)
                for t in range(5, L0_TILES):
                    read_tile(ch, L0_FIRST + t, t)
                for n in range(V_UNITS):
                    read_values(ch, L0_V + n, NKV, P, v0_at)
                for t in range(4):
                    read_tile(ch, L1_FIRST + t, L0_TILES + t)
                if not last:
                    roots(ch + 1)
                    read_turned(ch + 1, False)
                for t in range(4, L1_TILES):
                    read_tile(ch, L1_FIRST + t, L0_TILES + t)
                for n in range(V_UNITS):
                    read_values(ch, L1_V + n, NH1, 0, v1_at)
                if not last:
                    rms_scale(ch + 1)

            def rms_scale(ch):
                act.wait_ge(turned, ch * 2 * KT + KT)
                act.nop(nofuse=True)
                act.wait_ge(resid_ready, TT * ch + TT)
                act.nop(nofuse=True)
                act.wait_ge(norm_step, NORM_STEPS * ch + NORM_STEPS)
                act.nop(nofuse=True)
                for t in range(TT):
                    nc.scalar.activation(xn[:, t], xn[:, t], ACT.Copy, scale=root[:, 1, t:t + 1]).then_inc(xs_ready, 1)

            roots(0)
            read_turned(0, False)
            rms_scale(0)
            with act.Fori(0, NCH - 1) as ch:
                chunk(ch, False)
            chunk(NCH - 1, True)

        @block.vector
        def _(dve):
            nc.vector.memset(v0[:, :, D0:VW], 1.0).then_inc(ones_ready, 1)
            nc.vector.memset(v1[:, :, D0:VW], 1.0).then_inc(ones_ready, 1)
            dve.sem_inc(split_done, 4)
            dve.sem_inc(q_taken, 2)
            dve.sem_inc(rope_lo, 2)

            def step(ch, n, ins_):
                ins_.then_inc(norm_step, 1)
                dve.wait_ge(norm_step, NORM_STEPS * ch + n)
                dve.nop(nofuse=True)

            def inverse_root(ch, n, first):
                dve.wait_ge(root_ready, 2 * ch + n + 1)
                dve.nop(nofuse=True)
                step(ch, first, nc.vector.tensor_tensor(newt[:, n], root[:, n], root[:, n], ALU.mult))
                step(ch, first + 1, nc.vector.tensor_tensor(newt[:, n], newt[:, n], var[:, n], ALU.mult))
                step(ch, first + 2, nc.vector.tensor_scalar(newt[:, n], newt[:, n], -0.5, 1.5, ALU.mult, ALU.add))
                step(ch, first + 3, nc.vector.tensor_tensor(root[:, n], root[:, n], newt[:, n], ALU.mult))

            def norms(ch):
                dve.wait_ge(x_loaded, 16 * ch + 16)
                dve.nop(nofuse=True)
                for t in range(TT):
                    bn = nc.vector.bn_stats(stats[:, t], xin[:, t])
                step(ch, 1, bn)
                for t in range(TT):
                    bn = nc.vector.bn_aggr(mv[:, t], stats[:, t])
                step(ch, 2, bn)
                step(ch, 3, nc.vector.tensor_scalar(var[:, 0], mv[:, :, 1], LN_EPS, None, ALU.add))
                nc.vector.reciprocal(inv[:, 0], var[:, 0]).then_inc(inv_ready, 1)
                inverse_root(ch, 0, 4)
                if not (isinstance(ch, int) and ch == 0):
                    dve.wait_ge(turned, ch * 2 * KT)
                    dve.nop(nofuse=True)
                for t in range(TT):
                    nc.vector.tensor_scalar(xn[:, t], xin[:, t], mv[:, t, 0:1], root[:, 0, t:t + 1],
                                            ALU.subtract, ALU.mult).then_inc(xn_ready, 1)
                dve.wait_ge(squared, TT * ch + TT)
                dve.nop(nofuse=True)
                step(ch, 8, nc.vector.tensor_scalar(var[:, 1], sq[:], 1.0 / H, RMS_EPS, ALU.mult, ALU.add))
                nc.vector.reciprocal(inv[:, 1], var[:, 1]).then_inc(inv_ready, 1)
                inverse_root(ch, 1, 9)

            def split(ch, xs):
                for k in range(KT):
                    for n in range(2 if xs else 1):
                        job = first_job(ch, xs) + (2 * k + n if xs else k)
                        slot = (2 * k + n) % 4 if xs else k
                        dve.wait_ge(y_ready, job + 1)
                        dve.nop(nofuse=True)
                        if not xs:
                            hi, lo = xnt[:, HI, k], xnt[:, LO, k]
                            if k == 0 and not (isinstance(ch, int) and ch == 0):
                                dve.wait_ge(proj_done, ch * UNITS - UNITS + L1_FIRST)
                                dve.nop(nofuse=True)
                        elif n == 0:
                            hi, lo = x1t[:, HI, k], x1t[:, LO, k]
                            if k == 0:
                                dve.wait_ge(proj_done, ch * UNITS + 1)
                                dve.nop(nofuse=True)
                        else:
                            hi, lo = ht[:, k % 2, HI], ht[:, k % 2, LO]
                            dve.wait_ge(h_stored[k % 2], 32 * ch + 16 * (k // 2) + 16)
                            dve.nop(nofuse=True)
                        nc.vector.tensor_copy(hi, y[:, slot]).then_inc(split_hi, 1)
                        dve.wait_ge(split_hi, job + 1)
                        dve.nop(nofuse=True)
                        nc.vector.tensor_tensor(lo, y[:, slot], f32(hi), ALU.subtract).then_inc(split_done, 1)

            def rope_start(ch, t):
                s = t % 2
                dve.wait_ge(proj_read, ch * UNITS + t + 3)
                dve.nop(nofuse=True)
                dve.wait_ge(rope_lo, ch * L0_TILES + t + 1)
                dve.nop(nofuse=True)
                nc.vector.tensor_tensor(qc[:, s], qs[:, s], cos[:, bass.ds((ch % 2) * CH, CH)], ALU.mult).then_inc(cos_done, 1)
                nc.vector.stream_shuffle(qr[:, s], qs[:, s],
                                         [p // 16 * 16 + (p + 8) % 16 for p in range(32)]).then_inc(q_taken, 1)

            def rope_end(ch, t):
                s = t % 2
                n = ch * L0_TILES + t + 1
                dve.wait_ge(cos_done, n)
                dve.nop(nofuse=True)
                dve.wait_ge(sin_done, n)
                dve.nop(nofuse=True)
                nc.vector.tensor_tensor(qc[:, s], qc[:, s], qr[:, s], ALU.add).then_inc(rope_sum, 1)
                dve.wait_ge(rope_sum, n)
                dve.nop(nofuse=True)
                dve.wait_ge(q_stored[s], 16 * (ch * (TILES // 2) + t // 2 + 1))
                dve.nop(nofuse=True)
                nc.vector.tensor_copy(parts[:, s, HI], qc[:, s]).then_inc(rope_hi, 1)

            def plain(ch, t):
                s = t % 2
                n = ch * L1_TILES + t + 1
                dve.wait_ge(proj_read, ch * UNITS + L1_FIRST + t + 3)
                dve.nop(nofuse=True)
                dve.wait_ge(q_stored[s], 16 * (ch * (TILES // 2) + L0_TILES // 2 + t // 2 + 1))
                dve.nop(nofuse=True)
                nc.vector.tensor_copy(parts[:, s, HI], qs[:, s]).then_inc(plain_hi, 1)
                dve.wait_ge(plain_hi, n)
                dve.nop(nofuse=True)
                nc.vector.tensor_tensor(parts[:, s, LO], qs[:, s], f32(parts[:, s, HI]), ALU.subtract).then_inc(plain_lo, 1)
                dve.wait_ge(plain_lo, n)
                dve.sem_inc(q_taken, 1)

            def chunk(ch, last):
                for t in range(5):
                    rope_start(ch, t)
                    if t:
                        rope_end(ch, t - 1)
                rope_end(ch, 4)
                split(ch, True)
                for t in range(5, L0_TILES):
                    rope_start(ch, t)
                    if t > 5:
                        rope_end(ch, t - 1)
                rope_end(ch, L0_TILES - 1)
                for t in range(4):
                    plain(ch, t)
                if not last:
                    norms(ch + 1)
                    split(ch + 1, False)
                for t in range(4, L1_TILES):
                    plain(ch, t)

            dve.sem_inc(h_stored[0], 16)
            dve.sem_inc(h_stored[1], 16)
            dve.sem_inc(q_stored[0], 16)
            dve.sem_inc(q_stored[1], 16)
            norms(0)
            split(0, False)
            with dve.Fori(0, NCH - 1) as ch:
                chunk(ch, False)
            chunk(NCH - 1, True)

        @block.gpsimd
        def _(pool):
            pool.wait_ge(consts_loaded, 64)

            def residual(ch):
                for t in range(TT):
                    pool.wait_ge(xn_ready, TT * ch + t + 1)
                    pool.nop(nofuse=True)
                    nc.gpsimd.tensor_tensor(xin[:, t], xin[:, t], xn[:, t], ALU.add).then_inc(resid_ready, 1)

            def rope_sin(ch, t):
                s = t % 2
                pool.wait_ge(q_taken, ch * TILES + t + 3)
                pool.nop(nofuse=True)
                nc.gpsimd.tensor_tensor(qr[:, s], qr[:, s], sin[:, bass.ds((ch % 2) * CH, CH)], ALU.mult).then_inc(sin_done, 1)

            def rope_low(ch, t):
                s = t % 2
                pool.wait_ge(rope_hi, ch * L0_TILES + t + 1)
                pool.nop(nofuse=True)
                nc.gpsimd.tensor_tensor(parts[:, s, LO], qc[:, s], f32(parts[:, s, HI]), ALU.subtract).then_inc(rope_lo, 1)

            def chunk(ch, last):
                for first, end in ((0, 5), (5, L0_TILES)):
                    for t in range(first, end):
                        rope_sin(ch, t)
                        if t > first:
                            rope_low(ch, t - 1)
                    rope_low(ch, end - 1)
                if not last:
                    residual(ch + 1)

            residual(0)
            with pool.Fori(0, NCH - 1) as ch:
                chunk(ch, False)
            chunk(NCH - 1, True)


MAPS = 4
RING = 4
HALF = 512
PIECES = tuple((i, k, min(HALF, P * (i + 1) - k)) for i in range(QB) for k in range(0, P * (i + 1), HALF))
NP = len(PIECES)
STEPS = tuple((c, j) for c in range(S // HALF) for j in range((c + 1) * HALF // P))
NS = len(STEPS)
DIAGONAL = tuple(s for s, (c, j) in enumerate(STEPS) if P * j >= HALF * c)
TURNS = 3
PROBS = 3
EARLY = 16
LAG = 2
SLOTS = NS
FP32R_LEAST = 256


class Layer:

    def __init__(self, name, d, groups, combos, own_keys, scale):
        self.name, self.d, self.groups = name, d, groups
        self.combos = combos
        self.kmaps = MAPS if own_keys else 1
        self.scale = scale
        self.max_row = len(combos) * d
        self.loads = 2 * len(combos) + 1


def attention_block(nc, lay, q_scr, k_scr, zero_rows, v, out, neg_lambda, ident):
    differential = neg_lambda is not None
    groups = lay.groups
    with ExitStack() as ctx:
        def sb(name, shape, dt=F32):
            return ctx.enter_context(nc.sbuf_tensor(f"{lay.name}_{name}", shape, dt))

        def sem(name):
            return ctx.enter_context(nc.semaphore(f"{lay.name}_{name}"))

        def psum(name, shape):
            return ctx.enter_context(nc.psum_tensor(f"{lay.name}_{name}", shape, F32))

        qst = sb("q_stack", [P, RING, MAPS, S], F32R)
        kst = sb("k_stack", [P, RING, lay.kmaps, S], F32R)
        vst = sb("v_stack", [P, 2, lay.kmaps, QB, 32])
        mask = sb("mask", [P, HALF + P])
        ident_b = sb("ident_b", [P, P], BF16)
        future = sb("future", [P, P], BF16)
        tops = sb("tops", [P, 2, MAPS, QB])
        pair = sb("pair", [P, 2, MAPS, QB // 2, 2])
        ntop = sb("neg_top", [P, 2, MAPS, QB])
        ntop_r = sb("neg_top_hi", [P, MAPS, QB], F32R)
        mrow = sb("max_rows", [P, P])
        probs = sb("probs", [P, PROBS, MAPS, HALF])
        osb = sb("out_t", [P, 2, HALF])
        rec = sb("recip", [P, 2, QB // 2 * MAPS])
        kept = sb("kept", [P, 2, QB // 2, MAPS * D0])
        prod = sb("prod", [P, QB // 2, MAPS * D0])
        result = sb("result", [P, 2, QB // 2, MAPS * D0])
        ps_s = psum("scores", [P, 2, HALF])
        ps_t = psum("scores_t", [P, 2, 2, HALF])
        ps_o = psum("out", [P, HALF])
        ps_x = psum("turn", [P, HALF])

        loaded = [sem(f"loaded{u}") for u in range(RING)]
        pad_set = sem("pad_set")
        ones_set = sem("ones_set")
        mask_zero = sem("mask_zero")
        mask_ready = sem("mask_ready")
        v_zeroed = sem("v_zeroed")
        v_ready = sem("v_ready")
        scored = sem("scored")
        topped = sem("topped")
        top_step = sem("top_step")
        tops_split = sem("tops_split")
        turned = sem("turned")
        turn_read = sem("turn_read")
        rows_read = sem("rows_read")
        rows_set = sem("rows_set")
        scored_t = sem("scored_t")
        exped = sem("exped")
        future_ready = sem("future_ready")
        summed = sem("summed")
        out_read = sem("out_read")
        rec_done = sem("rec_done")
        prod_done = sem("prod_done")
        stored = [sem(f"stored{c}") for c in range(2)]
        divided = sem("divided")
        block = ctx.enter_context(nc.Block())

        UNITS_T = 2 * NS
        PIECES_G = MAPS * NP
        ROWS_AT, OUT0_AT = 8, 4
        rest = [EARLY + (PIECES_G - EARLY) * k // 7 for k in range(8)] + [PIECES_G] * 5
        early = [0] * 8 + [EARLY * (k + 1) // 5 for k in range(5)]

        def iterate(eng, body):
            rounds = groups // RING
            with eng.Fori(0, rounds - 1) as i:
                for u in range(RING):
                    body(i, u, RING)
            for u in range(RING):
                body(rounds - 1, u, RING - 1 - u)

        def after(i, u, n):
            return i * RING + (u + n), (u + n) % RING, i + (u + n) // RING

        def steps_of(i, u, ahead):
            own = [(i, u, s) for s in range(LAG, NS)]
            g, slot, rnd = after(i, u, 1)
            return own + ([(rnd, slot, s) for s in range(LAG)] if ahead else [])

        @block.sync
        def _(sp):
            def load(rnd, u):
                rows = MAPS * lay.d
                g = rnd * RING + u
                pairs = rnd * (RING // 2) + u // 2
                for n, (a, c) in enumerate(lay.combos):
                    at = slice(n * lay.d, (n + 1) * lay.d)
                    if differential:
                        q_src = q_scr[bass.ds(pairs * rows, rows), u % 2, a, :]
                        k_src = k_scr[bass.ds(pairs * lay.d, lay.d), u % 2, c, :]
                    else:
                        q_src = q_scr[bass.ds(g * rows, rows), a, :]
                        k_src = k_scr[bass.ds(g * rows, rows), c, :]
                    sp.dma_start(f32(qst[at, u]), q_src.rearrange("(m d) n -> d m n", m=MAPS)).then_inc(loaded[u], 16)
                    sp.dma_start(f32(kst[at, u]), k_src.rearrange("(m d) n -> d m n", m=lay.kmaps)).then_inc(loaded[u], 16)
                sp.dma_start(f32(qst[lay.max_row:lay.max_row + 2, u]), zero_rows).then_inc(loaded[u], 16)

            def set_rows(g, slot):
                sp.wait_ge(rows_read, g + 1)
                sp.nop(nofuse=True)
                for a in range(2):
                    row = f32(qst[lay.max_row + a:lay.max_row + a + 1, slot])
                    sp.dma_start(row.rearrange("o m (i n) -> o (m i) n", n=P),
                                 mrow[a * 32:a * 32 + 32]).then_inc(rows_set, 16)

            def store(i, u, c):
                n = i * (RING // 2) + u // 2 if differential else i * RING + u
                sp.wait_ge(divided, 2 * n + c + 1)
                sp.nop(nofuse=True)
                sp.dma_start(out[:, bass.ds(n * QB + c * (QB // 2), QB // 2), :], result[:, c]).then_inc(stored[c], 16)

            def body(i, u, ahead):
                stores = u % 2 or not differential
                if stores:
                    store(i, u, 0)
                if ahead:
                    g, slot, _ = after(i, u, 1)
                    set_rows(g, slot)
                if ahead == RING:
                    sp.wait_ge(scored_t, UNITS_T * (i * RING + u + 1))
                    sp.nop(nofuse=True)
                    load(i + 1, u)
                if stores:
                    store(i, u, 1)

            sp.wait_ge(pad_set, RING)
            for u in range(RING):
                load(0, u)
            set_rows(0, 0)
            iterate(sp, body)
            for c in range(2):
                sp.wait_ge(stored[c], 16 * (groups // 2 if differential else groups) + 16)

        @block.tensor
        def _(pe):
            pe.sem_inc(summed, PROBS)

            def pieces(i, u, n, ns):
                g, slot, rnd = after(i, u, n)
                for n in ns:
                    m, (r, k0, keys) = n // NP, PIECES[n % NP]
                    if n == 0:
                        pe.wait_ge(loaded[slot], rnd * (16 * lay.loads) + 16 * lay.loads)
                        pe.nop(nofuse=True)
                    pe.wait_ge(topped, g * PIECES_G + n + 1)
                    pe.nop(nofuse=True)
                    width = max(keys, FP32R_LEAST)
                    nc.tensor.matmul(ps_s[:, n % 2, 0:width], qst[:, slot, m, r * P:(r + 1) * P],
                                     kst[:, slot, m % lay.kmaps, k0:k0 + width],
                                     start=True, stop=True).then_inc(scored, 1)

            def turn_rows(g, turn):
                pe.wait_ge(tops_split, g + 1)
                pe.nop(nofuse=True)
                if turn is not None:
                    pe.wait_ge(turn_read, turn)
                    pe.nop(nofuse=True)
                nc.tensor.transpose(ps_x[0:64, 0:P], ntop[:].rearrange("p a m i -> p (a m i)"), ident[:]).then_inc(turned, 1)

            def turn_out(g, c, turn):
                pe.wait_ge(out_read, 2 * g + c + 1)
                pe.nop(nofuse=True)
                pe.wait_ge(turn_read, turn)
                pe.nop(nofuse=True)
                for q in range(HALF // P):
                    mm = nc.tensor.transpose(ps_x[:, q * P:(q + 1) * P], osb[:, c, q * P:(q + 1) * P], ident[:])
                mm.then_inc(turned, 1)

            def scores_t(i, u, s):
                g = i * RING + u
                c, j = STEPS[s]
                if s == 0:
                    pe.wait_ge(rows_set, 32 * g + 32)
                    pe.nop(nofuse=True)
                start = min(max(0, P * j - HALF * c), HALF - FP32R_LEAST)
                for pr in range(2):
                    pe.wait_ge(exped, UNITS_T * g + 2 * s + pr + 1)
                    pe.nop(nofuse=True)
                    for h in range(2):
                        m = 2 * pr + h
                        mm = nc.tensor.matmul(ps_t[:, pr, h, start:HALF], kst[:, u, m % lay.kmaps, j * P:(j + 1) * P],
                                              qst[:, u, m, c * HALF + start:(c + 1) * HALF],
                                              start=True, stop=s not in DIAGONAL)
                        if s in DIAGONAL:
                            lo = P * j - HALF * c
                            mm = nc.tensor.matmul(ps_t[:, pr, h, lo:lo + P], ident_b[:], future[:],
                                                  start=False, stop=True)
                    mm.then_inc(scored_t, 1)

            def pv(i, u, s, first=False):
                g = i * RING + u
                c, j = STEPS[s]
                lo = max(0, P * j - HALF * c)
                pe.wait_ge(exped, UNITS_T * g + 2 * s + 4)
                pe.nop(nofuse=True)
                if s == 0:
                    pe.wait_ge(v_ready, g + 1)
                    pe.nop(nofuse=True)
                if j == 0 and not first:
                    pe.wait_ge(out_read, 2 * g + c)
                    pe.nop(nofuse=True)
                for m in range(MAPS):
                    mm = nc.tensor.matmul(ps_o[32 * m:32 * m + 32, lo:HALF], vst[:, u % 2, m % lay.kmaps, j, :],
                                          probs[:, s % PROBS, m, lo:HALF],
                                          start=(j == 0), stop=(P * (j + 1) == HALF * (c + 1)))
                mm.then_inc(summed, 1)

            def body(i, u, ahead):
                g = i * RING + u
                before = (i, u, LAG - 1)
                for k, step in enumerate(steps_of(i, u, ahead)):
                    scores_t(*step)
                    pv(*before)
                    before = step
                    if ahead:
                        pieces(i, u, 1, range(rest[k], rest[k + 1]))
                    if ahead > 1:
                        pieces(i, u, 2, range(early[k], early[k + 1]))
                    if k == OUT0_AT:
                        turn_out(g, 0, TURNS * g + 1)
                    if k == ROWS_AT and ahead:
                        turn_rows(g + 1, TURNS * g + 2)
                if not ahead:
                    pv(*before)
                turn_out(g, 1, TURNS * g + (3 if ahead else 2))

            pe.wait_ge(ones_set, 2)
            pe.wait_ge(future_ready, 2)
            pieces(0, 0, 0, range(PIECES_G))
            turn_rows(0, None)
            pieces(0, 0, 1, range(EARLY))
            scores_t(0, 0, 0)
            scores_t(0, 0, 1)
            pv(0, 0, 0, first=True)
            iterate(pe, body)

        @block.scalar
        def _(act):
            act.sem_inc(exped, 2)

            def exp(i, u, s):
                g = i * RING + u
                c, j = STEPS[s]
                lo = max(0, P * j - HALF * c)
                act.wait_ge(summed, NS * g + s + 1)
                act.nop(nofuse=True)
                for pr in range(2):
                    act.wait_ge(scored_t, UNITS_T * g + 2 * s + pr + 1)
                    act.nop(nofuse=True)
                    nc.scalar.activation(probs[:, s % PROBS, 2 * pr:2 * pr + 2, lo:HALF], ps_t[:, pr, :, lo:HALF],
                                         ACT.Exp, scale=lay.scale).then_inc(exped, 1)

            def read_out(g, c):
                last_step = max(s for s in range(NS) if STEPS[s][0] == c)
                act.wait_ge(summed, NS * g + last_step + 1 + PROBS)
                act.nop(nofuse=True)
                nc.scalar.copy(osb[:, c], ps_o[:]).then_inc(out_read, 1)

            def body(i, u, ahead):
                g = i * RING + u
                for k, step in enumerate(steps_of(i, u, ahead)):
                    exp(*step)
                    if k == OUT0_AT - 1:
                        read_out(g, 0)
                    if k == NS - LAG:
                        read_out(g, 1)
                if not ahead:
                    read_out(g, 1)

            exp(0, 0, 0)
            exp(0, 0, 1)
            iterate(act, body)

        @block.vector
        def _(dve):
            for n in range(RING):
                zeros = nc.vector.memset(f32(kst[lay.max_row:P, n]), 0.0)
                nc.vector.memset(f32(qst[lay.max_row:P, n]), 0.0).then_inc(pad_set, 1)
            zeros.then_inc(ones_set, 1)
            dve.wait_ge(ones_set, 1)
            for n in range(RING):
                ones = nc.vector.memset(f32(kst[lay.max_row:lay.max_row + 2, n]), 1.0)
            ones.then_inc(ones_set, 1)
            nc.vector.memset(vst[:], 0.0).then_inc(v_zeroed, 1)
            dve.sem_inc(stored[0], 16)
            dve.sem_inc(stored[1], 16)
            dve.sem_inc(topped, 2)
            dve.wait_ge(mask_ready, 1)

            def maxima(i, u, n, ns):
                g, slot, _ = after(i, u, n)
                par = (u + n) % 2
                for n in ns:
                    m, (r, k0, keys) = n // NP, PIECES[n % NP]
                    dve.wait_ge(scored, g * PIECES_G + n + 1)
                    dve.nop(nofuse=True)
                    diagonal = k0 + keys == P * (r + 1)
                    zeros = mask[:, HALF + P - keys:HALF + P] if diagonal else mask[:, 0:keys]
                    top = tops[:, par, m, r:r + 1] if r < QB // 2 else pair[:, par, m, r - QB // 2, k0 // HALF:k0 // HALF + 1]
                    nc.vector.tensor_tensor_reduce(out=ps_s[:, n % 2, 0:keys], in0=ps_s[:, n % 2, 0:keys], in1=zeros,
                                                   scale=1.0, scalar=-3e38, op0=ALU.add, op1=ALU.max,
                                                   accum_out=top).then_inc(topped, 1)

            def split_tops(g, par):
                dve.wait_ge(topped, g * PIECES_G + PIECES_G + 2)
                dve.nop(nofuse=True)
                nc.vector.tensor_tensor(tops[:, par, :, QB // 2:QB], pair[:, par, :, :, 0], pair[:, par, :, :, 1],
                                        ALU.max).then_inc(top_step, 1)
                dve.wait_ge(top_step, 3 * g + 1)
                dve.nop(nofuse=True)
                nc.vector.tensor_scalar(ntop_r[:], tops[:, par], -1.0, None, ALU.mult).then_inc(top_step, 1)
                dve.wait_ge(top_step, 3 * g + 2)
                dve.nop(nofuse=True)
                nc.vector.tensor_copy(ntop[:, 0], f32(ntop_r[:])).then_inc(top_step, 1)
                dve.wait_ge(top_step, 3 * g + 3)
                dve.nop(nofuse=True)
                nc.vector.scalar_tensor_tensor(ntop[:, 1], tops[:, par], -1.0, f32(ntop_r[:]), ALU.mult,
                                               ALU.subtract).then_inc(tops_split, 1)

            def read_rows(g, turn, first=False):
                dve.wait_ge(turned, turn + 1)
                dve.nop(nofuse=True)
                if not first:
                    dve.wait_ge(rows_set, 32 * g)
                    dve.nop(nofuse=True)
                nc.vector.tensor_copy(mrow[0:64], ps_x[0:64, 0:P]).then_inc(rows_read, 1)
                dve.wait_ge(rows_read, g + 1)
                dve.sem_inc(turn_read, 1)

            def divide(i, u, c, turn):
                g = i * RING + u
                n = 2 * g + c
                dve.wait_ge(turned, turn + 1)
                dve.nop(nofuse=True)
                x = ps_x[:].rearrange("p (q e) -> p q e", e=32)
                nc.vector.reciprocal(rec[:, c], x[:, :, D0]).then_inc(rec_done, 1)
                dve.wait_ge(rec_done, n + 1)
                dve.nop(nofuse=True)
                over = rec[:, c].rearrange("p (q o) -> p q o", o=1).broadcast_to([P, HALF // 32, D0])

                def cols(t):
                    return t.rearrange("p b (m d) -> p (b m) d", d=D0)

                if not differential or u % 2:
                    dve.wait_ge(stored[c], 16 * ((i * RING + u if not differential else i * (RING // 2) + u // 2) + 1))
                    dve.nop(nofuse=True)
                if not differential:
                    nc.vector.tensor_tensor(cols(result[:, c]), x[:, :, 0:D0], over, ALU.mult).then_inc(turn_read, 1)
                    dve.wait_ge(turn_read, turn + 1)
                    dve.sem_inc(divided, 1)
                elif u % 2 == 0:
                    nc.vector.tensor_tensor(cols(kept[:, c]), x[:, :, 0:D0], over, ALU.mult).then_inc(turn_read, 1)
                else:
                    nc.vector.tensor_tensor(cols(prod[:]), x[:, :, 0:D0], over, ALU.mult).then_inc(turn_read, 1)
                    dve.wait_ge(turn_read, turn + 1)
                    dve.nop(nofuse=True)
                    pairs = i * (RING // 2) + u // 2
                    nc.vector.scalar_tensor_tensor(result[:, c], prod[:], neg_lambda[:], kept[:, c], ALU.mult,
                                                   ALU.add).then_inc(divided, 1)
                    dve.wait_ge(divided, 2 * (pairs) + c + 1)
                    dve.nop(nofuse=True)

            def body(i, u, ahead):
                g = i * RING + u
                g1, slot1, _ = after(i, u, 1)
                for k in range(SLOTS if ahead else SLOTS - LAG):
                    if ahead:
                        maxima(i, u, 1, range(rest[k], rest[k + 1]))
                        if rest[k + 1] == PIECES_G and rest[k] < PIECES_G:
                            split_tops(g1, (u + 1) % 2)
                    if ahead > 1:
                        maxima(i, u, 2, range(early[k], early[k + 1]))
                    if k == OUT0_AT + 1:
                        divide(i, u, 0, TURNS * g + 1)
                    if k == ROWS_AT and ahead:
                        read_rows(g1, TURNS * g + 2)
                divide(i, u, 1, TURNS * g + (3 if ahead else 2))

            maxima(0, 0, 0, range(PIECES_G))
            split_tops(0, 0)
            read_rows(0, 0, first=True)
            maxima(0, 0, 1, range(EARLY))
            iterate(dve, body)
            dve.wait_ge(turn_read, TURNS * groups)

        @block.gpsimd
        def _(pool):
            nc.gpsimd.memset(mask[:], 0.0).then_inc(mask_zero, 1)
            nc.gpsimd.memset(future[:], 0.0).then_inc(mask_zero, 1)
            nc.gpsimd.tensor_copy(ident_b[:], ident[:]).then_inc(future_ready, 1)
            pool.wait_ge(mask_zero, 2)
            nc.gpsimd.affine_select(out=future[:], in_=future[:], compare_op=ALU.is_ge, fill=NEG,
                                    base=0, pattern=[[1, P]], channel_multiplier=-1).then_inc(future_ready, 1)
            nc.gpsimd.affine_select(out=mask[:, HALF:], in_=mask[:, HALF:], compare_op=ALU.is_ge, fill=NEG,
                                    base=0, pattern=[[-1, P]], channel_multiplier=1).then_inc(mask_ready, 1)
            pool.wait_ge(v_zeroed, 1)

            def copy_values(i, u, n):
                g, slot, rnd = after(i, u, n)
                blocks = lay.kmaps * QB
                at = g * blocks if not differential else (i * (RING // 2) + (u + n) // 2) * QB
                pool.nop(nofuse=True)
                nc.gpsimd.tensor_copy(vst[:, (u + n) % 2, :, :, 0:VW].rearrange("p m k e -> p (m k) e"),
                                      v[:, bass.ds(at, blocks), :]).then_inc(v_ready, 1)

            def body(i, u, ahead):
                g = i * RING + u
                if ahead:
                    pool.wait_ge(summed, NS * g + PROBS)
                    copy_values(i, u, 1)

            copy_values(0, 0, 0)
            iterate(pool, body)


RR = 4 * RK


def modulate_block(nc, ins, scr, ht, mod, bst, ident):
    with ExitStack() as ctx:
        def sb(name, shape, dt=F32):
            return ctx.enter_context(nc.sbuf_tensor(name, shape, dt))

        def sem(name):
            return ctx.enter_context(nc.semaphore(name))

        def psum(name, shape):
            return ctx.enter_context(nc.psum_tensor(name, shape, F32))

        groups = B * NH1 // MAPS
        heads_a = sb("heads_rows", [P, groups * QB, MAPS * RK])
        a_raw = sb("a_raw", [P, KT, RK])
        a_wide = sb("a_wide", [P, 2, KT, P], F32R)
        b_raw = sb("b_raw", [RK, F])
        b_hi = sb("b_hi", [RK, F], F32R)
        part_sum = sb("part_sum", [P, groups * QB, RK])
        asum = sb("asum", [P, TOK // P, 4, RK])
        m32 = sb("mod32", [RR, TOK])
        ps_t = psum("ps_turn", [P, 4, CH])
        ps_h = psum("ps_ha", [P, 2, CH])

        loaded = sem("mod_loaded")
        heads_loaded = sem("heads_loaded")
        h_loaded = sem("mod_h_loaded")
        a_zeroed = sem("a_zeroed")
        mod_zeroed = sem("mod_zeroed")
        a_hi = sem("a_hi")
        a_ready = sem("a_ready")
        bh_ready = sem("bh_ready")
        bl_ready = sem("bl_ready")
        b_placed = sem("b_placed")
        heads_sum = sem("heads_sum")
        sum_ready = sem("sum_ready")
        sum_turned = sem("sum_turned")
        tanh_ready = sem("tanh_ready")
        ha_ready = sem("ha_ready")
        ha_read = sem("ha_read")
        mod_hi = sem("mod_hi")
        mod_lo = sem("mod_lo_ready")
        mod_ready = sem("mod_ready")
        block = ctx.enter_context(nc.Block())

        @block.sync
        def _(sp):
            sp.dma_start(heads_a[:], scr["heads"]).then_inc(heads_loaded, 16)
            sp.dma_start(a_raw[:], ins["a"].rearrange("(k p) n -> p k n", p=P)).then_inc(loaded, 16)
            sp.dma_start(b_raw[:], ins["b"]).then_inc(loaded, 16)
            for n in range(2):
                sp.dma_start(f32(ht[:, n]), scr["h"][:, n]).then_inc(h_loaded, 16)
            sp.wait_ge(mod_zeroed, 2)
            sp.wait_ge(bh_ready, 1)
            sp.wait_ge(bl_ready, 1)
            for n in range(4):
                sp.dma_start(f32(bst[n * RK:(n + 1) * RK]), (f32(b_hi[:]), b_raw[:])[n % 2]).then_inc(b_placed, 16)
            sp.wait_ge(b_placed, 64)

        @block.gpsimd
        def _(pool):
            nc.gpsimd.memset(f32(a_wide[:]), 0.0).then_inc(a_zeroed, 1)
            nc.gpsimd.memset(f32(bst[:]), 0.0).then_inc(mod_zeroed, 1)
            nc.gpsimd.memset(f32(mod[:]), 0.0).then_inc(mod_zeroed, 1)
            pool.wait_ge(mod_zeroed, 2)

        @block.tensor
        def _(pe):
            pe.wait_ge(sum_ready, 4)
            for t in range(TOK // P):
                mm = nc.tensor.transpose(ps_t[0:RR, t // TT, t % TT * P:(t % TT + 1) * P],
                                         asum[:, t].rearrange("p n r -> p (n r)"), ident[:])
            mm.then_inc(sum_turned, 1)
            pe.wait_ge(a_ready, 4)
            pe.wait_ge(h_loaded, 32)
            for c in range(NCH):
                if c >= 2:
                    pe.wait_ge(ha_read, c - 1)
                for k in range(KT):
                    for n, (a, x) in enumerate(PASSES):
                        mm = nc.tensor.matmul(ps_h[:, c % 2], a_wide[:, a, k, :], ht[:, x, k, c * CH:(c + 1) * CH],
                                              start=(k == 0 and n == 0), stop=(k == KT - 1 and n == 2))
                mm.then_inc(ha_ready, 1)

        @block.scalar
        def _(act):
            act.wait_ge(loaded, 32)
            act.wait_ge(a_zeroed, 1)
            for n in range(4):
                nc.scalar.copy(a_wide[:, HI, :, n * RK:(n + 1) * RK], a_raw[:]).then_inc(a_hi, 1)
            nc.scalar.copy(b_hi[:], b_raw[:]).then_inc(bh_ready, 1)
            act.wait_ge(sum_turned, 1)
            nc.scalar.activation(m32[:], ps_t[0:RR].rearrange("p c n -> p (c n)"), ACT.Tanh).then_inc(tanh_ready, 1)

        @block.vector
        def _(dve):
            for n in range(4):
                dve.wait_ge(a_hi, n + 1)
                cols = slice(n * RK, (n + 1) * RK)
                nc.vector.tensor_tensor(a_wide[:, LO, :, cols], a_raw[:], f32(a_wide[:, HI, :, cols]),
                                        ALU.subtract).then_inc(a_ready, 1)
            dve.wait_ge(heads_loaded, 16)
            nc.vector.tensor_reduce(part_sum[:], heads_a[:].rearrange("p n (m r) -> p n r m", m=MAPS),
                                    AX.X, ALU.add).then_inc(heads_sum, 1)
            dve.wait_ge(heads_sum, 1)
            for n in range(4):
                for b in range(B):
                    src = part_sum[:, b * groups // B * QB:(b + 1) * groups // B * QB, :]
                    red = nc.vector.tensor_reduce(asum[:, b * QB:(b + 1) * QB, n, :],
                                                  src.rearrange("p (g q) r -> p q r g", q=QB), AX.X, ALU.add)
                red.then_inc(sum_ready, 1)
            dve.wait_ge(bh_ready, 1)
            nc.vector.tensor_tensor(b_raw[:], b_raw[:], f32(b_hi[:]), ALU.subtract).then_inc(bl_ready, 1)
            dve.wait_ge(tanh_ready, 1)
            dve.wait_ge(mod_zeroed, 2)
            for c in range(NCH):
                dve.wait_ge(ha_ready, c + 1)
                cols = slice(c * CH, (c + 1) * CH)
                nc.vector.scalar_tensor_tensor(m32[:, cols], m32[:, cols], MOD_SCALE, ps_h[0:RR, c % 2], ALU.mult,
                                               ALU.mult).then_inc(ha_read, 1)
                dve.wait_ge(ha_read, c + 1)
                nc.vector.tensor_copy(mod[0:RR, cols], m32[:, cols]).then_inc(mod_hi, 1)
            dve.wait_ge(mod_hi, NCH)
            low = slice(RR // 2, RR)
            nc.vector.tensor_tensor(m32[low], m32[low], f32(mod[low]), ALU.subtract).then_inc(mod_lo, 1)
            dve.wait_ge(mod_lo, 1)
            nc.vector.tensor_copy(mod[low], m32[low]).then_inc(mod_ready, 1)
            dve.wait_ge(mod_ready, 1)


def output_block(nc, ins, scr, acc, ident):
    with ExitStack() as ctx:
        def sb(name, shape, dt=F32):
            return ctx.enter_context(nc.sbuf_tensor(name, shape, dt))

        def sem(name):
            return ctx.enter_context(nc.semaphore(name))

        def psum(name, shape):
            return ctx.enter_context(nc.psum_tensor(name, shape, F32))

        attn = sb("attn", [P, B, QB, NKV, MAPS * D0])
        wo_raw = sb("wo0_raw", [P, KT, H])
        wo = sb("wo0", [P, 2, KT, H], F32R)
        at = sb("attn_t", [P, 2, CH])
        apart = sb("attn_parts", [P, 2, 2, KT, CH], F32R)
        ps_t = psum("ps_turn0", [P, KT, CH])
        ps_y = psum("ps_y", [P, 4, CH])

        wo_loaded = sem("wo_loaded")
        attn_loaded = sem("attn_loaded")
        acc_loaded = sem("acc_loaded")
        wo_hi = sem("wo_hi")
        wo_ready = sem("wo_ready")
        at_turned = sem("at_turned")
        at_read = sem("at_read")
        at_hi = sem("at_hi")
        at_split = sem("at_split")
        y_ready = sem("y0_ready")
        y_added = sem("y0_added")
        block = ctx.enter_context(nc.Block())

        @block.sync
        def _(sp):
            for b in range(B):
                src = scr["attn"][:, b * NKV * QB:(b + 1) * NKV * QB, :].rearrange("p (k q) e -> p k q e", q=QB)
                for k in range(NKV):
                    sp.dma_start(attn[:, b, :, k, :], src[:, k]).then_inc(attn_loaded, 16)
            sp.dma_start(wo_raw[:], ins["wo0t"].rearrange("(k p) n -> p k n", p=P)).then_inc(wo_loaded, 16)
            sp.dma_start(acc[:], scr["resid"].rearrange("(t p) n -> p t n", p=P)).then_inc(acc_loaded, 16)
            sp.wait_ge(acc_loaded, 16)

        @block.tensor
        def _(pe):
            def turn(c):
                for k in range(KT):
                    if c:
                        pe.wait_ge(at_read, (c - 1) * KT + k + 1)
                    for t in range(TT):
                        b, qb = divmod(c * TT + t, QB)
                        src = attn[:, b, qb, 2 * k:2 * k + 2].rearrange("p k e -> p (k e)")
                        mm = nc.tensor.transpose(ps_t[:, k, t * P:(t + 1) * P], src, ident[:])
                    mm.then_inc(at_turned, 1)

            pe.wait_ge(attn_loaded, 16 * B * NKV)
            turn(0)
            pe.wait_ge(wo_ready, 1)
            for c in range(NCH):
                if c + 1 < NCH:
                    turn(c + 1)
                pe.wait_ge(at_split, (c + 1) * KT)
                for t in range(TT):
                    n = c * TT + t
                    if n >= 4:
                        pe.wait_ge(y_added, n - 3)
                    for k in range(KT):
                        for q, (a, x) in enumerate(PASSES):
                            mm = nc.tensor.matmul(ps_y[:, n % 4], apart[:, c % 2, a, k, t * P:(t + 1) * P], wo[:, x, k, :],
                                                  start=(k == 0 and q == 0), stop=(k == KT - 1 and q == 2))
                    mm.then_inc(y_ready, 1)

        @block.scalar
        def _(act):
            act.wait_ge(wo_loaded, 16)
            nc.scalar.copy(wo[:, HI], wo_raw[:]).then_inc(wo_hi, 1)
            for n in range(NCH * KT):
                act.wait_ge(at_turned, n + 1)
                if n >= 2:
                    act.wait_ge(at_split, n - 1)
                nc.scalar.copy(at[:, n % 2], ps_t[:, n % KT]).then_inc(at_read, 1)

        @block.vector
        def _(dve):
            dve.wait_ge(wo_hi, 1)
            nc.vector.tensor_tensor(wo[:, LO], wo_raw[:], f32(wo[:, HI]), ALU.subtract).then_inc(wo_ready, 1)

            def split(c):
                for k in range(KT):
                    n = c * KT + k
                    dve.wait_ge(at_read, n + 1)
                    if c >= 2 and k == 0:
                        dve.wait_ge(y_ready, (c - 1) * TT)
                    nc.vector.tensor_copy(apart[:, c % 2, HI, k], at[:, n % 2]).then_inc(at_hi, 1)
                    dve.wait_ge(at_hi, n + 1)
                    nc.vector.tensor_tensor(apart[:, c % 2, LO, k], at[:, n % 2], f32(apart[:, c % 2, HI, k]),
                                            ALU.subtract).then_inc(at_split, 1)

            split(0)
            dve.wait_ge(acc_loaded, 16)
            for c in range(NCH):
                if c + 1 < NCH:
                    split(c + 1)
                for t in range(TT):
                    n = c * TT + t
                    dve.wait_ge(y_ready, n + 1)
                    nc.vector.scalar_tensor_tensor(acc[:, n], ps_y[:, n % 4], 1.0 - LAMBDA_INIT, acc[:, n], ALU.mult,
                                                   ALU.add).then_inc(y_added, 1)
            dve.wait_ge(y_added, NCH * TT)


FG = 256
NFG = F // FG
FT = FG // P


def mlp_block(nc, ins, out, ht, acc, mod, bst):
    with ExitStack() as ctx:
        def sb(name, shape, dt=F32):
            return ctx.enter_context(nc.sbuf_tensor(name, shape, dt))

        def sem(name):
            return ctx.enter_context(nc.semaphore(name))

        def psum(name, shape):
            return ctx.enter_context(nc.psum_tensor(name, shape, F32))

        raw_in = sb("raw_in", [P, 2, KT, FG])
        raw_down = sb("raw_down", [P, FT, H])
        win = sb("win", [P, 2, 2, 2, KT, FG], F32R)
        wdown = sb("wdown", [P, 2, 2, FT, H], F32R)
        bgrp = sb("b_group", [P, 2, FG], F32R)
        th = sb("gate_tanh", [P, 2, CH])
        gate = sb("gate", [P, 2, CH])
        gu = sb("gate_up", [P, 2, CH])
        gp = sb("gate_up_parts", [P, 2, 2, FT, CH], F32R)
        ps_g = psum("ps_gate_up", [P, FT, 2, CH])
        ps_y = psum("ps_down", [P, TT, CH])

        raw_loaded = sem("mlp_raw_loaded")
        raw_hi = sem("mlp_raw_hi")
        raw_split = sem("mlp_raw_split")
        b_copied = sem("b_copied")
        gate_ready = sem("gate_ready")
        gate_tanh = sem("gate_tanh_ready")
        gate_step = sem("gate_step")
        gate_done = sem("gate_done")
        gp_hi = sem("gp_hi")
        gp_ready = sem("gp_ready")
        down_ready = sem("down_ready")
        down_added = sem("down_added")
        stored = sem("stored")
        block = ctx.enter_context(nc.Block())
        in_src = [ins["win_t"], ins["wup_t"]]

        def groups(eng, body):
            with eng.Fori(0, NFG // 2 - 1) as i:
                for slot in range(2):
                    body(i, slot, True)
            for slot in range(2):
                body(NFG // 2 - 1, slot, slot == 0)

        @block.sync
        def _(sp):
            def load(g):
                cols = bass.ds(g * FG, FG)
                for n in range(2):
                    sp.dma_start(raw_in[:, n], in_src[n].rearrange("(k p) f -> p k f", p=P)[:, :, cols]).then_inc(raw_loaded, 16)
                sp.dma_start(raw_down[:], ins["wdown_t"][cols].rearrange("(t p) n -> p t n", p=P)).then_inc(raw_loaded, 16)

            load(0)

            def body(i, slot, more):
                if more:
                    sp.wait_ge(raw_split, 2 * (2 * i + slot) + 2)
                    sp.nop(nofuse=True)
                    load(2 * i + slot + 1)

            groups(sp, body)
            for c in range(NCH):
                sp.wait_ge(down_added, (NFG - 1) * NCH * TT + (c + 2) * TT)
                sp.dma_start(out[c * CH:(c + 1) * CH].rearrange("(t p) n -> p t n", p=P),
                             acc[:, c * TT:(c + 1) * TT]).then_inc(stored, 16)
            sp.wait_ge(stored, 16 * NCH)

        @block.tensor
        def _(pe):
            def gates(i, slot, c):
                g = 2 * i + slot
                if c == 0:
                    pe.wait_ge(raw_split, 2 * g + 2)
                    pe.nop(nofuse=True)
                    pe.wait_ge(b_copied, g + 1)
                    pe.nop(nofuse=True)
                cols = slice(c * CH, (c + 1) * CH)
                for f in range(FT):
                    pe.wait_ge(gate_done, (g * NCH + c) * FT + f + 1)
                    pe.nop(nofuse=True)
                    at = slice(f * P, (f + 1) * P)
                    for w in range(2):
                        for k in range(KT):
                            for n, (a, x) in enumerate(PASSES):
                                last = k == KT - 1 and n == 2
                                mm = nc.tensor.matmul(ps_g[:, f, w], win[:, slot, a, w, k, at], ht[:, x, k, cols],
                                                      start=(k == 0 and n == 0), stop=last and w == 1)
                        if w == 0:
                            nc.tensor.matmul(ps_g[:, f, w], bgrp[:, slot, at], mod[:, cols], start=False, stop=True)
                    mm.then_inc(gate_ready, 1)

            def downs(i, slot, c):
                g = 2 * i + slot
                pe.wait_ge(gp_ready, (g * NCH + c + 1) * FT + 2)
                pe.nop(nofuse=True)
                for t in range(TT):
                    pe.wait_ge(down_added, (g * NCH + c) * TT + t + 1 - 0)
                    pe.nop(nofuse=True)
                    for f in range(FT):
                        for n, (a, x) in enumerate(PASSES):
                            mm = nc.tensor.matmul(ps_y[:, t], gp[:, c % 2, a, f, t * P:(t + 1) * P], wdown[:, slot, x, f, :],
                                                  start=(f == 0 and n == 0), stop=(f == FT - 1 and n == 2))
                    mm.then_inc(down_ready, 1)

            def body(i, slot, more):
                for c in range(NCH):
                    if c < NCH - 1:
                        gates(i, slot, c + 1)
                    elif more:
                        gates(i + slot, 1 - slot, 0)
                    downs(i, slot, c)

            gates(0, 0, 0)
            groups(pe, body)

        @block.scalar
        def _(act):
            def split_hi(i, slot, lead=False):
                g = 2 * i + slot
                act.wait_ge(raw_loaded, 48 * g + 48)
                act.nop(nofuse=True)
                if not lead:
                    act.wait_ge(down_added, (g - 1) * (NCH * TT) + TT)
                act.nop(nofuse=True)
                nc.scalar.copy(win[:, slot, HI], raw_in[:]).then_inc(raw_hi, 1)
                nc.scalar.copy(wdown[:, slot, HI], raw_down[:]).then_inc(raw_hi, 1)
                nc.scalar.copy(bgrp[:, slot], f32(bst[:, bass.ds(g * FG, FG)])).then_inc(b_copied, 1)

            def tanh(i, slot, c, f):
                n = ((2 * i + slot) * NCH + c) * FT + f
                act.wait_ge(gate_ready, n + 1)
                act.nop(nofuse=True)
                act.wait_ge(gate_step, n + 1)
                act.nop(nofuse=True)
                nc.scalar.activation(th[:, f], ps_g[:, f, 0], ACT.Tanh, scale=0.5).then_inc(gate_tanh, 1)

            def body(i, slot, more):
                for c in range(NCH):
                    for f in range(FT):
                        tanh(i, slot, c, f)
                    if c == 1 and more:
                        split_hi(i + slot, 1 - slot)

            split_hi(0, 0, lead=True)
            groups(act, body)

        @block.vector
        def _(dve):
            dve.sem_inc(gate_done, FT)
            dve.sem_inc(gate_step, 2)
            dve.sem_inc(down_added, TT)

            def split_lo(i, slot):
                g = 2 * i + slot
                dve.wait_ge(raw_hi, 2 * g + 2)
                dve.nop(nofuse=True)
                nc.vector.tensor_tensor(win[:, slot, LO], raw_in[:], f32(win[:, slot, HI]), ALU.subtract).then_inc(raw_split, 1)
                nc.vector.tensor_tensor(wdown[:, slot, LO], raw_down[:], f32(wdown[:, slot, HI]),
                                        ALU.subtract).then_inc(raw_split, 1)

            def act_gate(i, slot, c, f):
                n = ((2 * i + slot) * NCH + c) * FT + f
                dve.wait_ge(gate_tanh, n + 1)
                dve.nop(nofuse=True)
                nc.vector.scalar_tensor_tensor(gate[:, f], th[:, f], 1.0, ps_g[:, f, 0], ALU.add, ALU.mult).then_inc(gate_step, 1)
                dve.wait_ge(gate_step, n + 3)
                dve.nop(nofuse=True)
                dve.wait_ge(gp_ready, n + 1)
                dve.nop(nofuse=True)
                nc.vector.scalar_tensor_tensor(gu[:, f], gate[:, f], 0.5, ps_g[:, f, 1], ALU.mult, ALU.mult).then_inc(gate_done, 1)
                dve.wait_ge(gate_done, n + 1 + FT)
                dve.nop(nofuse=True)
                nc.vector.tensor_copy(gp[:, c % 2, HI, f], gu[:, f]).then_inc(gp_hi, 1)

            def add(i, slot, c):
                for t in range(TT):
                    n = ((2 * i + slot) * NCH + c) * TT + t
                    dve.wait_ge(down_ready, n + 1)
                    dve.nop(nofuse=True)
                    nc.vector.tensor_tensor(acc[:, c * TT + t], acc[:, c * TT + t], ps_y[:, t], ALU.add).then_inc(down_added, 1)

            def body(i, slot, more):
                for c in range(NCH):
                    if c < NCH - 1:
                        for f in range(FT):
                            act_gate(i, slot, c + 1, f)
                    elif more:
                        for f in range(FT):
                            act_gate(i + slot, 1 - slot, 0, f)
                    add(i, slot, c)
                    if c == 1 and more:
                        split_lo(i + slot, 1 - slot)

            split_lo(0, 0)
            for f in range(FT):
                act_gate(0, 0, 0, f)
            groups(dve, body)

        @block.gpsimd
        def _(pool):
            pool.sem_inc(gp_ready, 2)

            def low(i, slot, c, f):
                n = ((2 * i + slot) * NCH + c) * FT + f
                pool.wait_ge(gp_hi, n + 1)
                pool.nop(nofuse=True)
                nc.gpsimd.tensor_tensor(gp[:, c % 2, LO, f], gu[:, f], f32(gp[:, c % 2, HI, f]), ALU.subtract).then_inc(gp_ready, 1)

            def body(i, slot, more):
                for c in range(NCH):
                    for f in range(FT):
                        low(i, slot, c, f)

            groups(pool, body)


def lambda_block(nc, ins, neg_lambda, zeros_dram):
    with ExitStack() as ctx:
        def sb(name, shape, dt=F32):
            return ctx.enter_context(nc.sbuf_tensor(name, shape, dt))

        def sem(name):
            return ctx.enter_context(nc.semaphore(name))

        vec = sb("lambda_vectors", [P, 4, D0])
        prod = sb("lambda_products", [P, 2, D0])
        dot = sb("lambda_dots", [P, 2])
        e = sb("lambda_exps", [P, 2])
        diff = sb("lambda_diff", [P, 1])
        zeros = sb("zero_rows", [2, MAPS, S])
        zeroed = sem("zero_rows_set")
        zeros_stored = sem("zeros_stored")
        loaded = sem("lambda_loaded")
        step = sem("lambda_step")
        exp_done = sem("lambda_exp")
        block = ctx.enter_context(nc.Block())

        @block.sync
        def _(sp):
            for n, name in enumerate(("lq1", "lk1", "lq2", "lk2")):
                src = ins[name].rearrange("(o d) -> o d", o=1).broadcast_to([P, D0])
                sp.dma_start(vec[:, n], src).then_inc(loaded, 16)
            sp.wait_ge(zeroed, 1)
            sp.dma_start(zeros_dram, zeros[:]).then_inc(zeros_stored, 16)
            sp.wait_ge(zeros_stored, 16)

        @block.gpsimd
        def _(pool):
            nc.gpsimd.memset(zeros[:], 0.0).then_inc(zeroed, 1)

        @block.vector
        def _(dve):
            dve.wait_ge(loaded, 64)
            v = vec[:].rearrange("p (l s) d -> p l s d", s=2)
            nc.vector.tensor_tensor(prod[:], v[:, :, 0, :], v[:, :, 1, :], ALU.mult).then_inc(step, 1)
            dve.wait_ge(step, 1)
            nc.vector.tensor_reduce(dot[:], prod[:], AX.X, ALU.add).then_inc(step, 1)
            dve.wait_ge(exp_done, 1)
            nc.vector.tensor_tensor(diff[:], e[:, 1:2], e[:, 0:1], ALU.subtract).then_inc(step, 1)
            dve.wait_ge(step, 3)
            nc.vector.tensor_scalar(neg_lambda[:], diff[:], -LAMBDA_INIT, None, ALU.add).then_inc(step, 1)
            dve.wait_ge(step, 4)

        @block.scalar
        def _(act):
            act.wait_ge(step, 2)
            nc.scalar.activation(e[:], dot[:], ACT.Exp).then_inc(exp_done, 1)


def program(nc, ins, out):
    with ExitStack() as ctx:
        def sb(name, shape, dt=F32):
            return ctx.enter_context(nc.sbuf_tensor(name, shape, dt))

        scr = {
            "q0": nc.dram_tensor("q0_parts", [B * NH0 * D0, 2, 2, S], F32).ap(),
            "k0": nc.dram_tensor("k0_parts", [B * NKV * D0, 2, 2, S], F32).ap(),
            "q1": nc.dram_tensor("q1_parts", [B * H, 2, S], F32).ap(),
            "k1": nc.dram_tensor("k1_parts", [B * H, 2, S], F32).ap(),
            "h": nc.dram_tensor("h_parts", [P, 2, KT, TOK], F32).ap(),
            "resid": nc.dram_tensor("resid", [TOK, H], F32).ap(),
        }
        ident = sb("ident", [P, P])
        neg_lambda = sb("neg_lambda", [P, 1])
        zeros_dram = nc.dram_tensor("zero_rows_scratch", [2, MAPS, S], F32).ap()
        lambda_block(nc, ins, neg_lambda, zeros_dram)
        diff = Layer("diff", D0, 2 * B * NKV, ((HI, HI), (HI, LO), (LO, HI), (LO, LO)), False, 1.0 / math.sqrt(D0))
        plain = Layer("ffn", D1, B * NH1 // MAPS, PASSES, True, float(np.float32(1.0) / np.sqrt(np.float32(D1))))
        with ExitStack() as values:
            v0 = values.enter_context(nc.sbuf_tensor("v0", [P, B * NKV * QB, VW], F32))
            v1 = values.enter_context(nc.sbuf_tensor("v1", [P, B * NH1 * QB, VW], F32))
            with ExitStack() as weights:
                w0 = weights.enter_context(nc.sbuf_tensor("w0", [P, 2, KT, N0], F32R))
                w1 = weights.enter_context(nc.sbuf_tensor("w1", [P, 2, KT, N1], F32R))
                wp = weights.enter_context(nc.sbuf_tensor("wp", [P, 2, KT, NH1 * RK], F32R))
                weights_block(nc, ins, w0, w1, wp, ident)
                project_block(nc, ins, scr, w0, w1, wp, v0, v1, ident)
            heads_dram = nc.dram_tensor("heads_a", [P, B * NH1 // MAPS * QB, MAPS * RK], F32).ap()
            attn_dram = nc.dram_tensor("attn_out", [P, B * NKV * QB, MAPS * D0], F32).ap()
            attention_block(nc, plain, scr["q1"], scr["k1"], zeros_dram, v1, heads_dram, None, ident)
            attention_block(nc, diff, scr["q0"], scr["k0"], zeros_dram, v0, attn_dram, neg_lambda, ident)
        scr["heads"], scr["attn"] = heads_dram, attn_dram
        acc = sb("acc", [P, TOK // P, H])
        output_block(nc, ins, scr, acc, ident)
        ht = sb("ht_all", [P, 2, KT, TOK], F32R)
        mod = sb("mod_stack", [P, TOK], F32R)
        bst = sb("b_stack", [P, F], F32R)
        modulate_block(nc, ins, scr, ht, mod, bst, ident)
        mlp_block(nc, ins, out, ht, acc, mod, bst)


def rope_tables():
    inv_freq = 1.0 / np.float32(10000.0) ** (np.arange(0, D0, 2, dtype=np.float32) / np.float32(D0))
    freqs = np.arange(S, dtype=np.float32)[None, :] * inv_freq.astype(np.float32)[:, None]
    angle = np.tile(freqs, (P // (D0 // 2), 1)).astype(np.float64)
    sign = np.where(np.arange(P) % D0 < D0 // 2, -1.0, 1.0)[:, None]
    return np.cos(angle).astype(np.float32), (np.sin(angle) * sign).astype(np.float32)


def kernel(**inputs):
    import concourse.bacc as bacc
    from concourse.bass_utils import run_bass_kernel_spmd

    def arr(name):
        return np.asarray(inputs[name])

    cos, sin = rope_tables()
    arrays = {
        "x": arr("L0_attn_hidden_states").reshape(TOK, H),
        "w0t": np.concatenate([arr("L0_attn_wq").T, arr("L0_attn_wk").T, arr("L0_attn_wv").T], axis=1),
        "wo0t": arr("L0_attn_wo").T,
        "lq1": arr("L0_attn_lambda_q1"), "lk1": arr("L0_attn_lambda_k1"),
        "lq2": arr("L0_attn_lambda_q2"), "lk2": arr("L0_attn_lambda_k2"),
        "ln1": arr("L0_ffn_ln1_w").reshape(KT, P).T, "ln2": arr("L0_ffn_ln2_w").reshape(KT, P).T,
        "w1t": np.concatenate([arr("L0_ffn_Wq").T, arr("L0_ffn_Wk").T], axis=1),
        "wv1": arr("L0_ffn_Wv"), "wo1": arr("L0_ffn_Wo"), "a": arr("L0_ffn_A"), "b": arr("L0_ffn_B"),
        "win_t": arr("L0_ffn_W_in_base").T, "wup_t": arr("L0_ffn_W_up_base").T, "wdown_t": arr("L0_ffn_W_down").T,
        "cos": cos, "sin": sin,
    }
    nc = bacc.Bacc("TRN2", target_bir_lowering=False, num_devices=1)
    maps, ins = {}, {}
    for name, a in arrays.items():
        a = np.ascontiguousarray(a)
        maps[f"in_{name}"] = a
        ins[name] = nc.dram_tensor(f"in_{name}", a.shape, mybir.dt.from_np(a.dtype), kind="ExternalInput").ap()
    out = nc.dram_tensor("out", (TOK, H), F32, kind="ExternalOutput").ap()
    program(nc, ins, out)
    res = run_bass_kernel_spmd(nc, [maps], core_ids=[0])
    return res.results[0]["out"].reshape(B, S, H)
```

```python
from contextlib import ExitStack
import math

import numpy as np

import concourse.bass as bass
from concourse import mybir
from concourse.alu_op_type import AluOpType as ALU

F32 = mybir.dt.float32
BF16 = mybir.dt.bfloat16
F32R = mybir.dt.float32r
ACT = mybir.ActivationFunctionType
AX = mybir.AxisListType

P = 128
B, S, H = 2, 1024, 512
TOK = B * S
CH = 512
NCH = TOK // CH
KT = H // P
TT = CH // P
QB = S // P

NH0, NKV, D0 = 32, 8, 16
REP = NH0 // NKV
NQ0 = 2 * NH0 * D0 // P
NK0 = 2 * NKV * D0 // P
N0 = (2 * NH0 + 2 * NKV + NKV) * D0
NH1, D1, RK = 16, 32, 16
N1 = 2 * NH1 * D1
F = 2048
VW = D0 + 1
LAMBDA_INIT = 0.8 - 0.6 * math.exp(-0.3 * 12)
LN_EPS, RMS_EPS, MOD_SCALE = 1e-5, 1e-6, 0.1
NEG = -1e30

HI, LO = 0, 1
PASSES = ((HI, HI), (HI, LO), (LO, HI))


def f32(ap):
    return ap.bitcast(F32)


def weights_block(nc, ins, w0, w1, wp, ident):
    with ExitStack() as ctx:
        def sb(name, shape, dt=F32):
            return ctx.enter_context(nc.sbuf_tensor(name, shape, dt))

        def sem(name):
            return ctx.enter_context(nc.semaphore(name))

        raw0 = sb("raw0", [P, KT, N0])
        raw1 = sb("raw1", [P, KT, N1])
        wv = sb("wv_rows", [P, KT, H])
        wo = sb("wo_rows", [P, KT, H])
        a = sb("a_rows", [P, KT, RK])
        woa = sb("woa_heads", [P, KT, P // D1, RK])
        ps_woa = ctx.enter_context(nc.psum_tensor("ps_woa", [P, KT, RK], F32))
        ps_wp = ctx.enter_context(nc.psum_tensor("ps_wp", [P, KT, NH1 * RK], F32))

        small_loaded = sem("small_loaded")
        raw_loaded = [sem(f"raw_loaded{n}") for n in range(2)]
        woa_zeroed = sem("woa_zeroed")
        ident_zeroed = sem("ident_zeroed")
        ident_ready = sem("ident_ready")
        woa_summed = sem("woa_summed")
        woa_ready = sem("woa_ready")
        wp_summed = sem("wp_summed")
        hi_ready = sem("hi_ready")
        lo_ready = sem("lo_ready")
        block = ctx.enter_context(nc.Block())

        @block.sync
        def _(sp):
            sp.dma_start(wo[:], ins["wo1"].rearrange("(k p) n -> p k n", p=P)).then_inc(small_loaded, 16)
            sp.dma_start(a[:], ins["a"].rearrange("(k p) n -> p k n", p=P)).then_inc(small_loaded, 16)
            sp.dma_start(wv[:], ins["wv1"].rearrange("(k p) n -> p k n", p=P)).then_inc(small_loaded, 16)
            sp.dma_start(raw0[:], ins["w0t"].rearrange("(k p) n -> p k n", p=P)).then_inc(raw_loaded[0], 16)
            sp.dma_start(raw1[:], ins["w1t"].rearrange("(k p) n -> p k n", p=P)).then_inc(raw_loaded[1], 16)

        @block.gpsimd
        def _(pool):
            nc.gpsimd.memset(woa[:], 0.0).then_inc(woa_zeroed, 1)
            nc.gpsimd.memset(ident[:], 0.0).then_inc(ident_zeroed, 1)
            pool.wait_ge(ident_zeroed, 1)
            nc.gpsimd.affine_select(out=ident[:], in_=ident[:], compare_op=ALU.not_equal, fill=1.0,
                                    base=0, pattern=[[-1, P]], channel_multiplier=1).then_inc(ident_ready, 1)
            pool.wait_ge(ident_ready, 1)

        @block.tensor
        def _(pe):
            pe.wait_ge(small_loaded, 48)
            for m in range(KT):
                for k in range(KT):
                    mm = nc.tensor.matmul(ps_woa[:, m, :], wo[:, k, m * P:(m + 1) * P], a[:, k, :],
                                          start=(k == 0), stop=(k == KT - 1))
            mm.then_inc(woa_summed, 1)
            pe.wait_ge(woa_ready, P // D1)
            for n in range(KT):
                for m in range(KT):
                    mm = nc.tensor.matmul(ps_wp[:, n, m * 64:(m + 1) * 64], wv[:, m, n * P:(n + 1) * P],
                                          woa[:, m, :, :], start=True, stop=True)
            mm.then_inc(wp_summed, 1)

        @block.vector
        def _(dve):
            dve.wait_ge(woa_zeroed, 1)
            dve.wait_ge(woa_summed, 1)
            for j in range(P // D1):
                rows = slice(j * D1, (j + 1) * D1)
                nc.vector.tensor_copy(woa[rows, :, j, :], ps_woa[rows]).then_inc(woa_ready, 1)
            dve.wait_ge(hi_ready, 1)
            nc.vector.tensor_tensor(wp[:, LO], ps_wp[:], f32(wp[:, HI]), ALU.subtract).then_inc(lo_ready, 1)
            for n, (raw, w) in enumerate(((raw0, w0), (raw1, w1))):
                dve.wait_ge(hi_ready, n + 2)
                nc.vector.tensor_tensor(w[:, LO], raw[:], f32(w[:, HI]), ALU.subtract).then_inc(lo_ready, 1)
            dve.wait_ge(lo_ready, 3)

        @block.scalar
        def _(act):
            act.wait_ge(wp_summed, 1)
            nc.scalar.copy(wp[:, HI], ps_wp[:]).then_inc(hi_ready, 1)
            for n, (raw, w) in enumerate(((raw0, w0), (raw1, w1))):
                act.wait_ge(raw_loaded[n], 16)
                nc.scalar.copy(w[:, HI], raw[:]).then_inc(hi_ready, 1)
            act.wait_ge(hi_ready, 3)


L0_TILES = NQ0 + NK0
L1_TILES = N1 // P
TILES = L0_TILES + L1_TILES
V_UNITS = 2
UNITS = TILES + 2 * V_UNITS
L0_FIRST, L0_V, L1_FIRST, L1_V = 0, L0_TILES, L0_TILES + V_UNITS, L0_TILES + V_UNITS + L1_TILES
XN_JOBS, XS_JOBS = KT, 2 * KT
JOBS = XN_JOBS + XS_JOBS
NORM_STEPS = 12


def project_block(nc, ins, scr, w0, w1, wp, v0, v1, ident):
    with ExitStack() as ctx:
        def sb(name, shape, dt=F32):
            return ctx.enter_context(nc.sbuf_tensor(name, shape, dt))

        def sem(name):
            return ctx.enter_context(nc.semaphore(name))

        def psum(name, shape):
            return ctx.enter_context(nc.psum_tensor(name, shape, F32))

        cos = sb("cos", [P, S])
        sin = sb("sin", [P, S])
        ln1 = sb("ln1", [P, KT])
        ln2 = sb("ln2", [P, KT])
        xin = sb("xin", [P, TT, H])
        xn = sb("xn", [P, TT, H])
        stats = sb("stats", [P, TT, 6])
        mv = sb("mean_var", [P, TT, 2])
        var = sb("var", [P, 2, TT])
        inv = sb("inv", [P, 2, TT])
        root = sb("root", [P, 2, TT])
        newt = sb("newton", [P, 2, TT])
        sq = sb("square_sum", [P, TT])
        junk = sb("square", [P, H])
        y = sb("turned", [P, 4, CH])
        xnt = sb("xnt", [P, 2, KT, CH], F32R)
        x1t = sb("x1t", [P, 2, KT, CH], F32R)
        ht = sb("ht", [P, 2, 2, CH], F32R)
        qs = sb("q_raw", [P, 2, CH])
        qc = sb("q_cos", [P, 3, CH])
        qr = sb("q_rot", [P, 2, CH])
        parts = sb("q_parts", [P, 2, 2, CH], F32R)
        pj = psum("pj", [P, 2, CH])
        tp = psum("tp", [P, KT, CH])

        consts_loaded = sem("consts_loaded")
        ones_ready = sem("ones_ready")
        x_loaded = sem("x_loaded")
        norm_step = sem("norm_step")
        inv_ready = sem("inv_ready")
        root_ready = sem("root_ready")
        xn_ready = sem("xn_ready")
        squared = sem("squared")
        resid_ready = sem("resid_ready")
        resid_stored = sem("resid_stored")
        xs_ready = sem("xs_ready")
        turned = sem("turned")
        y_ready = sem("y_ready")
        split_done = sem("split_done")
        h_stored = [sem(f"h_stored{n}") for n in range(2)]
        proj_done = sem("proj_done")
        proj_read = sem("proj_read")
        q_taken = sem("q_taken")
        cos_done = sem("cos_done")
        sin_done = sem("sin_done")
        rope_sum = sem("rope_sum")
        rope_hi = sem("rope_hi")
        rope_lo = sem("rope_lo")
        plain_hi = sem("plain_hi")
        plain_lo = sem("plain_lo")
        q_stored = [sem(f"q_stored{n}") for n in range(2)]
        block = ctx.enter_context(nc.Block())

        def first_job(ch, xs):
            return ch * JOBS + (XN_JOBS if xs else 0)

        XS_AFTER, XN_AFTER = L0_TILES - XS_JOBS, 3

        def xs_jobs(t):
            return range(t - XS_AFTER, t - XS_AFTER + 1)

        def operand_tile(xs, n):
            if not xs:
                return xnt[:, HI, n], xnt[:, LO, n]
            return ((x1t[:, HI, n // 2], x1t[:, LO, n // 2]) if n % 2 == 0
                    else (ht[:, n // 2 % 2, HI], ht[:, n // 2 % 2, LO]))

        @block.sync
        def _(sp):
            sp.dma_start(xin[:], ins["x"][0:CH].rearrange("(t p) n -> p t n", p=P)).then_inc(x_loaded, 16)
            sp.dma_start(cos[:], ins["cos"]).then_inc(consts_loaded, 16)
            sp.dma_start(sin[:], ins["sin"]).then_inc(consts_loaded, 16)
            sp.dma_start(ln1[:], ins["ln1"]).then_inc(consts_loaded, 16)
            sp.dma_start(ln2[:], ins["ln2"]).then_inc(consts_loaded, 16)

            def residual_store(ch):
                sp.wait_ge(resid_ready, TT * ch + TT)
                sp.dma_start(scr["resid"][bass.ds(ch * CH, CH)].rearrange("(t p) n -> p t n", p=P),
                             xin[:]).then_inc(resid_stored, 16)

            def parts_store(dst, ready, count, slot):
                sp.wait_ge(ready, count)
                sp.nop(nofuse=True)
                sp.dma_start(dst, f32(parts[:, slot])).then_inc(q_stored[slot], 16)

            def chunk(ch, last):
                b, col = ch // 2, (ch % 2) * CH
                for t in range(L0_TILES):
                    rope_store(ch, t, b, col)
                    if t == 1 and not last:
                        sp.wait_ge(resid_stored, 16 * ch + 16)
                        sp.nop(nofuse=True)
                        sp.dma_start(xin[:], ins["x"][bass.ds((ch + 1) * CH, CH)].rearrange(
                            "(t p) n -> p t n", p=P)).then_inc(x_loaded, 16)
                    if t >= XS_AFTER and xs_jobs(t)[-1] % 2:
                        h_store(ch, xs_jobs(t)[-1] // 2)
                for t in range(L1_TILES):
                    plain_store(ch, t, b, col)
                    if t == 4 and not last:
                        residual_store(ch + 1)

            def rope_store(ch, t, b, col):
                s, m = (t // (NQ0 // 2), t % (NQ0 // 2)) if t < NQ0 else (t - NQ0, 0)
                dst = scr["q0"] if t < NQ0 else scr["k0"]
                rows = (NH0 if t < NQ0 else NKV) * D0
                parts_store(dst[bass.ds(b * rows + m * P, P), s, :, bass.ds(col, CH)],
                            rope_lo, ch * L0_TILES + t + 3, t % 2)

            def plain_store(ch, t, b, col):
                dst = scr["q1"] if t < L1_TILES // 2 else scr["k1"]
                parts_store(dst[bass.ds(b * H + (t % (L1_TILES // 2)) * P, P), :, bass.ds(col, CH)],
                            plain_lo, ch * L1_TILES + t + 1, t % 2)

            def h_store(ch, k):
                sp.wait_ge(split_done, first_job(ch, True) + 2 * k + 2 + 4)
                sp.nop(nofuse=True)
                sp.dma_start(scr["h"][:, :, k, bass.ds(ch * CH, CH)], f32(ht[:, k % 2])).then_inc(h_stored[k % 2], 16)

            residual_store(0)
            with sp.Fori(0, NCH - 1) as ch:
                chunk(ch, False)
            chunk(NCH - 1, True)
            sp.wait_ge(resid_stored, 16 * NCH)
            for n in range(2):
                sp.wait_ge(q_stored[n], 16 * NCH * TILES // 2 + 16)
                sp.wait_ge(h_stored[n], 16 * NCH * KT // 2 + 16)

        @block.tensor
        def _(pe):
            def turn(ch, xs):
                for k in range(KT):
                    if xs:
                        if k == 0:
                            pe.wait_ge(xs_ready, TT * ch + TT)
                        pe.wait_ge(y_ready, first_job(ch, False) + k + 1)
                    else:
                        if k == 0:
                            pe.wait_ge(xn_ready, TT * ch + TT)
                        if not (isinstance(ch, int) and ch == 0):
                            pe.wait_ge(y_ready, first_job(ch, False) - XS_JOBS + 2 * k + 2)
                    pe.nop(nofuse=True)
                    for t in range(TT):
                        mm = nc.tensor.transpose(tp[:, k, t * P:(t + 1) * P], xn[:, t, k * P:(k + 1) * P], ident[:])
                    mm.then_inc(turned, 1)

            def features(ch, u, w, col, xt):
                pe.wait_ge(proj_read, ch * UNITS + u + 1)
                pe.nop(nofuse=True)
                for k in range(KT):
                    for n, (a, c) in enumerate(PASSES):
                        mm = nc.tensor.matmul(pj[:, u % 2, :], w[:, a, k, col:col + P], xt[:, c, k, :],
                                              start=(k == 0 and n == 0), stop=(k == KT - 1 and n == 2))
                mm.then_inc(proj_done, 1)

            def values(ch, u, w, col, xt):
                pe.wait_ge(proj_read, ch * UNITS + u + 1)
                pe.nop(nofuse=True)
                for h in range(2):
                    t = 2 * (u % 2) + h
                    for k in range(KT):
                        for n, (a, c) in enumerate(PASSES):
                            mm = nc.tensor.matmul(pj[:, u % 2, h * 256:h * 256 + 256], xt[:, a, k, t * P:(t + 1) * P],
                                                  w[:, c, k, col:col + 256],
                                                  start=(k == 0 and n == 0), stop=(k == KT - 1 and n == 2))
                mm.then_inc(proj_done, 1)

            def chunk(ch, last):
                pe.wait_ge(split_done, first_job(ch, False) + XN_JOBS + 4)
                for t in range(L0_TILES):
                    features(ch, L0_FIRST + t, w0, t * P, xnt)
                    if t == 1:
                        turn(ch, True)
                for n in range(V_UNITS):
                    values(ch, L0_V + n, w0, N0 - 256, xnt)
                pe.wait_ge(split_done, first_job(ch, True) + XS_JOBS + 4)
                for t in range(L1_TILES):
                    features(ch, L1_FIRST + t, w1, t * P, x1t)
                    if t == 1 and not last:
                        turn(ch + 1, False)
                for n in range(V_UNITS):
                    values(ch, L1_V + n, wp, 0, x1t)

            turn(0, False)
            with pe.Fori(0, NCH - 1) as ch:
                chunk(ch, False)
            chunk(NCH - 1, True)

        @block.scalar
        def _(act):
            act.sem_inc(proj_read, 2)
            act.wait_ge(consts_loaded, 64)

            def layer_root(ch):
                act.wait_ge(inv_ready, 2 * ch + 1)
                act.nop(nofuse=True)
                nc.scalar.activation(root[:, 0], inv[:, 0], ACT.Sqrt).then_inc(root_ready, 1)

            def squares(ch):
                for t in range(TT):
                    act.wait_ge(xn_ready, TT * ch + t + 1)
                    act.nop(nofuse=True)
                    if t > 0:
                        act.wait_ge(squared, TT * ch + t)
                        act.nop(nofuse=True)
                    nc.scalar.activation(junk[:], xn[:, t], ACT.Square, accum_out=sq[:, t:t + 1]).then_inc(squared, 1)

            def rms_root(ch):
                act.wait_ge(inv_ready, 2 * ch + 2)
                act.nop(nofuse=True)
                nc.scalar.activation(root[:, 1], inv[:, 1], ACT.Sqrt).then_inc(root_ready, 1)

            def read_turned(ch, xs, n):
                k, w = (n // 2, n % 2) if xs else (n, 0)
                job = first_job(ch, xs) + n
                if w == 0:
                    act.wait_ge(turned, ch * 2 * KT + (KT if xs else 0) + k + 1)
                    act.nop(nofuse=True)
                act.wait_ge(split_done, job + 1)
                act.nop(nofuse=True)
                if xs and n % 2:
                    act.wait_ge(h_stored[k % 2], 32 * ch + 16 * (k // 2) + 16)
                    act.nop(nofuse=True)
                if not xs and n == 0 and not (isinstance(ch, int) and ch == 0):
                    act.wait_ge(proj_done, ch * UNITS - UNITS + L1_FIRST)
                    act.nop(nofuse=True)
                for dst in (y[:, n % 4], operand_tile(xs, n)[0]):
                    if xs:
                        cp = nc.scalar.activation(dst, tp[:, k], ACT.Copy, scale=(ln1, ln2)[w][:, k:k + 1])
                    else:
                        cp = nc.scalar.copy(dst, tp[:, k])
                cp.then_inc(y_ready, 1)

            def read_tile(ch, u, q):
                act.wait_ge(proj_done, ch * UNITS + u + 1)
                act.nop(nofuse=True)
                act.wait_ge(q_taken, ch * TILES + q + 1)
                act.nop(nofuse=True)
                nc.scalar.copy(qs[:, q % 2], pj[:, u % 2]).then_inc(proj_read, 1)

            def read_values(ch, u, heads, off, dst):
                act.wait_ge(proj_done, ch * UNITS + u + 1)
                act.nop(nofuse=True)
                b, half = ch // 2, ch % 2
                for h in range(2):
                    tb = half * TT + 2 * (u % 2) + h
                    src = pj[:, u % 2, h * 256 + off:h * 256 + off + heads * D0].rearrange("p (h d) -> p h d", d=D0)
                    cp = nc.scalar.copy(dst(b, tb), src)
                cp.then_inc(proj_read, 1)

            def v0_at(b, tb):
                return v0[:, bass.ds(b * (NKV * QB) + tb, NKV, QB), 0:D0]

            def v1_at(b, tb):
                return v1[:, bass.ds(b * (NH1 * QB) + tb, NH1, QB), 0:D0]

            def chunk(ch, last):
                for t in range(L0_TILES):
                    read_tile(ch, L0_FIRST + t, t)
                    if t >= XS_AFTER:
                        for n in xs_jobs(t):
                            read_turned(ch, True, n)
                for n in range(V_UNITS):
                    read_values(ch, L0_V + n, NKV, P, v0_at)
                    if n == 0 and not last:
                        layer_root(ch + 1)
                for t in range(L1_TILES):
                    read_tile(ch, L1_FIRST + t, L0_TILES + t)
                    if not last:
                        if t == 0:
                            squares(ch + 1)
                        if t == 2:
                            rms_root(ch + 1)
                        if XN_AFTER <= t < XN_AFTER + XN_JOBS:
                            read_turned(ch + 1, False, t - XN_AFTER)
                for n in range(V_UNITS):
                    read_values(ch, L1_V + n, NH1, 0, v1_at)
                if not last:
                    rms_scale(ch + 1)

            def rms_scale(ch):
                act.wait_ge(turned, ch * 2 * KT + KT)
                act.nop(nofuse=True)
                act.wait_ge(resid_ready, TT * ch + TT)
                act.nop(nofuse=True)
                act.wait_ge(norm_step, NORM_STEPS * ch + NORM_STEPS)
                act.nop(nofuse=True)
                for t in range(TT):
                    nc.scalar.activation(xn[:, t], xn[:, t], ACT.Copy, scale=root[:, 1, t:t + 1]).then_inc(xs_ready, 1)

            layer_root(0)
            squares(0)
            rms_root(0)
            for n in range(XN_JOBS):
                read_turned(0, False, n)
            rms_scale(0)
            with act.Fori(0, NCH - 1) as ch:
                chunk(ch, False)
            chunk(NCH - 1, True)

        @block.vector
        def _(dve):
            nc.vector.memset(v0[:, :, D0:VW], 1.0).then_inc(ones_ready, 1)
            nc.vector.memset(v1[:, :, D0:VW], 1.0).then_inc(ones_ready, 1)
            dve.sem_inc(split_done, 4)
            dve.sem_inc(q_taken, 2)
            dve.sem_inc(rope_lo, 2)

            def step(ch, n, ins_):
                ins_.then_inc(norm_step, 1)
                dve.wait_ge(norm_step, NORM_STEPS * ch + n)
                dve.nop(nofuse=True)

            def inverse_root(ch, n, first):
                dve.wait_ge(root_ready, 2 * ch + n + 1)
                dve.nop(nofuse=True)
                step(ch, first, nc.vector.tensor_tensor(newt[:, n], root[:, n], root[:, n], ALU.mult))
                step(ch, first + 1, nc.vector.tensor_tensor(newt[:, n], newt[:, n], var[:, n], ALU.mult))
                step(ch, first + 2, nc.vector.tensor_scalar(newt[:, n], newt[:, n], -0.5, 1.5, ALU.mult, ALU.add))
                step(ch, first + 3, nc.vector.tensor_tensor(root[:, n], root[:, n], newt[:, n], ALU.mult))

            def layer_stats(ch):
                dve.wait_ge(x_loaded, 16 * ch + 16)
                dve.nop(nofuse=True)
                for t in range(TT):
                    bn = nc.vector.bn_stats(stats[:, t], xin[:, t])
                step(ch, 1, bn)
                for t in range(TT):
                    bn = nc.vector.bn_aggr(mv[:, t], stats[:, t])
                step(ch, 2, bn)
                step(ch, 3, nc.vector.tensor_scalar(var[:, 0], mv[:, :, 1], LN_EPS, None, ALU.add))
                nc.vector.reciprocal(inv[:, 0], var[:, 0]).then_inc(inv_ready, 1)

            def layer_norm(ch):
                inverse_root(ch, 0, 4)
                if not (isinstance(ch, int) and ch == 0):
                    dve.wait_ge(turned, ch * 2 * KT)
                    dve.nop(nofuse=True)
                for t in range(TT):
                    nc.vector.tensor_scalar(xn[:, t], xin[:, t], mv[:, t, 0:1], root[:, 0, t:t + 1],
                                            ALU.subtract, ALU.mult).then_inc(xn_ready, 1)

            def rms_stats(ch):
                dve.wait_ge(squared, TT * ch + TT)
                dve.nop(nofuse=True)
                step(ch, 8, nc.vector.tensor_scalar(var[:, 1], sq[:], 1.0 / H, RMS_EPS, ALU.mult, ALU.add))
                nc.vector.reciprocal(inv[:, 1], var[:, 1]).then_inc(inv_ready, 1)

            def rms_norm(ch):
                inverse_root(ch, 1, 9)

            def split_low(ch, xs, n):
                hi, lo = operand_tile(xs, n)
                dve.wait_ge(y_ready, first_job(ch, xs) + n + 1)
                dve.nop(nofuse=True)
                nc.vector.tensor_tensor(lo, y[:, n % 4], f32(hi), ALU.subtract).then_inc(split_done, 1)

            def rope_start(ch, t):
                s = t % 2
                dve.wait_ge(proj_read, ch * UNITS + t + 3)
                dve.nop(nofuse=True)
                dve.wait_ge(rope_lo, ch * L0_TILES + max(t - 2, 0) + 2)
                dve.nop(nofuse=True)
                nc.vector.tensor_tensor(qc[:, t % 3], qs[:, s], cos[:, bass.ds((ch % 2) * CH, CH)], ALU.mult).then_inc(cos_done, 1)
                nc.vector.stream_shuffle(qr[:, s], qs[:, s],
                                         [p // 16 * 16 + (p + 8) % 16 for p in range(32)]).then_inc(q_taken, 1)

            def rope_add(ch, t):
                s = t % 2
                n = ch * L0_TILES + t + 1
                dve.wait_ge(cos_done, n)
                dve.nop(nofuse=True)
                dve.wait_ge(sin_done, n)
                dve.nop(nofuse=True)
                nc.vector.tensor_tensor(qc[:, t % 3], qc[:, t % 3], qr[:, s], ALU.add).then_inc(rope_sum, 1)

            def rope_high(ch, t):
                s = t % 2
                dve.wait_ge(rope_sum, ch * L0_TILES + t + 1)
                dve.nop(nofuse=True)
                dve.wait_ge(q_stored[s], 16 * (ch * (TILES // 2) + t // 2 + 1))
                dve.nop(nofuse=True)
                nc.vector.tensor_copy(parts[:, s, HI], qc[:, t % 3]).then_inc(rope_hi, 1)

            def plain_high(ch, t):
                s = t % 2
                dve.wait_ge(proj_read, ch * UNITS + L1_FIRST + t + 3)
                dve.nop(nofuse=True)
                dve.wait_ge(q_stored[s], 16 * (ch * (TILES // 2) + L0_TILES // 2 + t // 2 + 1))
                dve.nop(nofuse=True)
                nc.vector.tensor_copy(parts[:, s, HI], qs[:, s]).then_inc(plain_hi, 1)

            def plain_low(ch, t):
                s = t % 2
                n = ch * L1_TILES + t + 1
                dve.wait_ge(plain_hi, n)
                dve.nop(nofuse=True)
                nc.vector.tensor_tensor(parts[:, s, LO], qs[:, s], f32(parts[:, s, HI]), ALU.subtract).then_inc(plain_lo, 1)
                dve.wait_ge(plain_lo, n)
                dve.sem_inc(q_taken, 1)

            def chunk(ch, last):
                for t in range(L0_TILES + 1):
                    if t < L0_TILES:
                        rope_start(ch, t)
                    if t:
                        rope_add(ch, t - 1)
                    n = t - XS_AFTER
                    if t:
                        rope_high(ch, t - 1)
                    if 0 <= n < XS_JOBS:
                        split_low(ch, True, n)
                if not last:
                    layer_stats(ch + 1)
                    layer_norm(ch + 1)
                for t in range(L1_TILES):
                    n = t - XN_AFTER
                    turning = not last and 0 <= n < XN_JOBS
                    plain_high(ch, t)
                    plain_low(ch, t)
                    if turning:
                        split_low(ch + 1, False, n)
                    if not last:
                        if t == 1:
                            rms_stats(ch + 1)
                        if t == 3:
                            rms_norm(ch + 1)

            dve.sem_inc(h_stored[0], 16)
            dve.sem_inc(h_stored[1], 16)
            dve.sem_inc(q_stored[0], 16)
            dve.sem_inc(q_stored[1], 16)
            layer_stats(0)
            layer_norm(0)
            rms_stats(0)
            rms_norm(0)
            for n in range(XN_JOBS):
                split_low(0, False, n)
            with dve.Fori(0, NCH - 1) as ch:
                chunk(ch, False)
            chunk(NCH - 1, True)

        @block.gpsimd
        def _(pool):
            pool.wait_ge(consts_loaded, 64)

            def residual(ch):
                for t in range(TT):
                    pool.wait_ge(xn_ready, TT * ch + t + 1)
                    pool.nop(nofuse=True)
                    nc.gpsimd.tensor_tensor(xin[:, t], xin[:, t], xn[:, t], ALU.add).then_inc(resid_ready, 1)

            def rope_sin(ch, t):
                s = t % 2
                pool.wait_ge(q_taken, ch * TILES + t + 3)
                pool.nop(nofuse=True)
                nc.gpsimd.tensor_tensor(qr[:, s], qr[:, s], sin[:, bass.ds((ch % 2) * CH, CH)], ALU.mult).then_inc(sin_done, 1)

            def rope_low(ch, t):
                s = t % 2
                pool.wait_ge(rope_hi, ch * L0_TILES + t + 1)
                pool.nop(nofuse=True)
                nc.gpsimd.tensor_tensor(parts[:, s, LO], qc[:, t % 3], f32(parts[:, s, HI]), ALU.subtract).then_inc(rope_lo, 1)

            def chunk(ch, last):
                for t in range(L0_TILES):
                    rope_sin(ch, t)
                    if t:
                        rope_low(ch, t - 1)
                rope_low(ch, L0_TILES - 1)
                if not last:
                    residual(ch + 1)

            residual(0)
            with pool.Fori(0, NCH - 1) as ch:
                chunk(ch, False)
            chunk(NCH - 1, True)


MAPS = 4
RING = 4
HALF = 512
PIECES = tuple(piece for i, keys in enumerate(range(P, S + P, P)) for piece in
               ([(i, 0, keys)] if keys <= HALF else
                [(i, 0, min(HALF, keys - 2 * P)), (i, min(HALF, keys - 2 * P), max(keys - HALF, 2 * P))]))
NP = len(PIECES)
STEPS = tuple((c, j) for c in range(S // HALF) for j in range((c + 1) * HALF // P))
NS = len(STEPS)
DIAGONAL = tuple(s for s, (c, j) in enumerate(STEPS) if P * j >= HALF * c)
TURNS = 3
PROBS = 3
EARLY = 22
LAG = 3
SECOND_MAX_ROW = len(PASSES) * D1
BANKS = 3
APART = 2000
FP32R_LEAST = 256
PARTS = MAPS + 1


def columns(s):
    c, j = STEPS[s]
    return HALF - max(0, P * j - HALF * c)


def piece_stream():
    work = [0]
    for k in range(NS):
        s, old = (k + LAG) % NS, (k + 1) % NS
        diagonal = P if s in DIAGONAL else 0
        work += [work[-1] + (m + 1) * (max(columns(s), FP32R_LEAST) + diagonal) for m in range(MAPS)]
        work[-1] += 2 * columns(old)
        work.append(work[-1] + 2 * columns(old))
    order = [(EARLY + n) % (MAPS * NP) for n in range(MAPS * NP)]
    maxima = [0]
    for n in order:
        maxima.append(maxima[-1] + 64 + PIECES[n % NP][2])
    return [sum(m * work[-1] < w * maxima[-1] for m in maxima[:-1]) if w else 0 for w in work]


STREAM = piece_stream()
COMPLETE = next(p for p in range(NS * PARTS) if STREAM[p + 1] >= MAPS * NP - EARLY)
ROWS_AT, ROWS_READ_AT = COMPLETE + 6, COMPLETE + 7
OUT0_AT, OUT1_AT = 4 * PARTS, NS * PARTS - 2


class Layer:

    def __init__(self, name, d, groups, combos, own_keys, scale):
        self.name, self.d, self.groups = name, d, groups
        self.combos = combos
        self.kmaps = MAPS if own_keys else 1
        self.scale = scale
        self.max_row = len(combos) * d
        self.loads = 2 * len(combos) + 1


def attention_block(nc, lay, q_scr, k_scr, zero_rows, v, out, neg_lambda, ident, stacks, first):
    differential = neg_lambda is not None
    groups = lay.groups
    with ExitStack() as ctx:
        def sb(name, shape, dt=F32):
            return ctx.enter_context(nc.sbuf_tensor(f"{lay.name}_{name}", shape, dt))

        def sem(name):
            return ctx.enter_context(nc.semaphore(f"{lay.name}_{name}"))

        def psum(name, shape):
            return ctx.enter_context(nc.psum_tensor(f"{lay.name}_{name}", shape, F32))

        qst, kst, mask, ident_b, future = stacks
        vst = sb("v_stack", [P, 2, lay.kmaps, QB, 32])
        tops = sb("tops", [P, 2, MAPS, QB])
        pair = sb("pair", [P, 2, MAPS, QB // 2, 2])
        ntop = sb("neg_top", [P, 2, MAPS, QB])
        ntop_r = sb("neg_top_hi", [P, MAPS, QB], F32R)
        mrow = sb("max_rows", [P, P])
        probs = sb("probs", [P, PROBS, MAPS, HALF])
        osb = sb("out_t", [P, 2, HALF])
        rec = sb("recip", [P, 2, QB // 2 * MAPS])
        kept = sb("kept", [P, 2, QB // 2, MAPS * D0])
        prod = sb("prod", [P, QB // 2, MAPS * D0])
        result = sb("result", [P, 2, QB // 2, MAPS * D0])
        ps_s = psum("scores", [P, BANKS, HALF])
        ps_t = psum("scores_t", [P, BANKS, HALF])
        ps_o = psum("out", [P, HALF])
        ps_x = psum("turn", [P, HALF])

        loaded = [sem(f"loaded{u}") for u in range(RING)]
        q_pad = sem("q_pad")
        k_pad = sem("k_pad")
        k_ones = sem("k_ones")
        maps_pad = sem("maps_pad")
        mask_zero = sem("mask_zero")
        mask_ready = sem("mask_ready")
        v_zeroed = sem("v_zeroed")
        v_ready = sem("v_ready")
        scored = sem("scored")
        topped = sem("topped")
        top_step = sem("top_step")
        tops_split = sem("tops_split")
        turned = sem("turned")
        turn_read = sem("turn_read")
        rows_read = sem("rows_read")
        rows_set = sem("rows_set")
        scored_t = sem("scored_t")
        exped = sem("exped")
        future_ready = sem("future_ready")
        summed = sem("summed")
        out_read = sem("out_read")
        rec_done = sem("rec_done")
        prod_done = sem("prod_done")
        stored = [sem(f"stored{c}") for c in range(2)]
        divided = sem("divided")
        block = ctx.enter_context(nc.Block())

        UNITS_T = MAPS * NS
        PIECES_G = MAPS * NP

        def iterate(eng, body):
            rounds = groups // RING
            with eng.Fori(0, rounds - 1) as i:
                for u in range(RING):
                    body(i, u, RING)
            for u in range(RING):
                body(rounds - 1, u, RING - 1 - u)

        def after(i, u, n):
            return i * RING + (u + n), (u + n) % RING, i + (u + n) // RING

        def scored_step(i, u, k, ahead):
            if k + LAG < NS:
                return i, u, k + LAG
            return (*after(i, u, 1)[:0:-1], k + LAG - NS) if ahead else None

        def summed_step(i, u, k, ahead):
            if k + 1 < NS:
                return i, u, k + 1
            return (*after(i, u, 1)[:0:-1], 0) if ahead else None

        def pieces_of(p, ahead):
            first, last = EARLY + STREAM[p], EARLY + STREAM[p + 1]
            return (range(first, min(last, PIECES_G)) if ahead else (),
                    range(max(first - PIECES_G, 0), max(last - PIECES_G, 0)) if ahead > 1 else ())

        def prologue_pieces(n):
            bounds = [0] + [EARLY - (LAG * MAPS - k) * 14 // (LAG * MAPS) for k in range(LAG * MAPS + 1)]
            return range(bounds[n], bounds[n + 1])

        @block.sync
        def _(sp):
            def load(rnd, u):
                rows = MAPS * lay.d
                g = rnd * RING + u
                pairs = rnd * (RING // 2) + u // 2
                for n, (a, c) in enumerate(lay.combos):
                    at = slice(n * lay.d, (n + 1) * lay.d)
                    if differential:
                        q_src = q_scr[bass.ds(pairs * rows, rows), u % 2, a, :]
                        k_src = k_scr[bass.ds(pairs * lay.d, lay.d), u % 2, c, :]
                    else:
                        q_src = q_scr[bass.ds(g * rows, rows), a, :]
                        k_src = k_scr[bass.ds(g * rows, rows), c, :]
                    sp.dma_start(f32(qst[at, u]), q_src.rearrange("(m d) n -> d m n", m=MAPS)).then_inc(loaded[u], 16)
                    sp.dma_start(f32(kst[at, u, 0:lay.kmaps]), k_src.rearrange("(m d) n -> d m n", m=lay.kmaps)).then_inc(loaded[u], 16)
                sp.dma_start(f32(qst[lay.max_row:lay.max_row + 2, u]), zero_rows).then_inc(loaded[u], 16)

            def set_rows(g, slot):
                sp.wait_ge(rows_read, g + 1)
                sp.nop(nofuse=True)
                for a in range(2):
                    row = f32(qst[lay.max_row + a:lay.max_row + a + 1, slot])
                    sp.dma_start(row.rearrange("o m (i n) -> o (m i) n", n=P),
                                 mrow[a * 32:a * 32 + 32]).then_inc(rows_set, 16)

            def store(i, u, c):
                n = i * (RING // 2) + u // 2 if differential else i * RING + u
                sp.wait_ge(divided, 2 * n + c + 1)
                sp.nop(nofuse=True)
                sp.dma_start(out[:, bass.ds(n * QB + c * (QB // 2), QB // 2), :], result[:, c]).then_inc(stored[c], 16)

            def body(i, u, ahead):
                stores = u % 2 or not differential
                if stores:
                    store(i, u, 0)
                if ahead:
                    g, slot, _ = after(i, u, 1)
                    set_rows(g, slot)
                if ahead == RING:
                    sp.wait_ge(scored_t, UNITS_T * (i * RING + u + 1))
                    sp.nop(nofuse=True)
                    load(i + 1, u)
                if stores:
                    store(i, u, 1)

            for u in range(RING):
                if first:
                    sp.wait_ge(q_pad, u + 1)
                    sp.wait_ge(k_pad, u + 1)
                load(0, u)
            set_rows(0, 0)
            iterate(sp, body)
            for c in range(2):
                sp.wait_ge(stored[c], 16 * (groups // 2 if differential else groups) + 16)

        @block.tensor
        def _(pe):
            pe.sem_inc(summed, PROBS)

            def pieces(i, u, n, ns, ones=None):
                g, slot, rnd = after(i, u, n)
                for n in ns:
                    m, (r, k0, keys) = n // NP, PIECES[n % NP]
                    if n == 0:
                        if first and ones is not None:
                            pe.wait_ge(k_ones, 2 * ones)
                        pe.wait_ge(loaded[slot], rnd * (16 * lay.loads) + 16 * lay.loads)
                        pe.nop(nofuse=True)
                    pe.wait_ge(topped, g * PIECES_G + n + 1)
                    pe.nop(nofuse=True)
                    width = max(keys, FP32R_LEAST)
                    nc.tensor.matmul(ps_s[:, n % BANKS, 0:width], qst[:, slot, m, r * P:(r + 1) * P],
                                     kst[:, slot, m % lay.kmaps, k0:k0 + width],
                                     start=True, stop=True).then_inc(scored, 1)

            def turn_rows(g, turn):
                pe.wait_ge(tops_split, g + 1)
                pe.nop(nofuse=True)
                if turn is not None:
                    pe.wait_ge(turn_read, turn)
                    pe.nop(nofuse=True)
                nc.tensor.transpose(ps_x[0:64, 0:P], ntop[:].rearrange("p a m i -> p (a m i)"), ident[:]).then_inc(turned, 1)

            def turn_out(g, c, turn):
                pe.wait_ge(out_read, 2 * g + c + 1)
                pe.nop(nofuse=True)
                pe.wait_ge(turn_read, turn)
                pe.nop(nofuse=True)
                for q in range(HALF // P):
                    mm = nc.tensor.transpose(ps_x[:, q * P:(q + 1) * P], osb[:, c, q * P:(q + 1) * P], ident[:])
                mm.then_inc(turned, 1)

            def scores_t(i, u, s, m):
                g = i * RING + u
                c, j = STEPS[s]
                n = MAPS * s + m
                if n == 0:
                    pe.wait_ge(rows_set, 32 * g + 32)
                    pe.nop(nofuse=True)
                start = HALF - max(columns(s), FP32R_LEAST)
                pe.wait_ge(exped, UNITS_T * g + n + 1 + APART)
                pe.nop(nofuse=True)
                mm = nc.tensor.matmul(ps_t[:, n % BANKS, start:HALF], kst[:, u, m % lay.kmaps, j * P:(j + 1) * P],
                                      qst[:, u, m, c * HALF + start:(c + 1) * HALF],
                                      start=True, stop=s not in DIAGONAL)
                if s in DIAGONAL:
                    lo = HALF - columns(s)
                    mm = nc.tensor.matmul(ps_t[:, n % BANKS, lo:lo + P], ident_b[:], future[:], start=False, stop=True)
                mm.then_inc(scored_t, 1)

            def pv(i, u, s, first=False):
                g = i * RING + u
                c, j = STEPS[s]
                lo = HALF - columns(s)
                pe.wait_ge(exped, UNITS_T * g + MAPS * (s + 1) + BANKS + APART)
                pe.nop(nofuse=True)
                if s == 0:
                    pe.wait_ge(v_ready, g + 1)
                    pe.nop(nofuse=True)
                if j == 0 and not first:
                    pe.wait_ge(out_read, 2 * g + c)
                    pe.nop(nofuse=True)
                for m in range(MAPS):
                    mm = nc.tensor.matmul(ps_o[32 * m:32 * m + 32, lo:HALF], vst[:, u % 2, m % lay.kmaps, j, :],
                                          probs[:, s % PROBS, m, lo:HALF],
                                          start=(j == 0), stop=(P * (j + 1) == HALF * (c + 1)))
                mm.then_inc(summed, 1)

            def body(i, u, ahead):
                g = i * RING + u
                for k in range(NS):
                    step, old = scored_step(i, u, k, ahead), summed_step(i, u, k, ahead)
                    for part in range(PARTS):
                        p = PARTS * k + part
                        if part < MAPS and step:
                            scores_t(*step, part)
                        if part == MAPS and old:
                            pv(*old)
                        for n, ns in enumerate(pieces_of(p, ahead)):
                            pieces(i, u, n + 1, ns)
                        if p == OUT0_AT:
                            turn_out(g, 0, TURNS * g + 1)
                        if p == ROWS_AT and ahead:
                            turn_rows(g + 1, TURNS * g + 2)
                        if p == OUT1_AT:
                            turn_out(g, 1, TURNS * g + (3 if ahead else 2))

            if first:
                pe.wait_ge(future_ready, 2)
            pieces(0, 0, 0, range(PIECES_G), ones=1)
            turn_rows(0, None)
            pieces(0, 0, 1, prologue_pieces(0), ones=RING)
            for n in range(LAG * MAPS):
                scores_t(0, 0, n // MAPS, n % MAPS)
                pieces(0, 0, 1, prologue_pieces(n + 1))
            pv(0, 0, 0, first=True)
            iterate(pe, body)

        @block.scalar
        def _(act):
            act.sem_inc(exped, BANKS + APART)

            def exp(i, u, s):
                g = i * RING + u
                lo = HALF - columns(s)
                act.wait_ge(summed, NS * g + s + 1)
                act.nop(nofuse=True)
                for m in range(MAPS):
                    n = MAPS * s + m
                    act.wait_ge(scored_t, UNITS_T * g + n + 1)
                    act.nop(nofuse=True)
                    nc.scalar.activation(probs[:, s % PROBS, m, lo:HALF], ps_t[:, n % BANKS, lo:HALF],
                                         ACT.Exp, scale=lay.scale).then_inc(exped, 1)

            def read_out(g, c):
                last_step = max(s for s in range(NS) if STEPS[s][0] == c)
                act.wait_ge(summed, NS * g + last_step + 1 + PROBS)
                act.nop(nofuse=True)
                nc.scalar.copy(osb[:, c], ps_o[:]).then_inc(out_read, 1)

            def body(i, u, ahead):
                g = i * RING + u
                for k in range(NS):
                    if k == 3:
                        read_out(g, 0)
                    if k == NS - 1:
                        read_out(g, 1)
                    step = scored_step(i, u, k, ahead)
                    if step:
                        exp(*step)

            for s in range(LAG):
                exp(0, 0, s)
            iterate(act, body)

        @block.vector
        def _(dve):
            if first:
                nc.vector.memset(f32(qst[lay.max_row:P, 0]), 0.0).then_inc(q_pad, 1)
            dve.sem_inc(stored[0], 16)
            dve.sem_inc(stored[1], 16)
            dve.sem_inc(topped, BANKS)
            if first:
                dve.wait_ge(mask_ready, 1)

            def maxima(i, u, n, ns):
                g, slot, _ = after(i, u, n)
                par = (u + n) % 2
                for n in ns:
                    m, (r, k0, keys) = n // NP, PIECES[n % NP]
                    dve.wait_ge(scored, g * PIECES_G + n + 1)
                    dve.nop(nofuse=True)
                    diagonal = k0 + keys == P * (r + 1)
                    zeros = mask[:, HALF + P - keys:HALF + P] if diagonal else mask[:, 0:keys]
                    top = tops[:, par, m, r:r + 1] if r < QB // 2 else pair[:, par, m, r - QB // 2, int(k0 > 0):int(k0 > 0) + 1]
                    nc.vector.tensor_tensor_reduce(out=ps_s[:, n % BANKS, 0:keys], in0=ps_s[:, n % BANKS, 0:keys], in1=zeros,
                                                   scale=1.0, scalar=-3e38, op0=ALU.add, op1=ALU.max,
                                                   accum_out=top).then_inc(topped, 1)

            def split_tops(g, par, stage):
                if stage == 0:
                    dve.wait_ge(topped, g * PIECES_G + PIECES_G + BANKS)
                else:
                    dve.wait_ge(top_step, 3 * g + stage)
                dve.nop(nofuse=True)
                if stage == 0:
                    nc.vector.tensor_tensor(tops[:, par, :, QB // 2:QB], pair[:, par, :, :, 0], pair[:, par, :, :, 1],
                                            ALU.max).then_inc(top_step, 1)
                elif stage == 1:
                    nc.vector.tensor_scalar(ntop_r[:], tops[:, par], -1.0, None, ALU.mult).then_inc(top_step, 1)
                elif stage == 2:
                    nc.vector.tensor_copy(ntop[:, 0], f32(ntop_r[:])).then_inc(top_step, 1)
                else:
                    nc.vector.scalar_tensor_tensor(ntop[:, 1], tops[:, par], -1.0, f32(ntop_r[:]), ALU.mult,
                                                   ALU.subtract).then_inc(tops_split, 1)

            def read_rows(g, turn, first=False):
                dve.wait_ge(turned, turn + 1)
                dve.nop(nofuse=True)
                if not first:
                    dve.wait_ge(rows_set, 32 * g)
                    dve.nop(nofuse=True)
                nc.vector.tensor_copy(mrow[0:64], ps_x[0:64, 0:P]).then_inc(rows_read, 1)
                dve.wait_ge(rows_read, g + 1)
                dve.sem_inc(turn_read, 1)

            def divide(i, u, c, turn, stage):
                n = 2 * (i * RING + u) + c
                x = ps_x[:].rearrange("p (q e) -> p q e", e=32)
                over = rec[:, c].rearrange("p (q o) -> p q o", o=1).broadcast_to([P, HALF // 32, D0])

                def cols(t):
                    return t.rearrange("p b (m d) -> p (b m) d", d=D0)

                if stage == 0:
                    dve.wait_ge(turned, turn + 1)
                    dve.nop(nofuse=True)
                    nc.vector.reciprocal(rec[:, c], x[:, :, D0]).then_inc(rec_done, 1)
                elif stage == 1:
                    dve.wait_ge(rec_done, n + 1)
                    dve.nop(nofuse=True)
                    if not differential or u % 2:
                        dve.wait_ge(stored[c], 16 * ((i * RING + u if not differential else i * (RING // 2) + u // 2) + 1))
                        dve.nop(nofuse=True)
                    part = result[:, c] if not differential else prod[:] if u % 2 else kept[:, c]
                    nc.vector.tensor_tensor(cols(part), x[:, :, 0:D0], over, ALU.mult).then_inc(turn_read, 1)
                elif not differential:
                    dve.wait_ge(turn_read, turn + 1)
                    dve.sem_inc(divided, 1)
                elif u % 2:
                    dve.wait_ge(turn_read, turn + 1)
                    dve.nop(nofuse=True)
                    nc.vector.scalar_tensor_tensor(result[:, c], prod[:], neg_lambda[:], kept[:, c], ALU.mult,
                                                   ALU.add).then_inc(divided, 1)

            def body(i, u, ahead):
                g = i * RING + u
                g1 = after(i, u, 1)[0]
                for p in range(NS * PARTS):
                    if ahead and 0 <= p - COMPLETE - 1 < 4:
                        split_tops(g1, (u + 1) % 2, p - COMPLETE - 1)
                    if 0 <= p - OUT0_AT - 1 < 3:
                        divide(i, u, 0, TURNS * g + 1, p - OUT0_AT - 1)
                    if p == ROWS_READ_AT and ahead:
                        read_rows(g1, TURNS * g + 2)
                    if p == NS * PARTS - 1:
                        divide(i, u, 1, TURNS * g + (3 if ahead else 2), 0)
                    for n, ns in enumerate(pieces_of(p, ahead)):
                        maxima(i, u, n + 1, ns)
                for stage in (1, 2):
                    divide(i, u, 1, TURNS * g + (3 if ahead else 2), stage)

            maxima(0, 0, 0, range(PIECES_G))
            for stage in range(4):
                split_tops(0, 0, stage)
            read_rows(0, 0, first=True)
            maxima(0, 0, 1, range(EARLY))
            iterate(dve, body)
            dve.wait_ge(turn_read, TURNS * groups)

        @block.gpsimd
        def _(pool):
            nc.gpsimd.memset(vst[:], 0.0).then_inc(v_zeroed, 1)

            def set_slot(n):
                nc.gpsimd.memset(f32(kst[lay.max_row:P, n, 0]), 0.0).then_inc(k_pad, 1)
                pool.wait_ge(k_pad, n + 1)
                nc.gpsimd.memset(f32(kst[lay.max_row:lay.max_row + 2, n, 0]), 1.0).then_inc(k_ones, 1)
                pool.wait_ge(k_ones, 2 * n + 1)
                nc.gpsimd.memset(f32(kst[SECOND_MAX_ROW:SECOND_MAX_ROW + 2, n, 0]), 1.0).then_inc(k_ones, 1)
                pool.wait_ge(k_ones, 2 * n + 2)
                if n:
                    pool.wait_ge(q_pad, n)
                    nc.gpsimd.memset(f32(qst[lay.max_row:P, n]), 0.0).then_inc(q_pad, 1)
                    pool.wait_ge(q_pad, n + 1)

            if first:
                nc.gpsimd.memset(mask[:], 0.0).then_inc(mask_zero, 1)
                nc.gpsimd.memset(future[:], 0.0).then_inc(mask_zero, 1)
                nc.gpsimd.tensor_copy(ident_b[:], ident[:]).then_inc(future_ready, 1)
                pool.wait_ge(mask_zero, 2)
                nc.gpsimd.affine_select(out=future[:], in_=future[:], compare_op=ALU.is_ge, fill=NEG,
                                        base=0, pattern=[[1, P]], channel_multiplier=-1).then_inc(future_ready, 1)
                nc.gpsimd.affine_select(out=mask[:, HALF:], in_=mask[:, HALF:], compare_op=ALU.is_ge, fill=NEG,
                                        base=0, pattern=[[-1, P]], channel_multiplier=1).then_inc(mask_ready, 1)
                pool.wait_ge(v_zeroed, 1)
                pool.wait_ge(future_ready, 2)
                pool.wait_ge(mask_ready, 1)
                set_slot(0)
                set_slot(1)
            pool.wait_ge(v_zeroed, 1)

            def copy_values(i, u, n):
                g, slot, rnd = after(i, u, n)
                blocks = lay.kmaps * QB
                at = g * blocks if not differential else (i * (RING // 2) + (u + n) // 2) * QB
                pool.nop(nofuse=True)
                nc.gpsimd.tensor_copy(vst[:, (u + n) % 2, :, :, 0:VW].rearrange("p m k e -> p (m k) e"),
                                      v[:, bass.ds(at, blocks), :]).then_inc(v_ready, 1)

            def body(i, u, ahead):
                g = i * RING + u
                if ahead:
                    pool.wait_ge(summed, NS * g + PROBS)
                    copy_values(i, u, 1)

            copy_values(0, 0, 0)
            if first:
                pool.wait_ge(v_ready, 1)
                for n in range(2, RING):
                    set_slot(n)
                for n in range(RING):
                    nc.gpsimd.memset(f32(kst[SECOND_MAX_ROW:P, n, 1:MAPS]), 0.0).then_inc(maps_pad, 1)
                pool.wait_ge(maps_pad, RING)
                for n in range(RING):
                    nc.gpsimd.memset(f32(kst[SECOND_MAX_ROW:SECOND_MAX_ROW + 2, n, 1:MAPS]), 1.0).then_inc(maps_pad, 1)
                pool.wait_ge(maps_pad, 2 * RING)
            iterate(pool, body)


RR = 4 * RK


def modulate_block(nc, ins, scr, ht, mod, bst, ident):
    with ExitStack() as ctx:
        def sb(name, shape, dt=F32):
            return ctx.enter_context(nc.sbuf_tensor(name, shape, dt))

        def sem(name):
            return ctx.enter_context(nc.semaphore(name))

        def psum(name, shape):
            return ctx.enter_context(nc.psum_tensor(name, shape, F32))

        groups = B * NH1 // MAPS
        heads_a = sb("heads_rows", [P, groups * QB, MAPS * RK])
        a_raw = sb("a_raw", [P, KT, RK])
        a_wide = sb("a_wide", [P, 2, KT, P], F32R)
        b_raw = sb("b_raw", [RK, F])
        b_hi = sb("b_hi", [RK, F], F32R)
        part_sum = sb("part_sum", [P, groups * QB, RK])
        asum = sb("asum", [P, TOK // P, 4, RK])
        m32 = sb("mod32", [RR, TOK])
        ps_t = psum("ps_turn", [P, 4, CH])
        ps_h = psum("ps_ha", [P, 2, CH])

        loaded = sem("mod_loaded")
        heads_loaded = sem("heads_loaded")
        h_loaded = sem("mod_h_loaded")
        a_zeroed = sem("a_zeroed")
        mod_zeroed = sem("mod_zeroed")
        a_hi = sem("a_hi")
        a_ready = sem("a_ready")
        bh_ready = sem("bh_ready")
        bl_ready = sem("bl_ready")
        b_placed = sem("b_placed")
        heads_sum = sem("heads_sum")
        sum_ready = sem("sum_ready")
        sum_turned = sem("sum_turned")
        tanh_ready = sem("tanh_ready")
        ha_ready = sem("ha_ready")
        ha_read = sem("ha_read")
        mod_hi = sem("mod_hi")
        mod_lo = sem("mod_lo_ready")
        mod_ready = sem("mod_ready")
        block = ctx.enter_context(nc.Block())

        @block.sync
        def _(sp):
            sp.dma_start(heads_a[:], scr["heads"]).then_inc(heads_loaded, 16)
            sp.dma_start(a_raw[:], ins["a"].rearrange("(k p) n -> p k n", p=P)).then_inc(loaded, 16)
            sp.dma_start(b_raw[:], ins["b"]).then_inc(loaded, 16)
            for n in range(2):
                sp.dma_start(f32(ht[:, n]), scr["h"][:, n]).then_inc(h_loaded, 16)
            sp.wait_ge(mod_zeroed, 2)
            sp.wait_ge(bh_ready, 1)
            sp.wait_ge(bl_ready, 1)
            for n in range(4):
                sp.dma_start(f32(bst[n * RK:(n + 1) * RK]), (f32(b_hi[:]), b_raw[:])[n % 2]).then_inc(b_placed, 16)
            sp.wait_ge(b_placed, 64)

        @block.gpsimd
        def _(pool):
            nc.gpsimd.memset(f32(a_wide[:]), 0.0).then_inc(a_zeroed, 1)
            nc.gpsimd.memset(f32(bst[:]), 0.0).then_inc(mod_zeroed, 1)
            nc.gpsimd.memset(f32(mod[:]), 0.0).then_inc(mod_zeroed, 1)
            pool.wait_ge(mod_zeroed, 2)

        @block.tensor
        def _(pe):
            pe.wait_ge(sum_ready, 4)
            for t in range(TOK // P):
                mm = nc.tensor.transpose(ps_t[0:RR, t // TT, t % TT * P:(t % TT + 1) * P],
                                         asum[:, t].rearrange("p n r -> p (n r)"), ident[:])
            mm.then_inc(sum_turned, 1)
            pe.wait_ge(a_ready, 4)
            pe.wait_ge(h_loaded, 32)
            for c in range(NCH):
                if c >= 2:
                    pe.wait_ge(ha_read, c - 1)
                for k in range(KT):
                    for n, (a, x) in enumerate(PASSES):
                        mm = nc.tensor.matmul(ps_h[:, c % 2], a_wide[:, a, k, :], ht[:, x, k, c * CH:(c + 1) * CH],
                                              start=(k == 0 and n == 0), stop=(k == KT - 1 and n == 2))
                mm.then_inc(ha_ready, 1)

        @block.scalar
        def _(act):
            act.wait_ge(loaded, 32)
            act.wait_ge(a_zeroed, 1)
            for n in range(4):
                nc.scalar.copy(a_wide[:, HI, :, n * RK:(n + 1) * RK], a_raw[:]).then_inc(a_hi, 1)
            nc.scalar.copy(b_hi[:], b_raw[:]).then_inc(bh_ready, 1)
            act.wait_ge(sum_turned, 1)
            nc.scalar.activation(m32[:], ps_t[0:RR].rearrange("p c n -> p (c n)"), ACT.Tanh).then_inc(tanh_ready, 1)

        @block.vector
        def _(dve):
            for n in range(4):
                dve.wait_ge(a_hi, n + 1)
                cols = slice(n * RK, (n + 1) * RK)
                nc.vector.tensor_tensor(a_wide[:, LO, :, cols], a_raw[:], f32(a_wide[:, HI, :, cols]),
                                        ALU.subtract).then_inc(a_ready, 1)
            dve.wait_ge(heads_loaded, 16)
            nc.vector.tensor_reduce(part_sum[:], heads_a[:].rearrange("p n (m r) -> p n r m", m=MAPS),
                                    AX.X, ALU.add).then_inc(heads_sum, 1)
            dve.wait_ge(heads_sum, 1)
            for n in range(4):
                for b in range(B):
                    src = part_sum[:, b * groups // B * QB:(b + 1) * groups // B * QB, :]
                    red = nc.vector.tensor_reduce(asum[:, b * QB:(b + 1) * QB, n, :],
                                                  src.rearrange("p (g q) r -> p q r g", q=QB), AX.X, ALU.add)
                red.then_inc(sum_ready, 1)
            dve.wait_ge(bh_ready, 1)
            nc.vector.tensor_tensor(b_raw[:], b_raw[:], f32(b_hi[:]), ALU.subtract).then_inc(bl_ready, 1)
            dve.wait_ge(tanh_ready, 1)
            dve.wait_ge(mod_zeroed, 2)
            for c in range(NCH):
                dve.wait_ge(ha_ready, c + 1)
                cols = slice(c * CH, (c + 1) * CH)
                nc.vector.scalar_tensor_tensor(m32[:, cols], m32[:, cols], MOD_SCALE, ps_h[0:RR, c % 2], ALU.mult,
                                               ALU.mult).then_inc(ha_read, 1)
                dve.wait_ge(ha_read, c + 1)
                nc.vector.tensor_copy(mod[0:RR, cols], m32[:, cols]).then_inc(mod_hi, 1)
            dve.wait_ge(mod_hi, NCH)
            low = slice(RR // 2, RR)
            nc.vector.tensor_tensor(m32[low], m32[low], f32(mod[low]), ALU.subtract).then_inc(mod_lo, 1)
            dve.wait_ge(mod_lo, 1)
            nc.vector.tensor_copy(mod[low], m32[low]).then_inc(mod_ready, 1)
            dve.wait_ge(mod_ready, 1)


def output_block(nc, ins, scr, acc, ident):
    with ExitStack() as ctx:
        def sb(name, shape, dt=F32):
            return ctx.enter_context(nc.sbuf_tensor(name, shape, dt))

        def sem(name):
            return ctx.enter_context(nc.semaphore(name))

        def psum(name, shape):
            return ctx.enter_context(nc.psum_tensor(name, shape, F32))

        attn = sb("attn", [P, B, QB, NKV, MAPS * D0])
        wo_raw = sb("wo0_raw", [P, KT, H])
        wo = sb("wo0", [P, 2, KT, H], F32R)
        at = sb("attn_t", [P, 2, CH])
        apart = sb("attn_parts", [P, 2, 2, KT, CH], F32R)
        ps_t = psum("ps_turn0", [P, KT, CH])
        ps_y = psum("ps_y", [P, 4, CH])

        wo_loaded = sem("wo_loaded")
        attn_loaded = sem("attn_loaded")
        acc_loaded = sem("acc_loaded")
        wo_hi = sem("wo_hi")
        wo_ready = sem("wo_ready")
        at_turned = sem("at_turned")
        at_read = sem("at_read")
        at_hi = sem("at_hi")
        at_split = sem("at_split")
        y_ready = sem("y0_ready")
        y_added = sem("y0_added")
        block = ctx.enter_context(nc.Block())

        @block.sync
        def _(sp):
            for b in range(B):
                src = scr["attn"][:, b * NKV * QB:(b + 1) * NKV * QB, :].rearrange("p (k q) e -> p k q e", q=QB)
                for k in range(NKV):
                    sp.dma_start(attn[:, b, :, k, :], src[:, k]).then_inc(attn_loaded, 16)
            sp.dma_start(wo_raw[:], ins["wo0t"].rearrange("(k p) n -> p k n", p=P)).then_inc(wo_loaded, 16)
            sp.dma_start(acc[:], scr["resid"].rearrange("(t p) n -> p t n", p=P)).then_inc(acc_loaded, 16)
            sp.wait_ge(acc_loaded, 16)

        @block.tensor
        def _(pe):
            def turn(c):
                for k in range(KT):
                    if c:
                        pe.wait_ge(at_read, (c - 1) * KT + k + 1)
                    for t in range(TT):
                        b, qb = divmod(c * TT + t, QB)
                        src = attn[:, b, qb, 2 * k:2 * k + 2].rearrange("p k e -> p (k e)")
                        mm = nc.tensor.transpose(ps_t[:, k, t * P:(t + 1) * P], src, ident[:])
                    mm.then_inc(at_turned, 1)

            pe.wait_ge(attn_loaded, 16 * B * NKV)
            turn(0)
            pe.wait_ge(wo_ready, 1)
            for c in range(NCH):
                if c + 1 < NCH:
                    turn(c + 1)
                pe.wait_ge(at_split, (c + 1) * KT)
                for t in range(TT):
                    n = c * TT + t
                    if n >= 4:
                        pe.wait_ge(y_added, n - 3)
                    for k in range(KT):
                        for q, (a, x) in enumerate(PASSES):
                            mm = nc.tensor.matmul(ps_y[:, n % 4], apart[:, c % 2, a, k, t * P:(t + 1) * P], wo[:, x, k, :],
                                                  start=(k == 0 and q == 0), stop=(k == KT - 1 and q == 2))
                    mm.then_inc(y_ready, 1)

        @block.scalar
        def _(act):
            act.wait_ge(wo_loaded, 16)
            nc.scalar.copy(wo[:, HI], wo_raw[:]).then_inc(wo_hi, 1)
            for n in range(NCH * KT):
                act.wait_ge(at_turned, n + 1)
                if n >= 2:
                    act.wait_ge(at_split, n - 1)
                nc.scalar.copy(at[:, n % 2], ps_t[:, n % KT]).then_inc(at_read, 1)

        @block.vector
        def _(dve):
            dve.wait_ge(wo_hi, 1)
            nc.vector.tensor_tensor(wo[:, LO], wo_raw[:], f32(wo[:, HI]), ALU.subtract).then_inc(wo_ready, 1)

            def split(c):
                for k in range(KT):
                    n = c * KT + k
                    dve.wait_ge(at_read, n + 1)
                    if c >= 2 and k == 0:
                        dve.wait_ge(y_ready, (c - 1) * TT)
                    nc.vector.tensor_copy(apart[:, c % 2, HI, k], at[:, n % 2]).then_inc(at_hi, 1)
                    dve.wait_ge(at_hi, n + 1)
                    nc.vector.tensor_tensor(apart[:, c % 2, LO, k], at[:, n % 2], f32(apart[:, c % 2, HI, k]),
                                            ALU.subtract).then_inc(at_split, 1)

            split(0)
            dve.wait_ge(acc_loaded, 16)
            for c in range(NCH):
                if c + 1 < NCH:
                    split(c + 1)
                for t in range(TT):
                    n = c * TT + t
                    dve.wait_ge(y_ready, n + 1)
                    nc.vector.scalar_tensor_tensor(acc[:, n], ps_y[:, n % 4], 1.0 - LAMBDA_INIT, acc[:, n], ALU.mult,
                                                   ALU.add).then_inc(y_added, 1)
            dve.wait_ge(y_added, NCH * TT)


FG = 256
NFG = F // FG
FT = FG // P


def mlp_block(nc, ins, out, ht, acc, mod, bst):
    with ExitStack() as ctx:
        def sb(name, shape, dt=F32):
            return ctx.enter_context(nc.sbuf_tensor(name, shape, dt))

        def sem(name):
            return ctx.enter_context(nc.semaphore(name))

        def psum(name, shape):
            return ctx.enter_context(nc.psum_tensor(name, shape, F32))

        raw_in = sb("raw_in", [P, 2, KT, FG])
        raw_down = sb("raw_down", [P, FT, H])
        win = sb("win", [P, 2, 2, 2, KT, FG], F32R)
        wdown = sb("wdown", [P, 2, 2, FT, H], F32R)
        bgrp = sb("b_group", [P, 2, FG], F32R)
        th = sb("gate_tanh", [P, 2, CH])
        gate = sb("gate", [P, 2, CH])
        gu = sb("gate_up", [P, 2, CH])
        gp = sb("gate_up_parts", [P, 2, 2, FT, CH], F32R)
        ps_g = psum("ps_gate_up", [P, FT, 2, CH])
        ps_y = psum("ps_down", [P, TT, CH])

        raw_loaded = sem("mlp_raw_loaded")
        raw_hi = sem("mlp_raw_hi")
        raw_split = sem("mlp_raw_split")
        b_copied = sem("b_copied")
        gate_ready = sem("gate_ready")
        gate_tanh = sem("gate_tanh_ready")
        gate_step = sem("gate_step")
        gate_done = sem("gate_done")
        gp_hi = sem("gp_hi")
        gp_ready = sem("gp_ready")
        down_ready = sem("down_ready")
        down_added = sem("down_added")
        stored = sem("stored")
        block = ctx.enter_context(nc.Block())
        in_src = [ins["win_t"], ins["wup_t"]]

        def groups(eng, body):
            with eng.Fori(0, NFG // 2 - 1) as i:
                for slot in range(2):
                    body(i, slot, True)
            for slot in range(2):
                body(NFG // 2 - 1, slot, slot == 0)

        @block.sync
        def _(sp):
            def load(g):
                cols = bass.ds(g * FG, FG)
                for n in range(2):
                    sp.dma_start(raw_in[:, n], in_src[n].rearrange("(k p) f -> p k f", p=P)[:, :, cols]).then_inc(raw_loaded, 16)
                sp.dma_start(raw_down[:], ins["wdown_t"][cols].rearrange("(t p) n -> p t n", p=P)).then_inc(raw_loaded, 16)

            load(0)

            def body(i, slot, more):
                if more:
                    sp.wait_ge(raw_split, 2 * (2 * i + slot) + 2)
                    sp.nop(nofuse=True)
                    load(2 * i + slot + 1)

            groups(sp, body)
            for c in range(NCH):
                sp.wait_ge(down_added, (NFG - 1) * NCH * TT + (c + 2) * TT)
                sp.dma_start(out[c * CH:(c + 1) * CH].rearrange("(t p) n -> p t n", p=P),
                             acc[:, c * TT:(c + 1) * TT]).then_inc(stored, 16)
            sp.wait_ge(stored, 16 * NCH)

        @block.tensor
        def _(pe):
            def gates(i, slot, c):
                g = 2 * i + slot
                if c == 0:
                    pe.wait_ge(raw_split, 2 * g + 2)
                    pe.nop(nofuse=True)
                    pe.wait_ge(b_copied, g + 1)
                    pe.nop(nofuse=True)
                cols = slice(c * CH, (c + 1) * CH)
                for f in range(FT):
                    pe.wait_ge(gate_done, (g * NCH + c) * FT + f + 1)
                    pe.nop(nofuse=True)
                    at = slice(f * P, (f + 1) * P)
                    for w in range(2):
                        for k in range(KT):
                            for n, (a, x) in enumerate(PASSES):
                                last = k == KT - 1 and n == 2
                                mm = nc.tensor.matmul(ps_g[:, f, w], win[:, slot, a, w, k, at], ht[:, x, k, cols],
                                                      start=(k == 0 and n == 0), stop=last and w == 1)
                        if w == 0:
                            nc.tensor.matmul(ps_g[:, f, w], bgrp[:, slot, at], mod[:, cols], start=False, stop=True)
                    mm.then_inc(gate_ready, 1)

            def downs(i, slot, c):
                g = 2 * i + slot
                pe.wait_ge(gp_ready, (g * NCH + c + 1) * FT + 2)
                pe.nop(nofuse=True)
                for t in range(TT):
                    pe.wait_ge(down_added, (g * NCH + c) * TT + t + 1 - 0)
                    pe.nop(nofuse=True)
                    for f in range(FT):
                        for n, (a, x) in enumerate(PASSES):
                            mm = nc.tensor.matmul(ps_y[:, t], gp[:, c % 2, a, f, t * P:(t + 1) * P], wdown[:, slot, x, f, :],
                                                  start=(f == 0 and n == 0), stop=(f == FT - 1 and n == 2))
                    mm.then_inc(down_ready, 1)

            def body(i, slot, more):
                for c in range(NCH):
                    if c < NCH - 1:
                        gates(i, slot, c + 1)
                    elif more:
                        gates(i + slot, 1 - slot, 0)
                    downs(i, slot, c)

            gates(0, 0, 0)
            groups(pe, body)

        @block.scalar
        def _(act):
            def split_hi(i, slot, lead=False):
                g = 2 * i + slot
                act.wait_ge(raw_loaded, 48 * g + 48)
                act.nop(nofuse=True)
                if not lead:
                    act.wait_ge(down_added, (g - 1) * (NCH * TT) + TT)
                act.nop(nofuse=True)
                nc.scalar.copy(win[:, slot, HI], raw_in[:]).then_inc(raw_hi, 1)
                nc.scalar.copy(wdown[:, slot, HI], raw_down[:]).then_inc(raw_hi, 1)
                nc.scalar.copy(bgrp[:, slot], f32(bst[:, bass.ds(g * FG, FG)])).then_inc(b_copied, 1)

            def tanh(i, slot, c, f):
                n = ((2 * i + slot) * NCH + c) * FT + f
                act.wait_ge(gate_ready, n + 1)
                act.nop(nofuse=True)
                act.wait_ge(gate_step, n + 1)
                act.nop(nofuse=True)
                nc.scalar.activation(th[:, f], ps_g[:, f, 0], ACT.Tanh, scale=0.5).then_inc(gate_tanh, 1)

            def body(i, slot, more):
                for c in range(NCH):
                    for f in range(FT):
                        tanh(i, slot, c, f)
                    if c == 1 and more:
                        split_hi(i + slot, 1 - slot)

            split_hi(0, 0, lead=True)
            groups(act, body)

        @block.vector
        def _(dve):
            dve.sem_inc(gate_done, FT)
            dve.sem_inc(gate_step, 2)
            dve.sem_inc(down_added, TT)

            def split_lo(i, slot):
                g = 2 * i + slot
                dve.wait_ge(raw_hi, 2 * g + 2)
                dve.nop(nofuse=True)
                nc.vector.tensor_tensor(win[:, slot, LO], raw_in[:], f32(win[:, slot, HI]), ALU.subtract).then_inc(raw_split, 1)
                nc.vector.tensor_tensor(wdown[:, slot, LO], raw_down[:], f32(wdown[:, slot, HI]),
                                        ALU.subtract).then_inc(raw_split, 1)

            def act_gate(i, slot, c, f):
                n = ((2 * i + slot) * NCH + c) * FT + f
                dve.wait_ge(gate_tanh, n + 1)
                dve.nop(nofuse=True)
                nc.vector.scalar_tensor_tensor(gate[:, f], th[:, f], 1.0, ps_g[:, f, 0], ALU.add, ALU.mult).then_inc(gate_step, 1)
                dve.wait_ge(gate_step, n + 3)
                dve.nop(nofuse=True)
                dve.wait_ge(gp_ready, n + 1)
                dve.nop(nofuse=True)
                nc.vector.scalar_tensor_tensor(gu[:, f], gate[:, f], 0.5, ps_g[:, f, 1], ALU.mult, ALU.mult).then_inc(gate_done, 1)
                dve.wait_ge(gate_done, n + 1 + FT)
                dve.nop(nofuse=True)
                nc.vector.tensor_copy(gp[:, c % 2, HI, f], gu[:, f]).then_inc(gp_hi, 1)

            def add(i, slot, c):
                for t in range(TT):
                    n = ((2 * i + slot) * NCH + c) * TT + t
                    dve.wait_ge(down_ready, n + 1)
                    dve.nop(nofuse=True)
                    nc.vector.tensor_tensor(acc[:, c * TT + t], acc[:, c * TT + t], ps_y[:, t], ALU.add).then_inc(down_added, 1)

            def body(i, slot, more):
                for c in range(NCH):
                    if c < NCH - 1:
                        for f in range(FT):
                            act_gate(i, slot, c + 1, f)
                    elif more:
                        for f in range(FT):
                            act_gate(i + slot, 1 - slot, 0, f)
                    add(i, slot, c)
                    if c == 1 and more:
                        split_lo(i + slot, 1 - slot)

            split_lo(0, 0)
            for f in range(FT):
                act_gate(0, 0, 0, f)
            groups(dve, body)

        @block.gpsimd
        def _(pool):
            pool.sem_inc(gp_ready, 2)

            def low(i, slot, c, f):
                n = ((2 * i + slot) * NCH + c) * FT + f
                pool.wait_ge(gp_hi, n + 1)
                pool.nop(nofuse=True)
                nc.gpsimd.tensor_tensor(gp[:, c % 2, LO, f], gu[:, f], f32(gp[:, c % 2, HI, f]), ALU.subtract).then_inc(gp_ready, 1)

            def body(i, slot, more):
                for c in range(NCH):
                    for f in range(FT):
                        low(i, slot, c, f)

            groups(pool, body)


def lambda_block(nc, ins, neg_lambda, zeros_dram):
    with ExitStack() as ctx:
        def sb(name, shape, dt=F32):
            return ctx.enter_context(nc.sbuf_tensor(name, shape, dt))

        def sem(name):
            return ctx.enter_context(nc.semaphore(name))

        vec = sb("lambda_vectors", [P, 4, D0])
        prod = sb("lambda_products", [P, 2, D0])
        dot = sb("lambda_dots", [P, 2])
        e = sb("lambda_exps", [P, 2])
        diff = sb("lambda_diff", [P, 1])
        zeros = sb("zero_rows", [2, MAPS, S])
        zeroed = sem("zero_rows_set")
        zeros_stored = sem("zeros_stored")
        loaded = sem("lambda_loaded")
        step = sem("lambda_step")
        exp_done = sem("lambda_exp")
        block = ctx.enter_context(nc.Block())

        @block.sync
        def _(sp):
            for n, name in enumerate(("lq1", "lk1", "lq2", "lk2")):
                src = ins[name].rearrange("(o d) -> o d", o=1).broadcast_to([P, D0])
                sp.dma_start(vec[:, n], src).then_inc(loaded, 16)
            sp.wait_ge(zeroed, 1)
            sp.dma_start(zeros_dram, zeros[:]).then_inc(zeros_stored, 16)
            sp.wait_ge(zeros_stored, 16)

        @block.gpsimd
        def _(pool):
            nc.gpsimd.memset(zeros[:], 0.0).then_inc(zeroed, 1)

        @block.vector
        def _(dve):
            dve.wait_ge(loaded, 64)
            v = vec[:].rearrange("p (l s) d -> p l s d", s=2)
            nc.vector.tensor_tensor(prod[:], v[:, :, 0, :], v[:, :, 1, :], ALU.mult).then_inc(step, 1)
            dve.wait_ge(step, 1)
            nc.vector.tensor_reduce(dot[:], prod[:], AX.X, ALU.add).then_inc(step, 1)
            dve.wait_ge(exp_done, 1)
            nc.vector.tensor_tensor(diff[:], e[:, 1:2], e[:, 0:1], ALU.subtract).then_inc(step, 1)
            dve.wait_ge(step, 3)
            nc.vector.tensor_scalar(neg_lambda[:], diff[:], -LAMBDA_INIT, None, ALU.add).then_inc(step, 1)
            dve.wait_ge(step, 4)

        @block.scalar
        def _(act):
            act.wait_ge(step, 2)
            nc.scalar.activation(e[:], dot[:], ACT.Exp).then_inc(exp_done, 1)


def program(nc, ins, out):
    with ExitStack() as ctx:
        def sb(name, shape, dt=F32):
            return ctx.enter_context(nc.sbuf_tensor(name, shape, dt))

        scr = {
            "q0": nc.dram_tensor("q0_parts", [B * NH0 * D0, 2, 2, S], F32).ap(),
            "k0": nc.dram_tensor("k0_parts", [B * NKV * D0, 2, 2, S], F32).ap(),
            "q1": nc.dram_tensor("q1_parts", [B * H, 2, S], F32).ap(),
            "k1": nc.dram_tensor("k1_parts", [B * H, 2, S], F32).ap(),
            "h": nc.dram_tensor("h_parts", [P, 2, KT, TOK], F32).ap(),
            "resid": nc.dram_tensor("resid", [TOK, H], F32).ap(),
        }
        ident = sb("ident", [P, P])
        neg_lambda = sb("neg_lambda", [P, 1])
        zeros_dram = nc.dram_tensor("zero_rows_scratch", [2, MAPS, S], F32).ap()
        lambda_block(nc, ins, neg_lambda, zeros_dram)
        diff = Layer("diff", D0, 2 * B * NKV, ((HI, HI), (HI, LO), (LO, HI), (LO, LO)), False, 1.0 / math.sqrt(D0))
        plain = Layer("ffn", D1, B * NH1 // MAPS, PASSES, True, float(np.float32(1.0) / np.sqrt(np.float32(D1))))
        with ExitStack() as values:
            v0 = values.enter_context(nc.sbuf_tensor("v0", [P, B * NKV * QB, VW], F32))
            v1 = values.enter_context(nc.sbuf_tensor("v1", [P, B * NH1 * QB, VW], F32))
            with ExitStack() as weights:
                w0 = weights.enter_context(nc.sbuf_tensor("w0", [P, 2, KT, N0], F32R))
                w1 = weights.enter_context(nc.sbuf_tensor("w1", [P, 2, KT, N1], F32R))
                wp = weights.enter_context(nc.sbuf_tensor("wp", [P, 2, KT, NH1 * RK], F32R))
                weights_block(nc, ins, w0, w1, wp, ident)
                project_block(nc, ins, scr, w0, w1, wp, v0, v1, ident)
            heads_dram = nc.dram_tensor("heads_a", [P, B * NH1 // MAPS * QB, MAPS * RK], F32).ap()
            attn_dram = nc.dram_tensor("attn_out", [P, B * NKV * QB, MAPS * D0], F32).ap()
            stacks = [values.enter_context(nc.sbuf_tensor(name, shape, dt)) for name, shape, dt in (
                ("q_stack", [P, RING, MAPS, S], F32R),
                ("k_stack", [P, RING, MAPS, S], F32R),
                ("mask", [P, HALF + P], F32),
                ("ident_b", [P, P], BF16),
                ("future", [P, P], BF16))]
            attention_block(nc, diff, scr["q0"], scr["k0"], zeros_dram, v0, attn_dram, neg_lambda, ident, stacks, True)
            attention_block(nc, plain, scr["q1"], scr["k1"], zeros_dram, v1, heads_dram, None, ident, stacks, False)
        scr["heads"], scr["attn"] = heads_dram, attn_dram
        acc = sb("acc", [P, TOK // P, H])
        output_block(nc, ins, scr, acc, ident)
        ht = sb("ht_all", [P, 2, KT, TOK], F32R)
        mod = sb("mod_stack", [P, TOK], F32R)
        bst = sb("b_stack", [P, F], F32R)
        modulate_block(nc, ins, scr, ht, mod, bst, ident)
        mlp_block(nc, ins, out, ht, acc, mod, bst)


def rope_tables():
    inv_freq = 1.0 / np.float32(10000.0) ** (np.arange(0, D0, 2, dtype=np.float32) / np.float32(D0))
    freqs = np.arange(S, dtype=np.float32)[None, :] * inv_freq.astype(np.float32)[:, None]
    angle = np.tile(freqs, (P // (D0 // 2), 1)).astype(np.float64)
    sign = np.where(np.arange(P) % D0 < D0 // 2, -1.0, 1.0)[:, None]
    return np.cos(angle).astype(np.float32), (np.sin(angle) * sign).astype(np.float32)


def kernel(**inputs):
    import concourse.bacc as bacc
    from concourse.bass_utils import run_bass_kernel_spmd

    def arr(name):
        return np.asarray(inputs[name])

    cos, sin = rope_tables()
    arrays = {
        "x": arr("L0_attn_hidden_states").reshape(TOK, H),
        "w0t": np.concatenate([arr("L0_attn_wq").T, arr("L0_attn_wk").T, arr("L0_attn_wv").T], axis=1),
        "wo0t": arr("L0_attn_wo").T,
        "lq1": arr("L0_attn_lambda_q1"), "lk1": arr("L0_attn_lambda_k1"),
        "lq2": arr("L0_attn_lambda_q2"), "lk2": arr("L0_attn_lambda_k2"),
        "ln1": arr("L0_ffn_ln1_w").reshape(KT, P).T, "ln2": arr("L0_ffn_ln2_w").reshape(KT, P).T,
        "w1t": np.concatenate([arr("L0_ffn_Wq").T, arr("L0_ffn_Wk").T], axis=1),
        "wv1": arr("L0_ffn_Wv"), "wo1": arr("L0_ffn_Wo"), "a": arr("L0_ffn_A"), "b": arr("L0_ffn_B"),
        "win_t": arr("L0_ffn_W_in_base").T, "wup_t": arr("L0_ffn_W_up_base").T, "wdown_t": arr("L0_ffn_W_down").T,
        "cos": cos, "sin": sin,
    }
    nc = bacc.Bacc("TRN2", target_bir_lowering=False, num_devices=1)
    maps, ins = {}, {}
    for name, a in arrays.items():
        a = np.ascontiguousarray(a)
        maps[f"in_{name}"] = a
        ins[name] = nc.dram_tensor(f"in_{name}", a.shape, mybir.dt.from_np(a.dtype), kind="ExternalInput").ap()
    out = nc.dram_tensor("out", (TOK, H), F32, kind="ExternalOutput").ap()
    program(nc, ins, out)
    res = run_bass_kernel_spmd(nc, [maps], core_ids=[0])
    return res.results[0]["out"].reshape(B, S, H)
```

```python
from contextlib import ExitStack
import math

import numpy as np

import concourse.bass as bass
from concourse import mybir
from concourse.alu_op_type import AluOpType as ALU

F32 = mybir.dt.float32
BF16 = mybir.dt.bfloat16
F32R = mybir.dt.float32r
ACT = mybir.ActivationFunctionType
AX = mybir.AxisListType

P = 128
B, S, H = 2, 1024, 512
TOK = B * S
CH = 512
NCH = TOK // CH
KT = H // P
TT = CH // P
QB = S // P

NH0, NKV, D0 = 32, 8, 16
REP = NH0 // NKV
NQ0 = 2 * NH0 * D0 // P
NK0 = 2 * NKV * D0 // P
N0 = (2 * NH0 + 2 * NKV + NKV) * D0
NH1, D1, RK = 16, 32, 16
N1 = 2 * NH1 * D1
F = 2048
VW = D0 + 1
LAMBDA_INIT = 0.8 - 0.6 * math.exp(-0.3 * 12)
LN_EPS, RMS_EPS, MOD_SCALE = 1e-5, 1e-6, 0.1
NEG = -1e30

HI, LO = 0, 1
PASSES = ((HI, HI), (HI, LO), (LO, HI))


def f32(ap):
    return ap.bitcast(F32)


def weights_block(nc, ins, w0, w1, wp, ident, xin, x_loaded):
    with ExitStack() as ctx:
        def sb(name, shape, dt=F32):
            return ctx.enter_context(nc.sbuf_tensor(name, shape, dt))

        def sem(name):
            return ctx.enter_context(nc.semaphore(name))

        raw0 = sb("raw0", [P, KT, N0])
        raw1 = sb("raw1", [P, KT, N1])
        wv = sb("wv_rows", [P, KT, H])
        wo = sb("wo_rows", [P, KT, H])
        a = sb("a_rows", [P, KT, RK])
        woa = sb("woa_heads", [P, KT, P // D1, RK])
        ps_woa = ctx.enter_context(nc.psum_tensor("ps_woa", [P, KT, RK], F32))
        ps_wp = ctx.enter_context(nc.psum_tensor("ps_wp", [P, KT, NH1 * RK], F32))

        small_loaded = sem("small_loaded")
        raw_loaded = [sem(f"raw_loaded{n}") for n in range(2 * KT)]
        woa_zeroed = sem("woa_zeroed")
        ident_zeroed = sem("ident_zeroed")
        ident_ready = sem("ident_ready")
        woa_summed = sem("woa_summed")
        woa_ready = sem("woa_ready")
        wp_summed = sem("wp_summed")
        hi_ready = sem("hi_ready")
        lo_ready = sem("lo_ready")
        block = ctx.enter_context(nc.Block())

        @block.sync
        def _(sp):
            sp.dma_start(wo[:], ins["wo1"].rearrange("(k p) n -> p k n", p=P)).then_inc(small_loaded, 16)
            sp.dma_start(a[:], ins["a"].rearrange("(k p) n -> p k n", p=P)).then_inc(small_loaded, 16)
            sp.dma_start(wv[:], ins["wv1"].rearrange("(k p) n -> p k n", p=P)).then_inc(small_loaded, 16)
            for n, (raw, name) in enumerate(((raw0, "w0t"), (raw1, "w1t"))):
                for k in range(KT):
                    sp.dma_start(raw[:, k], ins[name][k * P:(k + 1) * P]).then_inc(raw_loaded[n * KT + k], 16)
                if n == 0:
                    sp.dma_start(xin[:], ins["x"][0:CH].rearrange("(t p) n -> p t n", p=P)).then_inc(x_loaded, 16)

        @block.gpsimd
        def _(pool):
            nc.gpsimd.memset(woa[:], 0.0).then_inc(woa_zeroed, 1)
            nc.gpsimd.memset(ident[:], 0.0).then_inc(ident_zeroed, 1)
            pool.wait_ge(ident_zeroed, 1)
            nc.gpsimd.affine_select(out=ident[:], in_=ident[:], compare_op=ALU.not_equal, fill=1.0,
                                    base=0, pattern=[[-1, P]], channel_multiplier=1).then_inc(ident_ready, 1)
            pool.wait_ge(ident_ready, 1)

        @block.tensor
        def _(pe):
            pe.wait_ge(small_loaded, 48)
            for m in range(KT):
                for k in range(KT):
                    mm = nc.tensor.matmul(ps_woa[:, m, :], wo[:, k, m * P:(m + 1) * P], a[:, k, :],
                                          start=(k == 0), stop=(k == KT - 1))
            mm.then_inc(woa_summed, 1)
            pe.wait_ge(woa_ready, P // D1)
            for n in range(KT):
                for m in range(KT):
                    mm = nc.tensor.matmul(ps_wp[:, n, m * 64:(m + 1) * 64], wv[:, m, n * P:(n + 1) * P],
                                          woa[:, m, :, :], start=True, stop=True)
            mm.then_inc(wp_summed, 1)

        @block.vector
        def _(dve):
            dve.wait_ge(woa_zeroed, 1)
            dve.wait_ge(woa_summed, 1)
            for j in range(P // D1):
                rows = slice(j * D1, (j + 1) * D1)
                nc.vector.tensor_copy(woa[rows, :, j, :], ps_woa[rows]).then_inc(woa_ready, 1)
            for n in range(2 * KT):
                w, raw, k = (w0, raw0, n) if n < KT else (w1, raw1, n - KT)
                dve.wait_ge(hi_ready, n + 1)
                nc.vector.tensor_tensor(w[:, LO, k], raw[:, k], f32(w[:, HI, k]), ALU.subtract).then_inc(lo_ready, 1)
            dve.wait_ge(hi_ready, 2 * KT + 1)
            nc.vector.tensor_tensor(wp[:, LO], ps_wp[:], f32(wp[:, HI]), ALU.subtract).then_inc(lo_ready, 1)
            dve.wait_ge(lo_ready, 2 * KT + 1)

        @block.scalar
        def _(act):
            for n in range(2 * KT):
                w, raw, k = (w0, raw0, n) if n < KT else (w1, raw1, n - KT)
                act.wait_ge(raw_loaded[n], 16)
                nc.scalar.copy(w[:, HI, k], raw[:, k]).then_inc(hi_ready, 1)
            act.wait_ge(wp_summed, 1)
            nc.scalar.copy(wp[:, HI], ps_wp[:]).then_inc(hi_ready, 1)
            act.wait_ge(hi_ready, 2 * KT + 1)


L0_TILES = NQ0 + NK0
L1_TILES = N1 // P
TILES = L0_TILES + L1_TILES
V_UNITS = 2
UNITS = TILES + 2 * V_UNITS
L0_FIRST, L0_V, L1_FIRST, L1_V = 0, L0_TILES, L0_TILES + V_UNITS, L0_TILES + V_UNITS + L1_TILES
XN_JOBS, XS_JOBS = KT, 2 * KT
JOBS = XN_JOBS + XS_JOBS
NORM_STEPS = 12


def project_block(nc, ins, scr, w0, w1, wp, v0, v1, ident, xin, x_loaded):
    with ExitStack() as ctx:
        def sb(name, shape, dt=F32):
            return ctx.enter_context(nc.sbuf_tensor(name, shape, dt))

        def sem(name):
            return ctx.enter_context(nc.semaphore(name))

        def psum(name, shape):
            return ctx.enter_context(nc.psum_tensor(name, shape, F32))

        cos = sb("cos", [P, S])
        sin = sb("sin", [P, S])
        ln1 = sb("ln1", [P, KT])
        ln2 = sb("ln2", [P, KT])
        xn = sb("xn", [P, TT, H])
        stats = sb("stats", [P, TT, 6])
        mv = sb("mean_var", [P, TT, 2])
        var = sb("var", [P, 2, TT])
        inv = sb("inv", [P, 2, TT])
        root = sb("root", [P, 2, TT])
        newt = sb("newton", [P, 2, TT])
        sq = sb("square_sum", [P, TT])
        junk = sb("square", [P, H])
        y = sb("turned", [P, 4, CH])
        xnt = sb("xnt", [P, 2, KT, CH], F32R)
        x1t = sb("x1t", [P, 2, KT, CH], F32R)
        ht = sb("ht", [P, 2, 2, CH], F32R)
        qs = sb("q_raw", [P, 2, CH])
        qc = sb("q_cos", [P, 3, CH])
        qr = sb("q_rot", [P, 2, CH])
        parts = sb("q_parts", [P, 2, 2, CH], F32R)
        pj = psum("pj", [P, 2, CH])
        tp = psum("tp", [P, KT, CH])

        consts_loaded = sem("consts_loaded")
        ones_ready = sem("ones_ready")
        norm_step = sem("norm_step")
        inv_ready = sem("inv_ready")
        root_ready = sem("root_ready")
        xn_ready = sem("xn_ready")
        squared = sem("squared")
        resid_ready = sem("resid_ready")
        resid_stored = sem("resid_stored")
        xs_ready = sem("xs_ready")
        turned = sem("turned")
        y_ready = sem("y_ready")
        split_done = sem("split_done")
        h_stored = [sem(f"h_stored{n}") for n in range(2)]
        proj_done = sem("proj_done")
        proj_read = sem("proj_read")
        q_taken = sem("q_taken")
        cos_done = sem("cos_done")
        sin_done = sem("sin_done")
        rope_sum = sem("rope_sum")
        rope_hi = sem("rope_hi")
        rope_lo = sem("rope_lo")
        plain_hi = sem("plain_hi")
        plain_lo = sem("plain_lo")
        q_stored = [sem(f"q_stored{n}") for n in range(2)]
        block = ctx.enter_context(nc.Block())

        def first_job(ch, xs):
            return ch * JOBS + (XN_JOBS if xs else 0)

        XS_AFTER, XN_AFTER = 2, 4

        def xs_jobs(t):
            return range(max(t - XS_AFTER, 0), min(t - XS_AFTER + 1, XS_JOBS))

        def operand_tile(xs, n):
            if not xs:
                return xnt[:, HI, n], xnt[:, LO, n]
            return ((x1t[:, HI, n // 2], x1t[:, LO, n // 2]) if n % 2 == 0
                    else (ht[:, n // 2 % 2, HI], ht[:, n // 2 % 2, LO]))

        @block.sync
        def _(sp):
            sp.dma_start(cos[:], ins["cos"]).then_inc(consts_loaded, 16)
            sp.dma_start(sin[:], ins["sin"]).then_inc(consts_loaded, 16)
            sp.dma_start(ln1[:], ins["ln1"]).then_inc(consts_loaded, 16)
            sp.dma_start(ln2[:], ins["ln2"]).then_inc(consts_loaded, 16)

            def residual_store(ch):
                sp.wait_ge(resid_ready, TT * ch + TT)
                sp.dma_start(scr["resid"][bass.ds(ch * CH, CH)].rearrange("(t p) n -> p t n", p=P),
                             xin[:]).then_inc(resid_stored, 16)

            def parts_store(dst, ready, count, slot):
                sp.wait_ge(ready, count)
                sp.nop(nofuse=True)
                sp.dma_start(dst, f32(parts[:, slot])).then_inc(q_stored[slot], 16)

            def chunk(ch, last):
                b, col = ch // 2, (ch % 2) * CH
                for t in range(L0_TILES):
                    rope_store(ch, t, b, col)
                    if t == 1 and not last:
                        sp.wait_ge(resid_stored, 16 * ch + 16)
                        sp.nop(nofuse=True)
                        sp.dma_start(xin[:], ins["x"][bass.ds((ch + 1) * CH, CH)].rearrange(
                            "(t p) n -> p t n", p=P)).then_inc(x_loaded, 16)
                    for n in xs_jobs(t):
                        if n % 2:
                            h_store(ch, n // 2)
                for t in range(L1_TILES):
                    plain_store(ch, t, b, col)
                    if t == 4 and not last:
                        residual_store(ch + 1)

            def rope_store(ch, t, b, col):
                s, m = (t // (NQ0 // 2), t % (NQ0 // 2)) if t < NQ0 else (t - NQ0, 0)
                dst = scr["q0"] if t < NQ0 else scr["k0"]
                rows = (NH0 if t < NQ0 else NKV) * D0
                parts_store(dst[bass.ds(b * rows + m * P, P), s, :, bass.ds(col, CH)],
                            rope_lo, ch * L0_TILES + t + 3, t % 2)

            def plain_store(ch, t, b, col):
                dst = scr["q1"] if t < L1_TILES // 2 else scr["k1"]
                parts_store(dst[bass.ds(b * H + (t % (L1_TILES // 2)) * P, P), :, bass.ds(col, CH)],
                            plain_lo, ch * L1_TILES + t + 1, t % 2)

            def h_store(ch, k):
                sp.wait_ge(split_done, first_job(ch, True) + 2 * k + 2 + 4)
                sp.nop(nofuse=True)
                sp.dma_start(scr["h"][:, :, k, bass.ds(ch * CH, CH)], f32(ht[:, k % 2])).then_inc(h_stored[k % 2], 16)

            residual_store(0)
            with sp.Fori(0, NCH - 1) as ch:
                chunk(ch, False)
            chunk(NCH - 1, True)
            sp.wait_ge(resid_stored, 16 * NCH)
            for n in range(2):
                sp.wait_ge(q_stored[n], 16 * NCH * TILES // 2 + 16)
                sp.wait_ge(h_stored[n], 16 * NCH * KT // 2 + 16)

        @block.tensor
        def _(pe):
            def turn(ch, xs):
                for k in range(KT):
                    if xs:
                        if k == 0:
                            pe.wait_ge(xs_ready, TT * ch + TT)
                        pe.wait_ge(y_ready, first_job(ch, False) + k + 1)
                    else:
                        if k == 0:
                            pe.wait_ge(xn_ready, TT * ch + TT)
                        if not (isinstance(ch, int) and ch == 0):
                            pe.wait_ge(y_ready, first_job(ch, False) - XS_JOBS + 2 * k + 2)
                    pe.nop(nofuse=True)
                    for t in range(TT):
                        mm = nc.tensor.transpose(tp[:, k, t * P:(t + 1) * P], xn[:, t, k * P:(k + 1) * P], ident[:])
                    mm.then_inc(turned, 1)

            def features(ch, u, w, col, xt):
                pe.wait_ge(proj_read, ch * UNITS + u + 1)
                pe.nop(nofuse=True)
                for k in range(KT):
                    for n, (a, c) in enumerate(PASSES):
                        mm = nc.tensor.matmul(pj[:, u % 2, :], w[:, a, k, col:col + P], xt[:, c, k, :],
                                              start=(k == 0 and n == 0), stop=(k == KT - 1 and n == 2))
                mm.then_inc(proj_done, 1)

            def values(ch, u, w, col, xt):
                pe.wait_ge(proj_read, ch * UNITS + u + 1)
                pe.nop(nofuse=True)
                for h in range(2):
                    t = 2 * (u % 2) + h
                    for k in range(KT):
                        for n, (a, c) in enumerate(PASSES):
                            mm = nc.tensor.matmul(pj[:, u % 2, h * 256:h * 256 + 256], xt[:, a, k, t * P:(t + 1) * P],
                                                  w[:, c, k, col:col + 256],
                                                  start=(k == 0 and n == 0), stop=(k == KT - 1 and n == 2))
                mm.then_inc(proj_done, 1)

            def chunk(ch, last):
                pe.wait_ge(split_done, first_job(ch, False) + XN_JOBS + 4)
                for t in range(L0_TILES):
                    features(ch, L0_FIRST + t, w0, t * P, xnt)
                    if t == 1:
                        turn(ch, True)
                for n in range(V_UNITS):
                    values(ch, L0_V + n, w0, N0 - 256, xnt)
                pe.wait_ge(split_done, first_job(ch, True) + XS_JOBS + 4)
                for t in range(L1_TILES):
                    features(ch, L1_FIRST + t, w1, t * P, x1t)
                    if t == 2 and not last:
                        turn(ch + 1, False)
                for n in range(V_UNITS):
                    values(ch, L1_V + n, wp, 0, x1t)

            turn(0, False)
            with pe.Fori(0, NCH - 1) as ch:
                chunk(ch, False)
            chunk(NCH - 1, True)

        @block.scalar
        def _(act):
            act.sem_inc(proj_read, 2)
            act.wait_ge(consts_loaded, 64)

            def layer_root(ch):
                act.wait_ge(inv_ready, 2 * ch + 1)
                act.nop(nofuse=True)
                nc.scalar.activation(root[:, 0], inv[:, 0], ACT.Sqrt).then_inc(root_ready, 1)

            def squares(ch):
                for t in range(TT):
                    act.wait_ge(xn_ready, TT * ch + t + 1)
                    act.nop(nofuse=True)
                    if t > 0:
                        act.wait_ge(squared, TT * ch + t)
                        act.nop(nofuse=True)
                    nc.scalar.activation(junk[:], xn[:, t], ACT.Square, accum_out=sq[:, t:t + 1]).then_inc(squared, 1)

            def rms_root(ch):
                act.wait_ge(inv_ready, 2 * ch + 2)
                act.nop(nofuse=True)
                nc.scalar.activation(root[:, 1], inv[:, 1], ACT.Sqrt).then_inc(root_ready, 1)

            def read_turned(ch, xs, n):
                k, w = (n // 2, n % 2) if xs else (n, 0)
                job = first_job(ch, xs) + n
                if w == 0:
                    act.wait_ge(turned, ch * 2 * KT + (KT if xs else 0) + k + 1)
                    act.nop(nofuse=True)
                act.wait_ge(split_done, job + 1)
                act.nop(nofuse=True)
                if xs and n % 2:
                    act.wait_ge(h_stored[k % 2], 32 * ch + 16 * (k // 2) + 16)
                    act.nop(nofuse=True)
                if not xs and n == 0 and not (isinstance(ch, int) and ch == 0):
                    act.wait_ge(proj_done, ch * UNITS - UNITS + L1_FIRST)
                    act.nop(nofuse=True)
                for dst in (y[:, n % 4], operand_tile(xs, n)[0]):
                    if xs:
                        cp = nc.scalar.activation(dst, tp[:, k], ACT.Copy, scale=(ln1, ln2)[w][:, k:k + 1])
                    else:
                        cp = nc.scalar.copy(dst, tp[:, k])
                cp.then_inc(y_ready, 1)

            def read_tile(ch, u, q):
                act.wait_ge(proj_done, ch * UNITS + u + 1)
                act.nop(nofuse=True)
                act.wait_ge(q_taken, ch * TILES + q + 1)
                act.nop(nofuse=True)
                nc.scalar.copy(qs[:, q % 2], pj[:, u % 2]).then_inc(proj_read, 1)

            def read_values(ch, u, heads, off, dst):
                act.wait_ge(proj_done, ch * UNITS + u + 1)
                act.nop(nofuse=True)
                b, half = ch // 2, ch % 2
                for h in range(2):
                    tb = half * TT + 2 * (u % 2) + h
                    src = pj[:, u % 2, h * 256 + off:h * 256 + off + heads * D0].rearrange("p (h d) -> p h d", d=D0)
                    cp = nc.scalar.copy(dst(b, tb), src)
                cp.then_inc(proj_read, 1)

            def v0_at(b, tb):
                return v0[:, bass.ds(b * (NKV * QB) + tb, NKV, QB), 0:D0]

            def v1_at(b, tb):
                return v1[:, bass.ds(b * (NH1 * QB) + tb, NH1, QB), 0:D0]

            def chunk(ch, last):
                for t in range(L0_TILES):
                    read_tile(ch, L0_FIRST + t, t)
                    for n in xs_jobs(t):
                        read_turned(ch, True, n)
                for n in range(V_UNITS):
                    read_values(ch, L0_V + n, NKV, P, v0_at)
                    if n == 0 and not last:
                        layer_root(ch + 1)
                for t in range(L1_TILES):
                    read_tile(ch, L1_FIRST + t, L0_TILES + t)
                    if not last:
                        if t == 0:
                            squares(ch + 1)
                        if t == 2:
                            rms_root(ch + 1)
                        if XN_AFTER <= t < XN_AFTER + XN_JOBS:
                            read_turned(ch + 1, False, t - XN_AFTER)
                for n in range(V_UNITS):
                    read_values(ch, L1_V + n, NH1, 0, v1_at)
                if not last:
                    rms_scale(ch + 1)

            def rms_scale(ch):
                act.wait_ge(turned, ch * 2 * KT + KT)
                act.nop(nofuse=True)
                act.wait_ge(resid_ready, TT * ch + TT)
                act.nop(nofuse=True)
                act.wait_ge(norm_step, NORM_STEPS * ch + NORM_STEPS)
                act.nop(nofuse=True)
                for t in range(TT):
                    nc.scalar.activation(xn[:, t], xn[:, t], ACT.Copy, scale=root[:, 1, t:t + 1]).then_inc(xs_ready, 1)

            layer_root(0)
            squares(0)
            rms_root(0)
            for n in range(XN_JOBS):
                read_turned(0, False, n)
            rms_scale(0)
            with act.Fori(0, NCH - 1) as ch:
                chunk(ch, False)
            chunk(NCH - 1, True)

        @block.vector
        def _(dve):
            nc.vector.memset(v0[:, :, D0:VW], 1.0).then_inc(ones_ready, 1)
            nc.vector.memset(v1[:, :, D0:VW], 1.0).then_inc(ones_ready, 1)
            dve.sem_inc(split_done, 4)
            dve.sem_inc(q_taken, 2)
            dve.sem_inc(rope_lo, 2)

            def step(ch, n, ins_):
                ins_.then_inc(norm_step, 1)
                dve.wait_ge(norm_step, NORM_STEPS * ch + n)
                dve.nop(nofuse=True)

            def inverse_root(ch, n, first):
                dve.wait_ge(root_ready, 2 * ch + n + 1)
                dve.nop(nofuse=True)
                step(ch, first, nc.vector.tensor_tensor(newt[:, n], root[:, n], root[:, n], ALU.mult))
                step(ch, first + 1, nc.vector.tensor_tensor(newt[:, n], newt[:, n], var[:, n], ALU.mult))
                step(ch, first + 2, nc.vector.tensor_scalar(newt[:, n], newt[:, n], -0.5, 1.5, ALU.mult, ALU.add))
                step(ch, first + 3, nc.vector.tensor_tensor(root[:, n], root[:, n], newt[:, n], ALU.mult))

            def layer_stats(ch):
                dve.wait_ge(x_loaded, 16 * ch + 16)
                dve.nop(nofuse=True)
                for t in range(TT):
                    bn = nc.vector.bn_stats(stats[:, t], xin[:, t])
                step(ch, 1, bn)
                for t in range(TT):
                    bn = nc.vector.bn_aggr(mv[:, t], stats[:, t])
                step(ch, 2, bn)
                step(ch, 3, nc.vector.tensor_scalar(var[:, 0], mv[:, :, 1], LN_EPS, None, ALU.add))
                nc.vector.reciprocal(inv[:, 0], var[:, 0]).then_inc(inv_ready, 1)

            def layer_norm(ch):
                inverse_root(ch, 0, 4)
                if not (isinstance(ch, int) and ch == 0):
                    dve.wait_ge(turned, ch * 2 * KT)
                    dve.nop(nofuse=True)
                for t in range(TT):
                    nc.vector.tensor_scalar(xn[:, t], xin[:, t], mv[:, t, 0:1], root[:, 0, t:t + 1],
                                            ALU.subtract, ALU.mult).then_inc(xn_ready, 1)

            def rms_stats(ch):
                dve.wait_ge(squared, TT * ch + TT)
                dve.nop(nofuse=True)
                step(ch, 8, nc.vector.tensor_scalar(var[:, 1], sq[:], 1.0 / H, RMS_EPS, ALU.mult, ALU.add))
                nc.vector.reciprocal(inv[:, 1], var[:, 1]).then_inc(inv_ready, 1)

            def rms_norm(ch):
                inverse_root(ch, 1, 9)

            def split_low(ch, xs, n):
                hi, lo = operand_tile(xs, n)
                dve.wait_ge(y_ready, first_job(ch, xs) + n + 1)
                dve.nop(nofuse=True)
                nc.vector.tensor_tensor(lo, y[:, n % 4], f32(hi), ALU.subtract).then_inc(split_done, 1)

            def rope_start(ch, t):
                s = t % 2
                dve.wait_ge(proj_read, ch * UNITS + t + 3)
                dve.nop(nofuse=True)
                dve.wait_ge(rope_lo, ch * L0_TILES + max(t - 2, 0) + 2)
                dve.nop(nofuse=True)
                nc.vector.tensor_tensor(qc[:, t % 3], qs[:, s], cos[:, bass.ds((ch % 2) * CH, CH)], ALU.mult).then_inc(cos_done, 1)
                nc.vector.stream_shuffle(qr[:, s], qs[:, s],
                                         [p // 16 * 16 + (p + 8) % 16 for p in range(32)]).then_inc(q_taken, 1)

            def rope_add(ch, t):
                s = t % 2
                n = ch * L0_TILES + t + 1
                dve.wait_ge(cos_done, n)
                dve.nop(nofuse=True)
                dve.wait_ge(sin_done, n)
                dve.nop(nofuse=True)
                nc.vector.tensor_tensor(qc[:, t % 3], qc[:, t % 3], qr[:, s], ALU.add).then_inc(rope_sum, 1)

            def rope_high(ch, t):
                s = t % 2
                dve.wait_ge(rope_sum, ch * L0_TILES + t + 1)
                dve.nop(nofuse=True)
                dve.wait_ge(q_stored[s], 16 * (ch * (TILES // 2) + t // 2 + 1))
                dve.nop(nofuse=True)
                nc.vector.tensor_copy(parts[:, s, HI], qc[:, t % 3]).then_inc(rope_hi, 1)

            def plain_high(ch, t):
                s = t % 2
                dve.wait_ge(proj_read, ch * UNITS + L1_FIRST + t + 3)
                dve.nop(nofuse=True)
                dve.wait_ge(q_stored[s], 16 * (ch * (TILES // 2) + L0_TILES // 2 + t // 2 + 1))
                dve.nop(nofuse=True)
                nc.vector.tensor_copy(parts[:, s, HI], qs[:, s]).then_inc(plain_hi, 1)

            def plain_low(ch, t):
                s = t % 2
                n = ch * L1_TILES + t + 1
                dve.wait_ge(plain_hi, n)
                dve.nop(nofuse=True)
                nc.vector.tensor_tensor(parts[:, s, LO], qs[:, s], f32(parts[:, s, HI]), ALU.subtract).then_inc(plain_lo, 1)
                dve.wait_ge(plain_lo, n)
                dve.sem_inc(q_taken, 1)

            def chunk(ch, last):
                for t in range(L0_TILES + 1):
                    if t < L0_TILES:
                        rope_start(ch, t)
                    if t:
                        rope_add(ch, t - 1)
                    n = t - XS_AFTER
                    if t:
                        rope_high(ch, t - 1)
                    if 0 <= n < XS_JOBS:
                        split_low(ch, True, n)
                if not last:
                    layer_stats(ch + 1)
                    layer_norm(ch + 1)
                for t in range(L1_TILES):
                    n = t - XN_AFTER
                    turning = not last and 0 <= n < XN_JOBS
                    plain_high(ch, t)
                    plain_low(ch, t)
                    if turning:
                        split_low(ch + 1, False, n)
                    if not last:
                        if t == 1:
                            rms_stats(ch + 1)
                        if t == 3:
                            rms_norm(ch + 1)

            dve.sem_inc(h_stored[0], 16)
            dve.sem_inc(h_stored[1], 16)
            dve.sem_inc(q_stored[0], 16)
            dve.sem_inc(q_stored[1], 16)
            layer_stats(0)
            layer_norm(0)
            rms_stats(0)
            rms_norm(0)
            for n in range(XN_JOBS):
                split_low(0, False, n)
            with dve.Fori(0, NCH - 1) as ch:
                chunk(ch, False)
            chunk(NCH - 1, True)

        @block.gpsimd
        def _(pool):
            pool.wait_ge(consts_loaded, 64)

            def residual(ch):
                for t in range(TT):
                    pool.wait_ge(xn_ready, TT * ch + t + 1)
                    pool.nop(nofuse=True)
                    nc.gpsimd.tensor_tensor(xin[:, t], xin[:, t], xn[:, t], ALU.add).then_inc(resid_ready, 1)

            def rope_sin(ch, t):
                s = t % 2
                pool.wait_ge(q_taken, ch * TILES + t + 3)
                pool.nop(nofuse=True)
                nc.gpsimd.tensor_tensor(qr[:, s], qr[:, s], sin[:, bass.ds((ch % 2) * CH, CH)], ALU.mult).then_inc(sin_done, 1)

            def rope_low(ch, t):
                s = t % 2
                pool.wait_ge(rope_hi, ch * L0_TILES + t + 1)
                pool.nop(nofuse=True)
                nc.gpsimd.tensor_tensor(parts[:, s, LO], qc[:, t % 3], f32(parts[:, s, HI]), ALU.subtract).then_inc(rope_lo, 1)

            def chunk(ch, last):
                for t in range(L0_TILES):
                    rope_sin(ch, t)
                    if t:
                        rope_low(ch, t - 1)
                rope_low(ch, L0_TILES - 1)
                if not last:
                    residual(ch + 1)

            residual(0)
            with pool.Fori(0, NCH - 1) as ch:
                chunk(ch, False)
            chunk(NCH - 1, True)


MAPS = 4
RING = 4
HALF = 512
PIECES = tuple(piece for i, keys in enumerate(range(P, S + P, P)) for piece in
               ([(i, 0, keys)] if keys <= HALF else
                [(i, 0, min(HALF, keys - 2 * P)), (i, min(HALF, keys - 2 * P), max(keys - HALF, 2 * P))]))
NP = len(PIECES)
ORDER = ((0, 3, 1, 2), (0, 6, 1, 2, 7, 3, 4, 5))
STEPS = tuple((c, j) for c in range(S // HALF) for j in ORDER[c])
NS = len(STEPS)
DIAGONAL = tuple(s for s, (c, j) in enumerate(STEPS) if P * j >= HALF * c)
TURNS = 3
PROBS = 3
EARLY = 28
LAG = 3
SECOND_MAX_ROW = len(PASSES) * D1
BANKS = 3
APART = 2000
FP32R_LEAST = 256
PARTS = MAPS + 1


def columns(s):
    c, j = STEPS[s]
    return HALF - max(0, P * j - HALF * c)


def piece_stream():
    work = [0]
    for k in range(NS):
        s, old = (k + LAG) % NS, (k + 1) % NS
        diagonal = P if s in DIAGONAL else 0
        work += [work[-1] + (m + 1) * (max(columns(s), FP32R_LEAST) + diagonal) for m in range(MAPS)]
        work[-1] += 2 * columns(old)
        work.append(work[-1] + 2 * columns(old))
    order = [(EARLY + n) % (MAPS * NP) for n in range(MAPS * NP)]
    maxima = [0]
    for n in order:
        maxima.append(maxima[-1] + 64 + PIECES[n % NP][2])
    return [sum(m * work[-1] < w * maxima[-1] for m in maxima[:-1]) if w else 0 for w in work]


STREAM = piece_stream()
COMPLETE = next(p for p in range(NS * PARTS) if STREAM[p + 1] >= MAPS * NP - EARLY)
ROWS_AT, ROWS_READ_AT = COMPLETE + 8, COMPLETE + 9
OUT0_AT, OUT1_AT = 4 * PARTS, NS * PARTS - 2


class Layer:

    def __init__(self, first_round, groups, d, combos, own_keys, scale, differential, q_scr, k_scr, v, out):
        self.first_round = first_round
        self.rounds = groups // RING
        self.d = d
        self.combos = combos
        self.kmaps = MAPS if own_keys else 1
        self.scale = scale
        self.differential = differential
        self.max_row = len(combos) * d
        self.loads = 2 * len(combos) + 1
        self.q_scr, self.k_scr, self.v, self.out = q_scr, k_scr, v, out


def attention_block(nc, layers, zero_rows, neg_lambda, ident):
    LAST = layers[1].first_round + layers[1].rounds - 1
    groups = (LAST + 1) * RING

    def layer_at(rnd):
        return layers[1] if isinstance(rnd, int) and rnd >= layers[1].first_round else layers[0]

    def loads_through(rnd):
        before = 16 * layers[0].loads * layers[1].first_round if layer_at(rnd) is layers[1] else 0
        return (rnd - layer_at(rnd).first_round) * (16 * layer_at(rnd).loads) + 16 * layer_at(rnd).loads + before

    def result_of(i, u):
        if layer_at(i) is layers[0]:
            return i * (RING // 2) + u // 2
        return layers[1].first_round * (RING // 2) + (i - layers[1].first_round) * RING + u

    with ExitStack() as ctx:
        def sb(name, shape, dt=F32):
            return ctx.enter_context(nc.sbuf_tensor(f"att_{name}", shape, dt))

        def sem(name):
            return ctx.enter_context(nc.semaphore(f"att_{name}"))

        def psum(name, shape):
            return ctx.enter_context(nc.psum_tensor(f"att_{name}", shape, F32))

        qst = sb("q_stack", [P, RING, MAPS, S], F32R)
        kst = sb("k_stack", [P, RING, MAPS, S], F32R)
        mask = sb("mask", [P, HALF + P])
        ident_b = sb("ident_b", [P, P], BF16)
        future = sb("future", [P, P], BF16)
        vst = sb("v_stack", [P, 2, MAPS, QB, 32])
        tops = sb("tops", [P, 2, MAPS, QB])
        pair = sb("pair", [P, 2, MAPS, QB // 2, 2])
        ntop = sb("neg_top", [P, 2, MAPS, QB])
        ntop_r = sb("neg_top_hi", [P, MAPS, QB], F32R)
        mrow = sb("max_rows", [P, P])
        probs = sb("probs", [P, PROBS, MAPS, HALF])
        osb = sb("out_t", [P, 2, HALF])
        rec = sb("recip", [P, 2, QB // 2 * MAPS])
        kept = sb("kept", [P, 2, QB // 2, MAPS * D0])
        prod = sb("prod", [P, QB // 2, MAPS * D0])
        result = sb("result", [P, 2, QB // 2, MAPS * D0])
        ps_s = psum("scores", [P, BANKS, HALF])
        ps_t = psum("scores_t", [P, BANKS, HALF])
        ps_o = psum("out", [P, HALF])
        ps_x = psum("turn", [P, HALF])

        loaded = [sem(f"loaded{u}") for u in range(RING)]
        q_pad = sem("q_pad")
        k_pad = sem("k_pad")
        k_ones = sem("k_ones")
        maps_pad = sem("maps_pad")
        mask_zero = sem("mask_zero")
        mask_ready = sem("mask_ready")
        v_zeroed = sem("v_zeroed")
        v_ready = sem("v_ready")
        scored = sem("scored")
        topped = sem("topped")
        top_step = sem("top_step")
        tops_split = sem("tops_split")
        turned = sem("turned")
        turn_read = sem("turn_read")
        rows_read = sem("rows_read")
        rows_set = sem("rows_set")
        scored_t = sem("scored_t")
        exped = sem("exped")
        future_ready = sem("future_ready")
        summed = sem("summed")
        out_read = sem("out_read")
        rec_done = sem("rec_done")
        prod_done = sem("prod_done")
        stored = [sem(f"stored{c}") for c in range(2)]
        divided = sem("divided")
        block = ctx.enter_context(nc.Block())

        UNITS_T = MAPS * NS
        PIECES_G = MAPS * NP

        def iterate(eng, body):
            with eng.Fori(0, layers[0].rounds - 1) as i:
                for u in range(RING):
                    body(i, u, RING)
            for i in range(layers[0].rounds - 1, LAST):
                for u in range(RING):
                    body(i, u, RING)
            for u in range(RING):
                body(LAST, u, RING - 1 - u)

        def after(i, u, n):
            return i * RING + (u + n), (u + n) % RING, i + (u + n) // RING

        def scored_step(i, u, k, ahead):
            if k + LAG < NS:
                return i, u, k + LAG
            return (*after(i, u, 1)[:0:-1], k + LAG - NS) if ahead else None

        def summed_step(i, u, k, ahead):
            if k + 1 < NS:
                return i, u, k + 1
            return (*after(i, u, 1)[:0:-1], 0) if ahead else None

        def pieces_of(p, ahead):
            first, last = EARLY + STREAM[p], EARLY + STREAM[p + 1]
            return (range(first, min(last, PIECES_G)) if ahead else (),
                    range(max(first - PIECES_G, 0), max(last - PIECES_G, 0)) if ahead > 1 else ())

        def prologue_pieces(n):
            bounds = [0] + [EARLY - (LAG * MAPS - k) * 14 // (LAG * MAPS) for k in range(LAG * MAPS + 1)]
            return range(bounds[n], bounds[n + 1])

        @block.sync
        def _(sp):
            def load(rnd, u, first_load=False):
                lay = layer_at(rnd)
                rows = MAPS * lay.d
                g = (rnd - lay.first_round) * RING + u
                pairs = rnd * (RING // 2) + u // 2
                for n, (a, c) in enumerate(lay.combos):
                    at = slice(n * lay.d, (n + 1) * lay.d)
                    if lay.differential:
                        q_src = lay.q_scr[bass.ds(pairs * rows, rows), u % 2, a, :]
                        k_src = lay.k_scr[bass.ds(pairs * lay.d, lay.d), u % 2, c, :]
                    else:
                        q_src = lay.q_scr[bass.ds(g * rows, rows), a, :]
                        k_src = lay.k_scr[bass.ds(g * rows, rows), c, :]
                    sp.dma_start(f32(qst[at, u]), q_src.rearrange("(m d) n -> d m n", m=MAPS)).then_inc(loaded[u], 16)
                    sp.dma_start(f32(kst[at, u, 0:lay.kmaps]), k_src.rearrange("(m d) n -> d m n", m=lay.kmaps)).then_inc(loaded[u], 16)
                if first_load:
                    sp.wait_ge(q_pad, u + 1)
                sp.dma_start(f32(qst[lay.max_row:lay.max_row + 2, u]), zero_rows).then_inc(loaded[u], 16)

            def set_rows(g, slot, lay):
                sp.wait_ge(rows_read, g + 1)
                sp.nop(nofuse=True)
                for a in range(2):
                    row = f32(qst[lay.max_row + a:lay.max_row + a + 1, slot])
                    sp.dma_start(row.rearrange("o m (i n) -> o (m i) n", n=P),
                                 mrow[a * 32:a * 32 + 32]).then_inc(rows_set, 16)

            def store(i, u, c):
                n, lay = result_of(i, u), layer_at(i)
                sp.wait_ge(divided, 2 * n + c + 1)
                sp.nop(nofuse=True)
                if lay.differential:
                    b = i // (NKV // (RING // 2))
                    dst = lay.out.rearrange("p t k e -> p (t k) e")[:, bass.ds(b * (QB * NKV - NKV) + n + c * (QB // 2 * NKV),
                                                                         QB // 2, NKV), :]
                else:
                    g = (i - lay.first_round) * RING + u
                    dst = lay.out[:, bass.ds(g * QB + c * (QB // 2), QB // 2), :]
                sp.dma_start(dst, result[:, c]).then_inc(stored[c], 16)

            def body(i, u, ahead):
                stores = u % 2 or not layer_at(i).differential
                if stores:
                    store(i, u, 0)
                if ahead:
                    g, slot, rnd = after(i, u, 1)
                    set_rows(g, slot, layer_at(rnd))
                if ahead == RING:
                    sp.wait_ge(scored_t, UNITS_T * (i * RING + u + 1))
                    sp.nop(nofuse=True)
                    load(i + 1, u)
                if stores:
                    store(i, u, 1)

            for u in range(RING):
                load(0, u, first_load=True)
            set_rows(0, 0, layers[0])
            iterate(sp, body)
            for c in range(2):
                sp.wait_ge(stored[c], 16 * result_of(LAST, RING - 1) + 32)

        @block.tensor
        def _(pe):
            pe.sem_inc(summed, PROBS)

            def pieces(i, u, n, ns, ones=None):
                g, slot, rnd = after(i, u, n)
                lay = layer_at(rnd)
                for n in ns:
                    m, (r, k0, keys) = n // NP, PIECES[n % NP]
                    if n == 0:
                        if ones is not None:
                            pe.wait_ge(k_ones, 2 * ones)
                        pe.wait_ge(loaded[slot], loads_through(rnd))
                        pe.nop(nofuse=True)
                    pe.wait_ge(topped, g * PIECES_G + n + 1)
                    pe.nop(nofuse=True)
                    width = max(keys, FP32R_LEAST)
                    nc.tensor.matmul(ps_s[:, n % BANKS, 0:width], qst[:, slot, m, r * P:(r + 1) * P],
                                     kst[:, slot, m % lay.kmaps, k0:k0 + width],
                                     start=True, stop=True).then_inc(scored, 1)

            def turn_rows(g, turn):
                pe.wait_ge(tops_split, g + 1)
                pe.nop(nofuse=True)
                if turn is not None:
                    pe.wait_ge(turn_read, turn)
                    pe.nop(nofuse=True)
                nc.tensor.transpose(ps_x[0:64, 0:P], ntop[:].rearrange("p a m i -> p (a m i)"), ident[:]).then_inc(turned, 1)

            def turn_out(g, c, turn):
                pe.wait_ge(out_read, 2 * g + c + 1)
                pe.nop(nofuse=True)
                pe.wait_ge(turn_read, turn)
                pe.nop(nofuse=True)
                for q in range(HALF // P):
                    mm = nc.tensor.transpose(ps_x[:, q * P:(q + 1) * P], osb[:, c, q * P:(q + 1) * P], ident[:])
                mm.then_inc(turned, 1)

            def scores_t(i, u, s, m):
                lay = layer_at(i)
                g = i * RING + u
                c, j = STEPS[s]
                n = MAPS * s + m
                if n == 0:
                    pe.wait_ge(rows_set, 32 * g + 32)
                    pe.nop(nofuse=True)
                start = HALF - max(columns(s), FP32R_LEAST)
                pe.wait_ge(exped, UNITS_T * g + n + 1 + APART)
                pe.nop(nofuse=True)
                mm = nc.tensor.matmul(ps_t[:, n % BANKS, start:HALF], kst[:, u, m % lay.kmaps, j * P:(j + 1) * P],
                                      qst[:, u, m, c * HALF + start:(c + 1) * HALF],
                                      start=True, stop=s not in DIAGONAL)
                if s in DIAGONAL:
                    lo = HALF - columns(s)
                    mm = nc.tensor.matmul(ps_t[:, n % BANKS, lo:lo + P], ident_b[:], future[:], start=False, stop=True)
                mm.then_inc(scored_t, 1)

            def pv(i, u, s, first=False):
                lay = layer_at(i)
                g = i * RING + u
                c, j = STEPS[s]
                lo = HALF - columns(s)
                pe.wait_ge(exped, UNITS_T * g + MAPS * (s + 1) + BANKS + APART)
                pe.nop(nofuse=True)
                if s == 0:
                    pe.wait_ge(v_ready, g + 1)
                    pe.nop(nofuse=True)
                if j == ORDER[c][0] and not first:
                    pe.wait_ge(out_read, 2 * g + c)
                    pe.nop(nofuse=True)
                for m in range(MAPS):
                    mm = nc.tensor.matmul(ps_o[32 * m:32 * m + 32, lo:HALF], vst[:, u % 2, m % lay.kmaps, j, :],
                                          probs[:, s % PROBS, m, lo:HALF],
                                          start=(j == ORDER[c][0]), stop=(j == ORDER[c][-1]))
                mm.then_inc(summed, 1)

            def body(i, u, ahead):
                g = i * RING + u
                for k in range(NS):
                    step, old = scored_step(i, u, k, ahead), summed_step(i, u, k, ahead)
                    for part in range(PARTS):
                        p = PARTS * k + part
                        if part < MAPS and step:
                            scores_t(*step, part)
                        if part == MAPS and old:
                            pv(*old)
                        for n, ns in enumerate(pieces_of(p, ahead)):
                            pieces(i, u, n + 1, ns)
                        if p == OUT0_AT:
                            turn_out(g, 0, TURNS * g + 1)
                        if p == ROWS_AT and ahead:
                            turn_rows(g + 1, TURNS * g + 2)
                        if p == OUT1_AT:
                            turn_out(g, 1, TURNS * g + (3 if ahead else 2))

            pe.wait_ge(future_ready, 2)
            pieces(0, 0, 0, range(PIECES_G), ones=1)
            turn_rows(0, None)
            pieces(0, 0, 1, prologue_pieces(0), ones=RING)
            for n in range(LAG * MAPS):
                scores_t(0, 0, n // MAPS, n % MAPS)
                pieces(0, 0, 1, prologue_pieces(n + 1))
            pv(0, 0, 0, first=True)
            iterate(pe, body)

        @block.scalar
        def _(act):
            act.sem_inc(exped, BANKS + APART)

            def exp(i, u, s):
                g = i * RING + u
                lo = HALF - columns(s)
                act.wait_ge(summed, NS * g + s + 1)
                act.nop(nofuse=True)
                for m in range(MAPS):
                    n = MAPS * s + m
                    act.wait_ge(scored_t, UNITS_T * g + n + 1)
                    act.nop(nofuse=True)
                    nc.scalar.activation(probs[:, s % PROBS, m, lo:HALF], ps_t[:, n % BANKS, lo:HALF],
                                         ACT.Exp, scale=layer_at(i).scale).then_inc(exped, 1)

            def read_out(g, c):
                last_step = max(s for s in range(NS) if STEPS[s][0] == c)
                act.wait_ge(summed, NS * g + last_step + 1 + PROBS)
                act.nop(nofuse=True)
                nc.scalar.copy(osb[:, c], ps_o[:]).then_inc(out_read, 1)

            def body(i, u, ahead):
                g = i * RING + u
                for k in range(NS):
                    if k == 3:
                        read_out(g, 0)
                    if k == NS - 1:
                        read_out(g, 1)
                    step = scored_step(i, u, k, ahead)
                    if step:
                        exp(*step)

            for s in range(LAG):
                exp(0, 0, s)
            iterate(act, body)

        @block.vector
        def _(dve):
            nc.vector.memset(f32(qst[layers[0].max_row:P, 0]), 0.0).then_inc(q_pad, 1)
            dve.sem_inc(stored[0], 16)
            dve.sem_inc(stored[1], 16)
            dve.sem_inc(topped, BANKS)
            dve.wait_ge(mask_ready, 1)

            def maxima(i, u, n, ns):
                g, slot, _ = after(i, u, n)
                par = (u + n) % 2
                for n in ns:
                    m, (r, k0, keys) = n // NP, PIECES[n % NP]
                    dve.wait_ge(scored, g * PIECES_G + n + 1)
                    dve.nop(nofuse=True)
                    diagonal = k0 + keys == P * (r + 1)
                    zeros = mask[:, HALF + P - keys:HALF + P] if diagonal else mask[:, 0:keys]
                    top = tops[:, par, m, r:r + 1] if r < QB // 2 else pair[:, par, m, r - QB // 2, int(k0 > 0):int(k0 > 0) + 1]
                    nc.vector.tensor_tensor_reduce(out=ps_s[:, n % BANKS, 0:keys], in0=ps_s[:, n % BANKS, 0:keys], in1=zeros,
                                                   scale=1.0, scalar=-3e38, op0=ALU.add, op1=ALU.max,
                                                   accum_out=top).then_inc(topped, 1)

            def split_tops(g, par, stage):
                if stage == 0:
                    dve.wait_ge(topped, g * PIECES_G + PIECES_G + BANKS)
                else:
                    dve.wait_ge(top_step, 3 * g + stage)
                dve.nop(nofuse=True)
                if stage == 0:
                    nc.vector.tensor_tensor(tops[:, par, :, QB // 2:QB], pair[:, par, :, :, 0], pair[:, par, :, :, 1],
                                            ALU.max).then_inc(top_step, 1)
                elif stage == 1:
                    nc.vector.tensor_scalar(ntop_r[:], tops[:, par], -1.0, None, ALU.mult).then_inc(top_step, 1)
                elif stage == 2:
                    nc.vector.tensor_copy(ntop[:, 0], f32(ntop_r[:])).then_inc(top_step, 1)
                else:
                    nc.vector.scalar_tensor_tensor(ntop[:, 1], tops[:, par], -1.0, f32(ntop_r[:]), ALU.mult,
                                                   ALU.subtract).then_inc(tops_split, 1)

            def read_rows(g, turn, first=False):
                dve.wait_ge(turned, turn + 1)
                dve.nop(nofuse=True)
                if not first:
                    dve.wait_ge(rows_set, 32 * g)
                    dve.nop(nofuse=True)
                nc.vector.tensor_copy(mrow[0:64], ps_x[0:64, 0:P]).then_inc(rows_read, 1)
                dve.wait_ge(rows_read, g + 1)
                dve.sem_inc(turn_read, 1)

            def divide(i, u, c, turn, stage):
                n = 2 * (i * RING + u) + c
                differential = layer_at(i).differential
                x = ps_x[:].rearrange("p (q e) -> p q e", e=32)
                over = rec[:, c].rearrange("p (q o) -> p q o", o=1).broadcast_to([P, HALF // 32, D0])

                def cols(t):
                    return t.rearrange("p b (m d) -> p (b m) d", d=D0)

                if stage == 0:
                    dve.wait_ge(turned, turn + 1)
                    dve.nop(nofuse=True)
                    nc.vector.reciprocal(rec[:, c], x[:, :, D0]).then_inc(rec_done, 1)
                elif stage == 1:
                    dve.wait_ge(rec_done, n + 1)
                    dve.nop(nofuse=True)
                    if not differential or u % 2:
                        dve.wait_ge(stored[c], 16 * result_of(i, u) + 16)
                        dve.nop(nofuse=True)
                    part = result[:, c] if not differential else prod[:] if u % 2 else kept[:, c]
                    nc.vector.tensor_tensor(cols(part), x[:, :, 0:D0], over, ALU.mult).then_inc(turn_read, 1)
                elif not differential:
                    dve.wait_ge(turn_read, turn + 1)
                    dve.sem_inc(divided, 1)
                elif u % 2:
                    dve.wait_ge(turn_read, turn + 1)
                    dve.nop(nofuse=True)
                    nc.vector.scalar_tensor_tensor(result[:, c], prod[:], neg_lambda[:], kept[:, c], ALU.mult,
                                                   ALU.add).then_inc(divided, 1)

            def body(i, u, ahead):
                g = i * RING + u
                g1 = after(i, u, 1)[0]
                for p in range(NS * PARTS):
                    if ahead and 0 <= p - COMPLETE - 1 < 4:
                        split_tops(g1, (u + 1) % 2, p - COMPLETE - 1)
                    if 0 <= p - OUT0_AT - 1 < 3:
                        divide(i, u, 0, TURNS * g + 1, p - OUT0_AT - 1)
                    if p == ROWS_READ_AT and ahead:
                        read_rows(g1, TURNS * g + 2)
                    if p == NS * PARTS - 1:
                        divide(i, u, 1, TURNS * g + (3 if ahead else 2), 0)
                    for n, ns in enumerate(pieces_of(p, ahead)):
                        maxima(i, u, n + 1, ns)
                for stage in (1, 2):
                    divide(i, u, 1, TURNS * g + (3 if ahead else 2), stage)

            maxima(0, 0, 0, range(PIECES_G))
            for stage in range(4):
                split_tops(0, 0, stage)
            read_rows(0, 0, first=True)
            maxima(0, 0, 1, range(EARLY))
            iterate(dve, body)
            dve.wait_ge(turn_read, TURNS * groups)

        @block.gpsimd
        def _(pool):
            max_row = layers[0].max_row

            def set_slot(n):
                nc.gpsimd.memset(f32(kst[max_row:P, n, 0]), 0.0).then_inc(k_pad, 1)
                pool.wait_ge(k_pad, n + 1)
                nc.gpsimd.memset(f32(kst[max_row:max_row + 2, n, 0]), 1.0).then_inc(k_ones, 1)
                pool.wait_ge(k_ones, 2 * n + 1)
                nc.gpsimd.memset(f32(kst[SECOND_MAX_ROW:SECOND_MAX_ROW + 2, n, 0]), 1.0).then_inc(k_ones, 1)
                pool.wait_ge(k_ones, 2 * n + 2)
                if n:
                    pool.wait_ge(q_pad, n)
                    nc.gpsimd.memset(f32(qst[max_row:P, n]), 0.0).then_inc(q_pad, 1)
                    pool.wait_ge(q_pad, n + 1)

            set_slot(0)
            nc.gpsimd.memset(mask[:], 0.0).then_inc(mask_zero, 1)
            nc.gpsimd.memset(future[:], 0.0).then_inc(mask_zero, 1)
            nc.gpsimd.tensor_copy(ident_b[:], ident[:]).then_inc(future_ready, 1)
            pool.wait_ge(mask_zero, 2)
            nc.gpsimd.affine_select(out=mask[:, HALF:], in_=mask[:, HALF:], compare_op=ALU.is_ge, fill=NEG,
                                    base=0, pattern=[[-1, P]], channel_multiplier=1).then_inc(mask_ready, 1)
            nc.gpsimd.affine_select(out=future[:], in_=future[:], compare_op=ALU.is_ge, fill=NEG,
                                    base=0, pattern=[[1, P]], channel_multiplier=-1).then_inc(future_ready, 1)
            nc.gpsimd.memset(vst[:], 0.0).then_inc(v_zeroed, 1)
            pool.wait_ge(v_zeroed, 1)
            pool.wait_ge(future_ready, 2)
            pool.wait_ge(mask_ready, 1)
            set_slot(1)

            def copy_values(i, u, n):
                g, slot, rnd = after(i, u, n)
                lay = layer_at(rnd)
                blocks = lay.kmaps * QB
                at = (i * (RING // 2) + (u + n) // 2) * QB if lay.differential else (g - lay.first_round * RING) * blocks
                pool.nop(nofuse=True)
                nc.gpsimd.tensor_copy(vst[:, (u + n) % 2, 0:lay.kmaps, :, 0:VW].rearrange("p m k e -> p (m k) e"),
                                      lay.v[:, bass.ds(at, blocks), :]).then_inc(v_ready, 1)

            def body(i, u, ahead):
                g = i * RING + u
                if ahead:
                    pool.wait_ge(summed, NS * g + PROBS)
                    copy_values(i, u, 1)

            copy_values(0, 0, 0)
            pool.wait_ge(v_ready, 1)
            for n in range(2, RING):
                set_slot(n)
            for n in range(RING):
                nc.gpsimd.memset(f32(kst[SECOND_MAX_ROW:P, n, 1:MAPS]), 0.0).then_inc(maps_pad, 1)
            pool.wait_ge(maps_pad, RING)
            for n in range(RING):
                nc.gpsimd.memset(f32(kst[SECOND_MAX_ROW:SECOND_MAX_ROW + 2, n, 1:MAPS]), 1.0).then_inc(maps_pad, 1)
            pool.wait_ge(maps_pad, 2 * RING)
            iterate(pool, body)


FG = 256
NFG = F // FG
FT = FG // P


def mlp_weights_load(sp, ins, raw_in, raw_down, raw_loaded, g):
    cols = bass.ds(g * FG, FG)
    for n, src in enumerate((ins["win_t"], ins["wup_t"])):
        sp.dma_start(raw_in[:, n], src.rearrange("(k p) f -> p k f", p=P)[:, :, cols]).then_inc(raw_loaded, 16)
    sp.dma_start(raw_down[:], ins["wdown_t"][cols].rearrange("(t p) n -> p t n", p=P)).then_inc(raw_loaded, 16)


RR = 4 * RK


def modulate_block(nc, ins, ahead, mod, bst, ident, raw_in, raw_down, raw_loaded):
    with ExitStack() as ctx:
        def sb(name, shape, dt=F32):
            return ctx.enter_context(nc.sbuf_tensor(name, shape, dt))

        def sem(name):
            return ctx.enter_context(nc.semaphore(name))

        def psum(name, shape):
            return ctx.enter_context(nc.psum_tensor(name, shape, F32))

        groups = B * NH1 // MAPS
        heads_a, a_raw, ht = head_rows(ahead["rows"]), ahead["a_raw"], ahead["ht"]
        heads_loaded, a_loaded, h_loaded = ahead["heads_loaded"], ahead["a_loaded"], ahead["h_loaded"]
        a_wide = sb("a_wide", [P, 2, KT, P], F32R)
        b_raw = sb("b_raw", [RK, F])
        b_hi = sb("b_hi", [RK, F], F32R)
        part_sum = sb("part_sum", [P, groups * QB, RK])
        asum = sb("asum", [P, TOK // P, 4, RK])
        m32 = sb("mod32", [RR, TOK])
        ps_t = psum("ps_turn", [P, 4, CH])
        ps_h = psum("ps_ha", [P, NCH, CH])

        b_loaded = sem("b_loaded")
        a_zeroed = sem("a_zeroed")
        mod_zeroed = sem("mod_zeroed")
        a_hi = sem("a_hi")
        a_ready = sem("a_ready")
        bh_ready = sem("bh_ready")
        bl_ready = sem("bl_ready")
        b_placed = sem("b_placed")
        heads_sum = sem("heads_sum")
        sum_ready = sem("sum_ready")
        sum_turned = sem("sum_turned")
        tanh_ready = sem("tanh_ready")
        ha_ready = sem("ha_ready")
        ha_read = sem("ha_read")
        mod_hi = sem("mod_hi")
        mod_lo = sem("mod_lo_ready")
        mod_ready = sem("mod_ready")
        block = ctx.enter_context(nc.Block())

        @block.sync
        def _(sp):
            sp.dma_start(b_raw[:], ins["b"]).then_inc(b_loaded, 16)
            mlp_weights_load(sp, ins, raw_in, raw_down, raw_loaded, 0)
            sp.wait_ge(mod_zeroed, 2)
            sp.wait_ge(bh_ready, 1)
            sp.wait_ge(bl_ready, 1)
            for n in range(4):
                sp.dma_start(f32(bst[n * RK:(n + 1) * RK]), (f32(b_hi[:]), b_raw[:])[n % 2]).then_inc(b_placed, 16)
            sp.wait_ge(b_placed, 64)

        @block.gpsimd
        def _(pool):
            nc.gpsimd.memset(f32(a_wide[:]), 0.0).then_inc(a_zeroed, 1)
            nc.gpsimd.memset(f32(bst[:]), 0.0).then_inc(mod_zeroed, 1)
            nc.gpsimd.memset(f32(mod[:]), 0.0).then_inc(mod_zeroed, 1)
            pool.wait_ge(mod_zeroed, 2)

        @block.tensor
        def _(pe):
            pe.wait_ge(a_ready, 4)
            pe.wait_ge(h_loaded, 32)
            for c in range(NCH):
                for k in range(KT):
                    for n, (a, x) in enumerate(PASSES):
                        mm = nc.tensor.matmul(ps_h[:, c], a_wide[:, a, k, :], ht[:, x, k, c * CH:(c + 1) * CH],
                                              start=(k == 0 and n == 0), stop=(k == KT - 1 and n == 2))
                mm.then_inc(ha_ready, 1)
            pe.wait_ge(sum_ready, 4)
            for t in range(TOK // P):
                mm = nc.tensor.transpose(ps_t[0:RR, t // TT, t % TT * P:(t % TT + 1) * P],
                                         asum[:, t].rearrange("p n r -> p (n r)"), ident[:])
            mm.then_inc(sum_turned, 1)

        @block.scalar
        def _(act):
            act.wait_ge(a_loaded, 16)
            act.wait_ge(a_zeroed, 1)
            for n in range(4):
                nc.scalar.copy(a_wide[:, HI, :, n * RK:(n + 1) * RK], a_raw[:]).then_inc(a_hi, 1)
            act.wait_ge(b_loaded, 16)
            nc.scalar.copy(b_hi[:], b_raw[:]).then_inc(bh_ready, 1)
            act.wait_ge(sum_turned, 1)
            nc.scalar.activation(m32[:], ps_t[0:RR].rearrange("p c n -> p (c n)"), ACT.Tanh).then_inc(tanh_ready, 1)

        @block.vector
        def _(dve):
            for n in range(4):
                dve.wait_ge(a_hi, n + 1)
                cols = slice(n * RK, (n + 1) * RK)
                nc.vector.tensor_tensor(a_wide[:, LO, :, cols], a_raw[:], f32(a_wide[:, HI, :, cols]),
                                        ALU.subtract).then_inc(a_ready, 1)
            dve.wait_ge(heads_loaded, 16)
            nc.vector.tensor_reduce(part_sum[:], heads_a.rearrange("p n (m r) -> p n r m", m=MAPS),
                                    AX.X, ALU.add).then_inc(heads_sum, 1)
            dve.wait_ge(heads_sum, 1)
            for n in range(4):
                for b in range(B):
                    src = part_sum[:, b * groups // B * QB:(b + 1) * groups // B * QB, :]
                    red = nc.vector.tensor_reduce(asum[:, b * QB:(b + 1) * QB, n, :],
                                                  src.rearrange("p (g q) r -> p q r g", q=QB), AX.X, ALU.add)
                red.then_inc(sum_ready, 1)
            dve.wait_ge(bh_ready, 1)
            nc.vector.tensor_tensor(b_raw[:], b_raw[:], f32(b_hi[:]), ALU.subtract).then_inc(bl_ready, 1)
            dve.wait_ge(tanh_ready, 1)
            dve.wait_ge(mod_zeroed, 2)
            for c in range(NCH):
                dve.wait_ge(ha_ready, c + 1)
                cols = slice(c * CH, (c + 1) * CH)
                nc.vector.scalar_tensor_tensor(m32[:, cols], m32[:, cols], MOD_SCALE, ps_h[0:RR, c], ALU.mult,
                                               ALU.mult).then_inc(ha_read, 1)
                dve.wait_ge(ha_read, c + 1)
                nc.vector.tensor_copy(mod[0:RR, cols], m32[:, cols]).then_inc(mod_hi, 1)
            dve.wait_ge(mod_hi, NCH)
            low = slice(RR // 2, RR)
            nc.vector.tensor_tensor(m32[low], m32[low], f32(mod[low]), ALU.subtract).then_inc(mod_lo, 1)
            dve.wait_ge(mod_lo, 1)
            nc.vector.tensor_copy(mod[low], m32[low]).then_inc(mod_ready, 1)
            dve.wait_ge(mod_ready, 1)


def head_rows(rows):
    return rows[:, 0:TOK // P // 2].rearrange("p t (g e) -> p (t g) e", e=MAPS * RK)


def output_block(nc, ins, scr, acc, ident, ahead, raw_in):
    with ExitStack() as ctx:
        def sb(name, shape, dt=F32):
            return ctx.enter_context(nc.sbuf_tensor(name, shape, dt))

        def sem(name):
            return ctx.enter_context(nc.semaphore(name))

        def psum(name, shape):
            return ctx.enter_context(nc.psum_tensor(name, shape, F32))

        attn = ahead["rows"]
        wo_raw = raw_in[:].rearrange("p w k f -> p (w k f)").rearrange("p (k n) -> p k n", k=KT)
        wo = sb("wo0", [P, 2, KT, H], F32R)
        apart = sb("attn_parts", [P, 2, 2, KT, CH], F32R)
        ps_t = psum("ps_turn0", [P, KT, CH])
        ps_y = psum("ps_y", [P, 4, CH])

        wo_loaded = sem("wo_loaded")
        attn_loaded = [sem(f"attn_loaded{c}") for c in range(NCH)]
        acc_loaded = sem("acc_loaded")
        wo_hi = sem("wo_hi")
        wo_ready = sem("wo_ready")
        at_turned = sem("at_turned")
        at_hi = sem("at_hi")
        at_split = sem("at_split")
        y_ready = sem("y0_ready")
        y_added = sem("y0_added")
        block = ctx.enter_context(nc.Block())

        @block.sync
        def _(sp):
            for c in range(NCH):
                sp.dma_start(attn[:, c * TT:(c + 1) * TT], scr["attn"][:, c * TT:(c + 1) * TT].rearrange(
                    "p t k e -> p t (k e)")).then_inc(attn_loaded[c], 16)
                if c == 0:
                    sp.dma_start(wo_raw, ins["wo0t"].rearrange("(k p) n -> p k n", p=P)).then_inc(wo_loaded, 16)
            sp.dma_start(acc[:], scr["resid"].rearrange("(t p) n -> p t n", p=P)).then_inc(acc_loaded, 16)
            sp.dma_start(ahead["a_raw"][:], ins["a"].rearrange("(k p) n -> p k n", p=P)).then_inc(ahead["a_loaded"], 16)
            for n in range(2):
                sp.dma_start(f32(ahead["ht"][:, n]), scr["h"][:, n]).then_inc(ahead["h_loaded"], 16)
            sp.wait_ge(at_turned, 2 * KT)
            sp.dma_start(head_rows(ahead["rows"]), scr["heads"]).then_inc(ahead["heads_loaded"], 16)
            sp.wait_ge(acc_loaded, 16)

        @block.tensor
        def _(pe):
            def turn(c):
                pe.wait_ge(attn_loaded[c], 16)
                for k in range(KT):
                    if c:
                        pe.wait_ge(at_split, (c - 1) * KT + k + 1)
                    for t in range(TT):
                        mm = nc.tensor.transpose(ps_t[:, k, t * P:(t + 1) * P], attn[:, c * TT + t, k * P:(k + 1) * P],
                                                 ident[:])
                    mm.then_inc(at_turned, 1)

            turn(0)
            pe.wait_ge(wo_ready, 1)
            for c in range(NCH):
                if c + 1 < NCH:
                    turn(c + 1)
                pe.wait_ge(at_split, (c + 1) * KT)
                for t in range(TT):
                    n = c * TT + t
                    if n >= 4:
                        pe.wait_ge(y_added, n - 3)
                    for k in range(KT):
                        for q, (a, x) in enumerate(PASSES):
                            mm = nc.tensor.matmul(ps_y[:, n % 4], apart[:, c % 2, a, k, t * P:(t + 1) * P], wo[:, x, k, :],
                                                  start=(k == 0 and q == 0), stop=(k == KT - 1 and q == 2))
                    mm.then_inc(y_ready, 1)

        @block.scalar
        def _(act):
            act.wait_ge(wo_loaded, 16)
            nc.scalar.copy(wo[:, HI], wo_raw).then_inc(wo_hi, 1)
            for n in range(NCH * KT):
                act.wait_ge(at_turned, n + 1)
                c, k = divmod(n, KT)
                if c >= 2 and k == 0:
                    act.wait_ge(y_ready, (c - 1) * TT)
                nc.scalar.copy(apart[:, c % 2, HI, k], ps_t[:, k]).then_inc(at_hi, 1)

        @block.vector
        def _(dve):
            dve.wait_ge(wo_hi, 1)
            nc.vector.tensor_tensor(wo[:, LO], wo_raw, f32(wo[:, HI]), ALU.subtract).then_inc(wo_ready, 1)

            def split(c):
                for k in range(KT):
                    n = c * KT + k
                    dve.wait_ge(at_hi, n + 1)
                    nc.vector.tensor_tensor(apart[:, c % 2, LO, k], ps_t[:, k], f32(apart[:, c % 2, HI, k]),
                                            ALU.subtract).then_inc(at_split, 1)

            split(0)
            dve.wait_ge(acc_loaded, 16)
            for c in range(NCH):
                if c + 1 < NCH:
                    split(c + 1)
                for t in range(TT):
                    n = c * TT + t
                    dve.wait_ge(y_ready, n + 1)
                    nc.vector.scalar_tensor_tensor(acc[:, n], ps_y[:, n % 4], 1.0 - LAMBDA_INIT, acc[:, n], ALU.mult,
                                                   ALU.add).then_inc(y_added, 1)
            dve.wait_ge(y_added, NCH * TT)


def mlp_block(nc, ins, out, ht, acc, mod, bst, raw_in, raw_down, raw_loaded):
    with ExitStack() as ctx:
        def sb(name, shape, dt=F32):
            return ctx.enter_context(nc.sbuf_tensor(name, shape, dt))

        def sem(name):
            return ctx.enter_context(nc.semaphore(name))

        def psum(name, shape):
            return ctx.enter_context(nc.psum_tensor(name, shape, F32))

        win = sb("win", [P, 2, 2, 2, KT, FG], F32R)
        wdown = sb("wdown", [P, 2, 2, FT, H], F32R)
        bgrp = sb("b_group", [P, 2, FG], F32R)
        th = sb("gate_tanh", [P, 2, CH])
        gate = sb("gate", [P, 2, CH])
        gu = sb("gate_up", [P, 2, CH])
        gp = sb("gate_up_parts", [P, 2, 2, FT, CH], F32R)
        ps_g = psum("ps_gate_up", [P, FT, 2, CH])
        ps_y = psum("ps_down", [P, TT, CH])

        raw_hi = sem("mlp_raw_hi")
        raw_split = sem("mlp_raw_split")
        b_copied = sem("b_copied")
        gate_ready = sem("gate_ready")
        gate_tanh = sem("gate_tanh_ready")
        gate_step = sem("gate_step")
        gate_done = sem("gate_done")
        gp_hi = sem("gp_hi")
        gp_ready = sem("gp_ready")
        down_ready = sem("down_ready")
        down_added = sem("down_added")
        stored = sem("stored")
        block = ctx.enter_context(nc.Block())

        def groups(eng, body):
            with eng.Fori(0, NFG // 2 - 1) as i:
                for slot in range(2):
                    body(i, slot, True)
            for slot in range(2):
                body(NFG // 2 - 1, slot, slot == 0)

        @block.sync
        def _(sp):
            def body(i, slot, more):
                if more:
                    sp.wait_ge(raw_split, 2 * (2 * i + slot) + 2)
                    sp.nop(nofuse=True)
                    mlp_weights_load(sp, ins, raw_in, raw_down, raw_loaded, 2 * i + slot + 1)

            groups(sp, body)
            for c in range(NCH):
                sp.wait_ge(down_added, (NFG - 1) * NCH * TT + (c + 2) * TT)
                sp.dma_start(out[c * CH:(c + 1) * CH].rearrange("(t p) n -> p t n", p=P),
                             acc[:, c * TT:(c + 1) * TT]).then_inc(stored, 16)
            sp.wait_ge(stored, 16 * NCH)

        @block.tensor
        def _(pe):
            def gates(i, slot, c):
                g = 2 * i + slot
                if c == 0:
                    pe.wait_ge(raw_split, 2 * g + 1)
                    pe.nop(nofuse=True)
                    pe.wait_ge(b_copied, g + 1)
                    pe.nop(nofuse=True)
                cols = slice(c * CH, (c + 1) * CH)
                for f in range(FT):
                    pe.wait_ge(gate_done, (g * NCH + c) * FT + f + 1)
                    pe.nop(nofuse=True)
                    at = slice(f * P, (f + 1) * P)
                    for w in range(2):
                        for k in range(KT):
                            for n, (a, x) in enumerate(PASSES):
                                last = k == KT - 1 and n == 2
                                mm = nc.tensor.matmul(ps_g[:, f, w], win[:, slot, a, w, k, at], ht[:, x, k, cols],
                                                      start=(k == 0 and n == 0), stop=last and w == 1)
                        if w == 0:
                            nc.tensor.matmul(ps_g[:, f, w], bgrp[:, slot, at], mod[:, cols], start=False, stop=True)
                    mm.then_inc(gate_ready, 1)

            def downs(i, slot, c):
                g = 2 * i + slot
                if c == 0:
                    pe.wait_ge(raw_split, 2 * g + 2)
                    pe.nop(nofuse=True)
                pe.wait_ge(gp_ready, (g * NCH + c + 1) * FT + 2)
                pe.nop(nofuse=True)
                for t in range(TT):
                    pe.wait_ge(down_added, (g * NCH + c) * TT + t + 1)
                    pe.nop(nofuse=True)
                    for f in range(FT):
                        for n, (a, x) in enumerate(PASSES):
                            mm = nc.tensor.matmul(ps_y[:, t], gp[:, c % 2, a, f, t * P:(t + 1) * P], wdown[:, slot, x, f, :],
                                                  start=(f == 0 and n == 0), stop=(f == FT - 1 and n == 2))
                    mm.then_inc(down_ready, 1)

            def body(i, slot, more):
                for c in range(NCH):
                    if c < NCH - 1:
                        gates(i, slot, c + 1)
                    elif more:
                        gates(i + slot, 1 - slot, 0)
                    downs(i, slot, c)

            gates(0, 0, 0)
            groups(pe, body)

        @block.scalar
        def _(act):
            def split_hi(i, slot, lead=False):
                g = 2 * i + slot
                act.wait_ge(raw_loaded, 48 * g + 48)
                act.nop(nofuse=True)
                if not lead:
                    act.wait_ge(down_added, (g - 1) * (NCH * TT) + TT)
                act.nop(nofuse=True)
                nc.scalar.copy(win[:, slot, HI], raw_in[:]).then_inc(raw_hi, 1)
                nc.scalar.copy(wdown[:, slot, HI], raw_down[:]).then_inc(raw_hi, 1)
                nc.scalar.copy(bgrp[:, slot], f32(bst[:, bass.ds(g * FG, FG)])).then_inc(b_copied, 1)

            def tanh(i, slot, c, f):
                n = ((2 * i + slot) * NCH + c) * FT + f
                act.wait_ge(gate_ready, n + 1)
                act.nop(nofuse=True)
                act.wait_ge(gate_step, n + 1)
                act.nop(nofuse=True)
                nc.scalar.activation(th[:, f], ps_g[:, f, 0], ACT.Tanh, scale=0.5).then_inc(gate_tanh, 1)

            def body(i, slot, more):
                for c in range(NCH):
                    for f in range(FT):
                        tanh(i, slot, c, f)
                    if c == 1 and more:
                        split_hi(i + slot, 1 - slot)

            split_hi(0, 0, lead=True)
            groups(act, body)

        @block.vector
        def _(dve):
            dve.sem_inc(gate_done, FT)
            dve.sem_inc(gate_step, 2)
            dve.sem_inc(down_added, TT)

            def split_lo(i, slot):
                g = 2 * i + slot
                dve.wait_ge(raw_hi, 2 * g + 2)
                dve.nop(nofuse=True)
                nc.vector.tensor_tensor(win[:, slot, LO], raw_in[:], f32(win[:, slot, HI]), ALU.subtract).then_inc(raw_split, 1)
                nc.vector.tensor_tensor(wdown[:, slot, LO], raw_down[:], f32(wdown[:, slot, HI]),
                                        ALU.subtract).then_inc(raw_split, 1)

            def act_gate(i, slot, c, f):
                n = ((2 * i + slot) * NCH + c) * FT + f
                dve.wait_ge(gate_tanh, n + 1)
                dve.nop(nofuse=True)
                nc.vector.scalar_tensor_tensor(gate[:, f], th[:, f], 1.0, ps_g[:, f, 0], ALU.add, ALU.mult).then_inc(gate_step, 1)
                dve.wait_ge(gate_step, n + 3)
                dve.nop(nofuse=True)
                dve.wait_ge(gp_ready, n + 1)
                dve.nop(nofuse=True)
                nc.vector.scalar_tensor_tensor(gu[:, f], gate[:, f], 0.5, ps_g[:, f, 1], ALU.mult, ALU.mult).then_inc(gate_done, 1)
                dve.wait_ge(gate_done, n + 1 + FT)
                dve.nop(nofuse=True)
                nc.vector.tensor_copy(gp[:, c % 2, HI, f], gu[:, f]).then_inc(gp_hi, 1)

            def add(i, slot, c):
                for t in range(TT):
                    n = ((2 * i + slot) * NCH + c) * TT + t
                    dve.wait_ge(down_ready, n + 1)
                    dve.nop(nofuse=True)
                    nc.vector.tensor_tensor(acc[:, c * TT + t], acc[:, c * TT + t], ps_y[:, t], ALU.add).then_inc(down_added, 1)

            def body(i, slot, more):
                for c in range(NCH):
                    if c < NCH - 1:
                        for f in range(FT):
                            act_gate(i, slot, c + 1, f)
                    elif more:
                        for f in range(FT):
                            act_gate(i + slot, 1 - slot, 0, f)
                    add(i, slot, c)
                    if c == 1 and more:
                        split_lo(i + slot, 1 - slot)

            split_lo(0, 0)
            for f in range(FT):
                act_gate(0, 0, 0, f)
            groups(dve, body)

        @block.gpsimd
        def _(pool):
            pool.sem_inc(gp_ready, 2)

            def low(i, slot, c, f):
                n = ((2 * i + slot) * NCH + c) * FT + f
                pool.wait_ge(gp_hi, n + 1)
                pool.nop(nofuse=True)
                nc.gpsimd.tensor_tensor(gp[:, c % 2, LO, f], gu[:, f], f32(gp[:, c % 2, HI, f]), ALU.subtract).then_inc(gp_ready, 1)

            def body(i, slot, more):
                for c in range(NCH):
                    for f in range(FT):
                        low(i, slot, c, f)

            groups(pool, body)


def lambda_block(nc, ins, neg_lambda, zeros_dram):
    with ExitStack() as ctx:
        def sb(name, shape, dt=F32):
            return ctx.enter_context(nc.sbuf_tensor(name, shape, dt))

        def sem(name):
            return ctx.enter_context(nc.semaphore(name))

        vec = sb("lambda_vectors", [P, 4, D0])
        prod = sb("lambda_products", [P, 2, D0])
        dot = sb("lambda_dots", [P, 2])
        e = sb("lambda_exps", [P, 2])
        diff = sb("lambda_diff", [P, 1])
        zeros = sb("zero_rows", [2, MAPS, S])
        zeroed = sem("zero_rows_set")
        zeros_stored = sem("zeros_stored")
        loaded = sem("lambda_loaded")
        step = sem("lambda_step")
        exp_done = sem("lambda_exp")
        block = ctx.enter_context(nc.Block())

        @block.sync
        def _(sp):
            for n, name in enumerate(("lq1", "lk1", "lq2", "lk2")):
                src = ins[name].rearrange("(o d) -> o d", o=1).broadcast_to([P, D0])
                sp.dma_start(vec[:, n], src).then_inc(loaded, 16)
            sp.wait_ge(zeroed, 1)
            sp.dma_start(zeros_dram, zeros[:]).then_inc(zeros_stored, 16)
            sp.wait_ge(zeros_stored, 16)

        @block.gpsimd
        def _(pool):
            nc.gpsimd.memset(zeros[:], 0.0).then_inc(zeroed, 1)

        @block.vector
        def _(dve):
            dve.wait_ge(loaded, 64)
            v = vec[:].rearrange("p (l s) d -> p l s d", s=2)
            nc.vector.tensor_tensor(prod[:], v[:, :, 0, :], v[:, :, 1, :], ALU.mult).then_inc(step, 1)
            dve.wait_ge(step, 1)
            nc.vector.tensor_reduce(dot[:], prod[:], AX.X, ALU.add).then_inc(step, 1)
            dve.wait_ge(exp_done, 1)
            nc.vector.tensor_tensor(diff[:], e[:, 1:2], e[:, 0:1], ALU.subtract).then_inc(step, 1)
            dve.wait_ge(step, 3)
            nc.vector.tensor_scalar(neg_lambda[:], diff[:], -LAMBDA_INIT, None, ALU.add).then_inc(step, 1)
            dve.wait_ge(step, 4)

        @block.scalar
        def _(act):
            act.wait_ge(step, 2)
            nc.scalar.activation(e[:], dot[:], ACT.Exp).then_inc(exp_done, 1)


def program(nc, ins, out):
    with ExitStack() as ctx:
        def sb(name, shape, dt=F32):
            return ctx.enter_context(nc.sbuf_tensor(name, shape, dt))

        scr = {
            "q0": nc.dram_tensor("q0_parts", [B * NH0 * D0, 2, 2, S], F32).ap(),
            "k0": nc.dram_tensor("k0_parts", [B * NKV * D0, 2, 2, S], F32).ap(),
            "q1": nc.dram_tensor("q1_parts", [B * H, 2, S], F32).ap(),
            "k1": nc.dram_tensor("k1_parts", [B * H, 2, S], F32).ap(),
            "h": nc.dram_tensor("h_parts", [P, 2, KT, TOK], F32).ap(),
            "resid": nc.dram_tensor("resid", [TOK, H], F32).ap(),
        }
        ident = sb("ident", [P, P])
        neg_lambda = sb("neg_lambda", [P, 1])
        zeros_dram = nc.dram_tensor("zero_rows_scratch", [2, MAPS, S], F32).ap()
        lambda_block(nc, ins, neg_lambda, zeros_dram)
        with ExitStack() as values:
            v0 = values.enter_context(nc.sbuf_tensor("v0", [P, B * NKV * QB, VW], F32))
            v1 = values.enter_context(nc.sbuf_tensor("v1", [P, B * NH1 * QB, VW], F32))
            with ExitStack() as weights:
                w0 = weights.enter_context(nc.sbuf_tensor("w0", [P, 2, KT, N0], F32R))
                w1 = weights.enter_context(nc.sbuf_tensor("w1", [P, 2, KT, N1], F32R))
                wp = weights.enter_context(nc.sbuf_tensor("wp", [P, 2, KT, NH1 * RK], F32R))
                xin = weights.enter_context(nc.sbuf_tensor("xin", [P, TT, H], F32))
                x_loaded = weights.enter_context(nc.semaphore("x_loaded"))
                weights_block(nc, ins, w0, w1, wp, ident, xin, x_loaded)
                project_block(nc, ins, scr, w0, w1, wp, v0, v1, ident, xin, x_loaded)
            heads_dram = nc.dram_tensor("heads_a", [P, B * NH1 // MAPS * QB, MAPS * RK], F32).ap()
            attn_dram = nc.dram_tensor("attn_out", [P, B * QB, NKV, MAPS * D0], F32).ap()
            rounds0 = 2 * B * NKV // RING
            layers = (
                Layer(0, 2 * B * NKV, D0, ((HI, HI), (HI, LO), (LO, HI), (LO, LO)), False, 1.0 / math.sqrt(D0), True,
                      scr["q0"], scr["k0"], v0, attn_dram),
                Layer(rounds0, B * NH1 // MAPS, D1, PASSES, True, float(np.float32(1.0) / np.sqrt(np.float32(D1))), False,
                      scr["q1"], scr["k1"], v1, heads_dram))
            attention_block(nc, layers, zeros_dram, neg_lambda, ident)
        scr["heads"], scr["attn"] = heads_dram, attn_dram
        acc = sb("acc", [P, TOK // P, H])
        ht = sb("ht_all", [P, 2, KT, TOK], F32R)
        h_loaded = ctx.enter_context(nc.semaphore("h_loaded"))
        raw_loaded = ctx.enter_context(nc.semaphore("mlp_raw_loaded"))
        mod = sb("mod_stack", [P, TOK], F32R)
        bst = sb("b_stack", [P, F], F32R)
        raw_in = sb("raw_in", [P, 2, KT, FG])
        raw_down = sb("raw_down", [P, FT, H])
        with ExitStack() as early:
            ahead = {"ht": ht, "h_loaded": h_loaded,
                     "rows": early.enter_context(nc.sbuf_tensor("attn_rows", [P, TOK // P, H], F32)),
                     "a_raw": early.enter_context(nc.sbuf_tensor("a_raw", [P, KT, RK], F32)),
                     "heads_loaded": early.enter_context(nc.semaphore("heads_loaded")),
                     "a_loaded": early.enter_context(nc.semaphore("a_loaded"))}
            output_block(nc, ins, scr, acc, ident, ahead, raw_in)
            modulate_block(nc, ins, ahead, mod, bst, ident, raw_in, raw_down, raw_loaded)
        mlp_block(nc, ins, out, ht, acc, mod, bst, raw_in, raw_down, raw_loaded)


def rope_tables():
    inv_freq = 1.0 / np.float32(10000.0) ** (np.arange(0, D0, 2, dtype=np.float32) / np.float32(D0))
    freqs = np.arange(S, dtype=np.float32)[None, :] * inv_freq.astype(np.float32)[:, None]
    angle = np.tile(freqs, (P // (D0 // 2), 1)).astype(np.float64)
    sign = np.where(np.arange(P) % D0 < D0 // 2, -1.0, 1.0)[:, None]
    return np.cos(angle).astype(np.float32), (np.sin(angle) * sign).astype(np.float32)


def kernel(**inputs):
    import concourse.bacc as bacc
    from concourse.bass_utils import run_bass_kernel_spmd

    def arr(name):
        return np.asarray(inputs[name])

    cos, sin = rope_tables()
    arrays = {
        "x": arr("L0_attn_hidden_states").reshape(TOK, H),
        "w0t": np.concatenate([arr("L0_attn_wq").T, arr("L0_attn_wk").T, arr("L0_attn_wv").T], axis=1),
        "wo0t": arr("L0_attn_wo").T,
        "lq1": arr("L0_attn_lambda_q1"), "lk1": arr("L0_attn_lambda_k1"),
        "lq2": arr("L0_attn_lambda_q2"), "lk2": arr("L0_attn_lambda_k2"),
        "ln1": arr("L0_ffn_ln1_w").reshape(KT, P).T, "ln2": arr("L0_ffn_ln2_w").reshape(KT, P).T,
        "w1t": np.concatenate([arr("L0_ffn_Wq").T, arr("L0_ffn_Wk").T], axis=1),
        "wv1": arr("L0_ffn_Wv"), "wo1": arr("L0_ffn_Wo"), "a": arr("L0_ffn_A"), "b": arr("L0_ffn_B"),
        "win_t": arr("L0_ffn_W_in_base").T, "wup_t": arr("L0_ffn_W_up_base").T, "wdown_t": arr("L0_ffn_W_down").T,
        "cos": cos, "sin": sin,
    }
    nc = bacc.Bacc("TRN2", target_bir_lowering=False, num_devices=1)
    maps, ins = {}, {}
    for name, a in arrays.items():
        a = np.ascontiguousarray(a)
        maps[f"in_{name}"] = a
        ins[name] = nc.dram_tensor(f"in_{name}", a.shape, mybir.dt.from_np(a.dtype), kind="ExternalInput").ap()
    out = nc.dram_tensor("out", (TOK, H), F32, kind="ExternalOutput").ap()
    program(nc, ins, out)
    res = run_bass_kernel_spmd(nc, [maps], core_ids=[0])
    return res.results[0]["out"].reshape(B, S, H)
```
